# Optimizing a Trainium2 kernel written in Bass

```python
import numpy as np
import jax
import jax.numpy as jnp

def _softmax(x, axis=-1):
    return jax.nn.softmax(x, axis=axis)

def _gelu(x):
    return jax.nn.gelu(x, approximate=True)

def _silu(x):
    return jax.nn.silu(x)

def _sigmoid(x):
    return jax.nn.sigmoid(x)

def _layernorm(x, axis=-1, eps=1e-05):
    m = jnp.mean(x, axis=axis, keepdims=True)
    v = jnp.var(x, axis=axis, keepdims=True)
    return (x - m) / jnp.sqrt(v + eps)

def _scatter_add(tgt, idx, src, axis=0):
    return tgt.at[idx].add(src)

def _segment_sum(src, seg, n):
    return jax.ops.segment_sum(src, seg, n)
kernel_name = 'mk_flamingo_gated_d2_seqx_r8_d0bdba'

def setup_inputs(seed: int=0):
    np.random.seed(seed)
    _w = jnp.asarray

    def _rec_inputs():
        import jax
        import jax.numpy as jnp
        _rk = jax.random.key(seed)
        x = -0.0002928 + 1 * jax.random.normal(jax.random.fold_in(_rk, 1), (8, 256, 128), jnp.float32)
        _lenS = 256 - jax.random.randint(jax.random.fold_in(_rk, 7), (8,), 0, max(1, 256 // 4) + 1, jnp.int32)
        _lenS2 = 256 - jax.random.randint(jax.random.fold_in(_rk, 8), (8,), 0, max(1, 256 // 4) + 1, jnp.int32)
        _ctx_1024P = jax.random.normal(jax.random.fold_in(_rk, 11), (8, 16, 128), jnp.float32)
        _ctx_1024c = jax.random.dirichlet(jax.random.fold_in(_rk, 511), 0.3 * jnp.ones((16,), jnp.float32), (8, 256))
        _ctx_1024t = jnp.einsum('bsk,bkd->bsd', _ctx_1024c, _ctx_1024P)
        _ctx_1024t = _ctx_1024t * jax.lax.rsqrt(jnp.mean(jnp.square(_ctx_1024t)) + 1e-12) * 0.953939
        ctx_1024 = -1.39393e-06 + 0.999914 * (_ctx_1024t + 0.3 * jax.random.normal(jax.random.fold_in(_rk, 611), (8, 256, 128), jnp.float32))
        _g = jax.random.normal(jax.random.fold_in(_rk, 9001), (2, 2), jnp.float32)
        _g = jnp.sign(_g) * jnp.maximum(jnp.abs(_g), 1.0) + (_g == 0) * 1.0
        g_xattn = _g[0]
        g_ffn = _g[1]
        return (x, ctx_1024, g_xattn, g_ffn)
    x, ctx_1024, g_xattn, g_ffn = _rec_inputs()

    def _L0_xattn_setup():
        import jax, jax.numpy as jnp
        import numpy as np
        B, S, D, NH = (2, 256, 128, 8)
        DH = D // NH
        EPS = 1e-06
        LN_EPS = 1e-05

        def _mlstm_cell(q, k, v, igate_w, igate_b, fgate_w, fgate_b, ln_scale):
            Slen = q.shape[0]
            ifg = jnp.concatenate([q, k, v], axis=-1)
            ig = (ifg @ igate_w.T + igate_b).T
            fg = (ifg @ fgate_w.T + fgate_b).T
            qh = q.reshape(Slen, NH, DH).transpose(1, 0, 2)
            kh = k.reshape(Slen, NH, DH).transpose(1, 0, 2)
            vh = v.reshape(Slen, NH, DH).transpose(1, 0, 2)
            log_f = jax.nn.log_sigmoid(fg)
            cs = jnp.cumsum(log_f, axis=1)
            fg_mat = cs[:, :, None] - cs[:, None, :]
            mask = jnp.tril(jnp.ones((Slen, Slen), dtype=bool))
            log_fg_mat = jnp.where(mask, fg_mat, -jnp.inf)
            log_D = log_fg_mat + ig[:, None, :]
            max_log_D = jnp.max(log_D, axis=-1, keepdims=True)
            D_mat = jnp.exp(log_D - max_log_D)
            qk = jnp.einsum('hsd,htd->hst', qh, kh) / np.sqrt(DH)
            C = qk * D_mat
            normalizer = jnp.maximum(jnp.abs(C.sum(axis=-1, keepdims=True)), jnp.exp(-max_log_D))
            h = jnp.einsum('hst,htd->hsd', C / (normalizer + EPS), vh)
            h = h.transpose(1, 0, 2).reshape(Slen, D)
            mu = h.mean(axis=-1, keepdims=True)
            var = h.var(axis=-1, keepdims=True)
            return (h - mu) / jnp.sqrt(var + LN_EPS) * ln_scale
        key = jax.random.key(seed)
        ks = jax.random.split(key, 8)
        rnd = lambda k, sh, s=1.0: jax.random.normal(k, sh, dtype=jnp.float32) * s
        return {'q': rnd(ks[0], (B, S, D)), 'k': rnd(ks[1], (B, S, D)), 'v': rnd(ks[2], (B, S, D)), 'igate_w': rnd(ks[3], (NH, 3 * D), 0.02), 'igate_b': jnp.linspace(3.0, 6.0, NH, dtype=jnp.float32), 'fgate_w': rnd(ks[4], (NH, 3 * D), 0.02), 'fgate_b': rnd(ks[5], (NH,), 0.3162278), 'ln_scale': jnp.ones((D,), dtype=jnp.float32)}
    _L0_xattn_all = _L0_xattn_setup()
    _L0_xattn_in = {k: v for k, v in _L0_xattn_all.items() if k in ('igate_w', 'igate_b', 'fgate_w', 'fgate_b', 'ln_scale')}
    del _L0_xattn_all

    def _L0_ffn_setup():
        import jax, jax.numpy as jnp
        import numpy as np
        TOP_K = 2
        key = jax.random.key(seed)
        ks = jax.random.split(key, 5)
        B, T, D, F, E = (4, 256, 128, 512, 8)
        s = 0.02
        return {'x': jax.random.normal(ks[0], (B, T, D), jnp.float32), 'gate_w': jax.random.normal(ks[1], (D, E), jnp.float32) * s, 'w1': jax.random.normal(ks[2], (E, D, F), jnp.float32) * s, 'w3': jax.random.normal(ks[3], (E, D, F), jnp.float32) * s, 'w2': jax.random.normal(ks[4], (E, F, D), jnp.float32) * s}
    _L0_ffn_all = _L0_ffn_setup()
    _L0_ffn_in = {k: v for k, v in _L0_ffn_all.items() if k in ('gate_w', 'w1', 'w3', 'w2')}
    del _L0_ffn_all

    def _L1_xattn_setup():
        import jax, jax.numpy as jnp
        import numpy as np
        D = 128
        H = 16
        E = 8
        DK = D // H
        B, S = (2, 256)
        key = jax.random.key(seed)
        ks = jax.random.split(key, 16)
        sc = 1.0 / np.sqrt(D)
        inp = {'query': jax.random.normal(ks[0], (B, S, D), jnp.float32), 'key': jax.random.normal(ks[1], (B, S, D), jnp.float32), 'value': jax.random.normal(ks[2], (B, S, D), jnp.float32), 'Wq': jax.random.normal(ks[3], (D, D), jnp.float32) * sc, 'bq': jax.random.normal(ks[4], (D,), jnp.float32) * sc, 'Wk': jax.random.normal(ks[5], (D, D), jnp.float32) * sc, 'bk': jax.random.normal(ks[6], (D,), jnp.float32) * sc, 'Wv': jax.random.normal(ks[7], (D, D), jnp.float32) * sc, 'bv': jax.random.normal(ks[8], (D,), jnp.float32) * sc, 'We': jax.random.normal(ks[9], (E, D, D), jnp.float32) * sc, 'be': jax.random.normal(ks[10], (E, D), jnp.float32) * sc, 'Wo': jax.random.normal(ks[11], (D, D), jnp.float32) * sc, 'bo': jax.random.normal(ks[12], (D,), jnp.float32) * sc}
        return inp
    _L1_xattn_all = _L1_xattn_setup()
    _L1_xattn_in = {k: v for k, v in _L1_xattn_all.items() if k in ('Wq', 'bq', 'Wk', 'bk', 'Wv', 'bv', 'We', 'be', 'Wo', 'bo')}
    del _L1_xattn_all

    def _L1_ffn_setup():
        import jax, jax.numpy as jnp
        import numpy as np
        B, S, H = (1, 256, 128)
        E, K = (16, 4)
        G, TG = (4, 2)
        I_MOE = 64
        N_SH = 2
        SCALE = 2.5

        def _mlp(x, gw, uw, dw):
            return jax.nn.silu(x @ gw.T) * (x @ uw.T) @ dw.T

        def _route(x2d, router_weight, e_bias):
            T = x2d.shape[0]
            scores = jax.nn.sigmoid(x2d @ router_weight.T)
            sc = scores + e_bias[None, :]
            group_scores = jnp.sum(jax.lax.top_k(sc.reshape(T, G, E // G), 2)[0], axis=-1)
            _, gidx = jax.lax.top_k(group_scores, TG)
            gmask = jnp.zeros((T, G), sc.dtype).at[jnp.arange(T)[:, None], gidx].set(1.0)
            smask = jnp.repeat(gmask, E // G, axis=1)
            masked = jnp.where(smask > 0, sc, 0.0)
            _, tidx = jax.lax.top_k(masked, K)
            tw = jnp.take_along_axis(scores, tidx, axis=1)
            tw = tw / (jnp.sum(tw, axis=-1, keepdims=True) + 1e-20)
            tw = tw * SCALE
            return (tidx, tw)

        def _moe_forward(hidden_states, router_weight, e_bias, gate_w, up_w, down_w, sh_gate_w, sh_up_w, sh_down_w):
            orig_shape = hidden_states.shape
            x = hidden_states.reshape(-1, H)
            T = x.shape[0]
            tidx, tw = _route(x, router_weight, e_bias)
            g = jnp.einsum('th,eih->tei', x, gate_w)
            u = jnp.einsum('th,eih->tei', x, up_w)
            h = jax.nn.silu(g) * u
            yo = jnp.einsum('tei,ehi->teh', h, down_w)
            combine = jnp.zeros((T, E), tw.dtype).at[jnp.arange(T)[:, None], tidx].add(tw)
            routed = jnp.einsum('te,teh->th', combine, yo)
            shared = _mlp(hidden_states.reshape(-1, H), sh_gate_w, sh_up_w, sh_down_w)
            return (routed + shared).reshape(orig_shape)
        key = jax.random.key(seed)
        ks = jax.random.split(key, 9)
        s = 0.02
        return {'hidden_states': jax.random.normal(ks[0], (B, S, H), jnp.float32), 'router_weight': jax.random.normal(ks[1], (E, H), jnp.float32) * s, 'e_bias': jnp.zeros((E,), jnp.float32), 'gate_w': jax.random.normal(ks[2], (E, I_MOE, H), jnp.float32) * s, 'up_w': jax.random.normal(ks[3], (E, I_MOE, H), jnp.float32) * s, 'down_w': jax.random.normal(ks[4], (E, H, I_MOE), jnp.float32) * s, 'sh_gate_w': jax.random.normal(ks[5], (N_SH * I_MOE, H), jnp.float32) * s, 'sh_up_w': jax.random.normal(ks[6], (N_SH * I_MOE, H), jnp.float32) * s, 'sh_down_w': jax.random.normal(ks[7], (H, N_SH * I_MOE), jnp.float32) * s}
    _L1_ffn_all = _L1_ffn_setup()
    _L1_ffn_in = {k: v for k, v in _L1_ffn_all.items() if k in ('router_weight', 'e_bias', 'gate_w', 'up_w', 'down_w', 'sh_gate_w', 'sh_up_w', 'sh_down_w')}
    del _L1_ffn_all
    return {'x': x, 'ctx_1024': ctx_1024, 'g_xattn': g_xattn, 'g_ffn': g_ffn, 'L0_xattn_igate_w': _L0_xattn_in['igate_w'], 'L0_xattn_igate_b': _L0_xattn_in['igate_b'], 'L0_xattn_fgate_w': _L0_xattn_in['fgate_w'], 'L0_xattn_fgate_b': _L0_xattn_in['fgate_b'], 'L0_xattn_ln_scale': _L0_xattn_in['ln_scale'], 'L0_ffn_gate_w': _L0_ffn_in['gate_w'], 'L0_ffn_w1': _L0_ffn_in['w1'], 'L0_ffn_w3': _L0_ffn_in['w3'], 'L0_ffn_w2': _L0_ffn_in['w2'], 'L1_xattn_Wq': _L1_xattn_in['Wq'], 'L1_xattn_bq': _L1_xattn_in['bq'], 'L1_xattn_Wk': _L1_xattn_in['Wk'], 'L1_xattn_bk': _L1_xattn_in['bk'], 'L1_xattn_Wv': _L1_xattn_in['Wv'], 'L1_xattn_bv': _L1_xattn_in['bv'], 'L1_xattn_We': _L1_xattn_in['We'], 'L1_xattn_be': _L1_xattn_in['be'], 'L1_xattn_Wo': _L1_xattn_in['Wo'], 'L1_xattn_bo': _L1_xattn_in['bo'], 'L1_ffn_router_weight': _L1_ffn_in['router_weight'], 'L1_ffn_e_bias': _L1_ffn_in['e_bias'], 'L1_ffn_gate_w': _L1_ffn_in['gate_w'], 'L1_ffn_up_w': _L1_ffn_in['up_w'], 'L1_ffn_down_w': _L1_ffn_in['down_w'], 'L1_ffn_sh_gate_w': _L1_ffn_in['sh_gate_w'], 'L1_ffn_sh_up_w': _L1_ffn_in['sh_up_w'], 'L1_ffn_sh_down_w': _L1_ffn_in['sh_down_w']}

def reference(x, ctx_1024, g_xattn, g_ffn, L0_xattn_igate_w, L0_xattn_igate_b, L0_xattn_fgate_w, L0_xattn_fgate_b, L0_xattn_ln_scale, L0_ffn_gate_w, L0_ffn_w1, L0_ffn_w3, L0_ffn_w2, L1_xattn_Wq, L1_xattn_bq, L1_xattn_Wk, L1_xattn_bk, L1_xattn_Wv, L1_xattn_bv, L1_xattn_We, L1_xattn_be, L1_xattn_Wo, L1_xattn_bo, L1_ffn_router_weight, L1_ffn_e_bias, L1_ffn_gate_w, L1_ffn_up_w, L1_ffn_down_w, L1_ffn_sh_gate_w, L1_ffn_sh_up_w, L1_ffn_sh_down_w):
    import jax
    import jax.numpy as jnp

    def _L0_xattn_ref(q, k, v, igate_w, igate_b, fgate_w, fgate_b, ln_scale):
        import jax, jax.numpy as jnp
        import numpy as np
        B, S, D, NH = (2, 256, 128, 8)
        DH = D // NH
        EPS = 1e-06
        LN_EPS = 1e-05

        def _mlstm_cell(q, k, v, igate_w, igate_b, fgate_w, fgate_b, ln_scale):
            Slen = q.shape[0]
            ifg = jnp.concatenate([q, k, v], axis=-1)
            ig = (ifg @ igate_w.T + igate_b).T
            fg = (ifg @ fgate_w.T + fgate_b).T
            qh = q.reshape(Slen, NH, DH).transpose(1, 0, 2)
            kh = k.reshape(Slen, NH, DH).transpose(1, 0, 2)
            vh = v.reshape(Slen, NH, DH).transpose(1, 0, 2)
            log_f = jax.nn.log_sigmoid(fg)
            cs = jnp.cumsum(log_f, axis=1)
            fg_mat = cs[:, :, None] - cs[:, None, :]
            mask = jnp.tril(jnp.ones((Slen, Slen), dtype=bool))
            log_fg_mat = jnp.where(mask, fg_mat, -jnp.inf)
            log_D = log_fg_mat + ig[:, None, :]
            max_log_D = jnp.max(log_D, axis=-1, keepdims=True)
            D_mat = jnp.exp(log_D - max_log_D)
            qk = jnp.einsum('hsd,htd->hst', qh, kh) / np.sqrt(DH)
            C = qk * D_mat
            normalizer = jnp.maximum(jnp.abs(C.sum(axis=-1, keepdims=True)), jnp.exp(-max_log_D))
            h = jnp.einsum('hst,htd->hsd', C / (normalizer + EPS), vh)
            h = h.transpose(1, 0, 2).reshape(Slen, D)
            mu = h.mean(axis=-1, keepdims=True)
            var = h.var(axis=-1, keepdims=True)
            return (h - mu) / jnp.sqrt(var + LN_EPS) * ln_scale
        return jax.vmap(lambda qq, kk, vv: _mlstm_cell(qq, kk, vv, igate_w, igate_b, fgate_w, fgate_b, ln_scale))(q, k, v)

    def _L0_ffn_ref(x, gate_w, w1, w3, w2):
        import jax, jax.numpy as jnp
        import numpy as np
        TOP_K = 2
        logits = jnp.einsum('btd,de->bte', x, gate_w)
        probs = jax.nn.softmax(logits, axis=-1)
        expert_weights, expert_indices = jax.lax.top_k(probs, TOP_K)
        expert_weights = expert_weights / expert_weights.sum(-1, keepdims=True)
        E = w1.shape[0]
        out = jnp.zeros_like(x)
        for i in range(E):
            wi = jnp.where(expert_indices == i, expert_weights, 0.0).sum(-1)
            h = jax.nn.silu(jnp.einsum('btd,df->btf', x, w1[i])) * jnp.einsum('btd,df->btf', x, w3[i])
            out = out + jnp.einsum('btf,fd->btd', h, w2[i]) * wi[..., None]
        return out

    def _L1_xattn_ref(query, key, value, Wq, bq, Wk, bk, Wv, bv, We, be, Wo, bo):
        import jax, jax.numpy as jnp
        import numpy as np
        D = 128
        H = 16
        E = 8
        DK = D // H
        B, S = (2, 256)
        b = query.shape[0]
        Q = (query @ Wq.T + bq).reshape(b, -1, H, DK).transpose(0, 2, 1, 3)
        K = (key @ Wk.T + bk).reshape(b, -1, H, DK).transpose(0, 2, 1, 3)
        V = (value @ Wv.T + bv).reshape(b, -1, H, DK).transpose(0, 2, 1, 3)
        scores = jnp.einsum('bhqd,bhkd->bhqk', Q, K) / jnp.sqrt(jnp.asarray(DK, Q.dtype))
        attn = jax.nn.softmax(scores, axis=-1)
        out = jnp.einsum('bhqk,bhkd->bhqd', attn, V)
        out = out.transpose(0, 2, 1, 3).reshape(b, -1, D)
        expert = jnp.einsum('bsd,eod->ebso', out, We) + be[:, None, None, :]
        expert = expert.mean(axis=0)
        return expert @ Wo.T + bo

    def _L1_ffn_ref(hidden_states, router_weight, e_bias, gate_w, up_w, down_w, sh_gate_w, sh_up_w, sh_down_w):
        import jax, jax.numpy as jnp
        import numpy as np
        B, S, H = (1, 256, 128)
        E, K = (16, 4)
        G, TG = (4, 2)
        I_MOE = 64
        N_SH = 2
        SCALE = 2.5

        def _mlp(x, gw, uw, dw):
            return jax.nn.silu(x @ gw.T) * (x @ uw.T) @ dw.T

        def _route(x2d, router_weight, e_bias):
            T = x2d.shape[0]
            scores = jax.nn.sigmoid(x2d @ router_weight.T)
            sc = scores + e_bias[None, :]
            group_scores = jnp.sum(jax.lax.top_k(sc.reshape(T, G, E // G), 2)[0], axis=-1)
            _, gidx = jax.lax.top_k(group_scores, TG)
            gmask = jnp.zeros((T, G), sc.dtype).at[jnp.arange(T)[:, None], gidx].set(1.0)
            smask = jnp.repeat(gmask, E // G, axis=1)
            masked = jnp.where(smask > 0, sc, 0.0)
            _, tidx = jax.lax.top_k(masked, K)
            tw = jnp.take_along_axis(scores, tidx, axis=1)
            tw = tw / (jnp.sum(tw, axis=-1, keepdims=True) + 1e-20)
            tw = tw * SCALE
            return (tidx, tw)

        def _moe_forward(hidden_states, router_weight, e_bias, gate_w, up_w, down_w, sh_gate_w, sh_up_w, sh_down_w):
            orig_shape = hidden_states.shape
            x = hidden_states.reshape(-1, H)
            T = x.shape[0]
            tidx, tw = _route(x, router_weight, e_bias)
            g = jnp.einsum('th,eih->tei', x, gate_w)
            u = jnp.einsum('th,eih->tei', x, up_w)
            h = jax.nn.silu(g) * u
            yo = jnp.einsum('tei,ehi->teh', h, down_w)
            combine = jnp.zeros((T, E), tw.dtype).at[jnp.arange(T)[:, None], tidx].add(tw)
            routed = jnp.einsum('te,teh->th', combine, yo)
            shared = _mlp(hidden_states.reshape(-1, H), sh_gate_w, sh_up_w, sh_down_w)
            return (routed + shared).reshape(orig_shape)
        return _moe_forward(hidden_states, router_weight, e_bias, gate_w, up_w, down_w, sh_gate_w, sh_up_w, sh_down_w)
    x = x + jnp.tanh(g_xattn[0]) * _L0_xattn_ref(_layernorm(x, axis=-1), ctx_1024, ctx_1024, L0_xattn_igate_w, L0_xattn_igate_b, L0_xattn_fgate_w, L0_xattn_fgate_b, L0_xattn_ln_scale)
    x = x + jnp.tanh(g_ffn[0]) * _L0_ffn_ref(_layernorm(x, axis=-1), L0_ffn_gate_w, L0_ffn_w1, L0_ffn_w3, L0_ffn_w2)
    x = x + jnp.tanh(g_xattn[1]) * _L1_xattn_ref(_layernorm(x, axis=-1), ctx_1024, ctx_1024, L1_xattn_Wq, L1_xattn_bq, L1_xattn_Wk, L1_xattn_bk, L1_xattn_Wv, L1_xattn_bv, L1_xattn_We, L1_xattn_be, L1_xattn_Wo, L1_xattn_bo)
    x = x + jnp.tanh(g_ffn[1]) * _L1_ffn_ref(_layernorm(x, axis=-1), L1_ffn_router_weight, L1_ffn_e_bias, L1_ffn_gate_w, L1_ffn_up_w, L1_ffn_down_w, L1_ffn_sh_gate_w, L1_ffn_sh_up_w, L1_ffn_sh_down_w)
    return x

_drawn_inputs = setup_inputs


def setup_inputs(seed=0):
    import zlib

    import numpy as np

    out = dict(_drawn_inputs(seed))
    spreads = {'g_ffn': (-1.0, 0.6), 'L0_xattn_ln_scale': (1.0, 0.2), 'L1_ffn_e_bias': (0.0, 0.8)}
    factors = {'L0_ffn_gate_w': 8.0,
     'L0_ffn_w1': 8.0,
     'L0_ffn_w3': 8.0,
     'L0_ffn_w2': 8.0,
     'L1_xattn_bq': 8.0,
     'L1_xattn_bk': 8.0,
     'L1_xattn_bv': 2.843,
     'L1_xattn_be': 2.734,
     'L1_ffn_router_weight': 8.0,
     'L1_ffn_gate_w': 8.0,
     'L1_ffn_up_w': 8.0,
     'L1_ffn_down_w': 8.0,
     'L1_ffn_sh_gate_w': 8.0,
     'L1_ffn_sh_up_w': 8.0,
     'L1_ffn_sh_down_w': 8.0}
    for name, (base, spread) in spreads.items():
        noise = np.random.default_rng([zlib.crc32(name.encode()), seed]).standard_normal(out[name].shape)
        drawn = base * np.exp(spread * noise) if base else spread * noise
        out[name] = jnp.asarray(drawn.astype(out[name].dtype))
    for name, factor in factors.items():
        out[name] = (out[name] * factor).astype(out[name].dtype)
    return out
```

```python
from contextlib import ExitStack

import concourse.bass as bass
from concourse import mybir

P = 128
B, S, D = 8, 256, 128
T = B * S
NT = T // P
CH = S // P
H0, DH0 = 8, 16
VW = DH0 + 1
BH = B * H0
E0, F0 = 8, 512
FC0 = F0 // P
NBLK = (2 * T + E0 * (P - 1)) // P
NBLK += NBLK % 2
H1, DH1 = 16, 8
HG, HJ = 4, 4
ST = P // HJ
SM = 3 * DH1
EO = 8
E1, I1, K1 = 16, 64, 4
SHARE1 = 2.5
NG1 = 4
FC1 = E1 * I1 // P + 1
TT = 512
LN_EPS = 1e-5
NORM_EPS = 1e-6
NEG = -1.0e30
LOWEST = -3.0e38

ALU = mybir.AluOpType
ACT = mybir.ActivationFunctionType
AX = mybir.AxisListType
F32 = mybir.dt.float32
F32R = mybir.dt.float32r
BF16 = mybir.dt.bfloat16
I32 = mybir.dt.int32
U32 = mybir.dt.uint32


def layout(widths):
    at, out = 0, {}
    for name, w in widths:
        out[name] = (at, at + w)
        at += w
    return out, at


CONST, NCONST = layout([
    ("ident", P), ("future", P), ("before", P), ("of_seq", B), ("neg_of_head", H0),
    ("of_head", H0), ("quarter_of_head", H0), ("quarter_block", H0 * VW), ("block_start", NT),
    ("not_first", P), ("block_index", NBLK * E0), ("rev8", E0), ("rev16", E1),
    ("query_lo", 1), ("key_lo", 1), ("expert_cols", (FC1 - 1) * P),
])
PARAM, NPARAM = layout([
    ("gwq", 2 * H0), ("gwk", 2 * H0), ("gwv", 2 * H0), ("gate_b", 2), ("ln_scale", D), ("gates", 4),
    ("router0", E0), ("router1", E1), ("e_bias", E1), ("bq", HG), ("bk", HG), ("bv", D),
    ("wv", D), ("wo", D), ("be", EO), ("bo", D),
])


def rd(ap):
    return ap.bitcast(F32R)


class Chain:

    def __init__(self, eng, sem):
        self.eng, self.sem, self.base, self.n, self.turn, self.per = eng, sem, 0, 0, None, 0

    def enter(self, turn, per):
        self.base, self.n, self.turn, self.per = self.base + self.n, 0, turn, per

    def leave(self, turns):
        assert self.n == self.per, (self.n, self.per)
        self.base, self.n, self.turn = self.base + turns * self.per, 0, None

    def value(self):
        return self.base + self.n if self.turn is None else self.turn * self.per + (self.base + self.n)

    def link(self, ins):
        ins.then_inc(self.sem, 1)
        self.n += 1
        self.eng.wait_ge(self.sem, self.value())


def ge(eng, sem, value):
    if not (isinstance(value, int) and value <= 0):
        eng.wait_ge(sem, value)


def pipelined(eng, n, stages, extra=None, peel=0):
    least, most = min(lag for _, lag in stages), max(lag for _, lag in stages)
    first = most + peel

    def turn(k, parity):
        for stage, lag in stages:
            if not isinstance(k, int) or 0 <= k - lag < n + (stage is extra):
                stage(k - lag, (parity - lag) % 2)

    passes = (n + least - first) // 2
    for k in range(least, first):
        turn(k, k % 2)
    with eng.Fori(0, passes) as it:
        for i in range(2):
            turn(it * 2 + (first + i), (first + i) % 2)
    for k in range(first + 2 * passes, n + most):
        turn(k, k % 2)


def build(nc, a, scr_x, scr_y, out, stage=9):
    es = ExitStack()
    with es:
        def sb(name, shape, dt=F32, stack=es):
            return stack.enter_context(nc.sbuf_tensor(name, shape, dt))

        def sem(name):
            return es.enter_context(nc.semaphore(name))

        ps = [es.enter_context(nc.psum_tensor(f"bank{i}", [P, 512], F32)) for i in range(4)]
        pw = [es.enter_context(nc.psum_tensor(f"wide{i}", [P, 1024], F32)) for i in range(2)]

        con = sb("con", [P, NCONST])
        par = sb("par", [P, NPARAM])
        x = sb("x", [P, NT, D])
        xn = sb("xn", [P, NT, D])
        xT = sb("xT", [P, T])
        ctxT = sb("ctxT", [P, T])
        st = sb("st", [P, NT, 6])
        lnw = sb("lnw", [P, 8, NT])
        tg = sb("tg", [P, 4])
        ctS = [sb(f"ctS{i}", [P, S]) for i in range(2)]
        before_bf = sb("before_bf", [P, P], BF16)
        ones_bf = sb("ones_bf", [P, P], BF16)

        def C(name):
            return con[:, CONST[name][0]:CONST[name][1]]

        def A(name):
            return par[:, PARAM[name][0]:PARAM[name][1]]

        ffn = ExitStack()
        wh = sb("w13h", [P, 2 * E0 * F0], F32, ffn)
        wl = sb("w13l", [P, 2 * E0 * F0], F32, ffn)

        ml = ExitStack()
        wst = [sb(f"wst{i}", [P, F0], F32, ml) for i in range(2)]
        zero = sb("zero", [P, P], F32, ml)
        vaug = sb("vaug", [P, NT, H0 * VW], F32, ml)
        num = sb("num", [P, NT, H0 * VW], F32, ml)
        gwc = sb("gwc", [P, 2 * H0], F32, ml)
        lnsg = sb("lnsg", [P, D], F32, ml)
        ident_bf = sb("ident_bf", [P, P], BF16, ml)
        future_bf = sb("future_bf", [P, 4, P], BF16, ml)
        g64 = sb("g64", [BH, 10, S], F32, ml)
        negM = sb("negM", [BH, 2], F32, ml)
        t64 = sb("t64", [BH, 4 * P], F32, ml)
        wT = sb("wT", [P, 4, BH], F32, ml)
        ahl = sb("ahl", [P, 3 * P], F32, ml)
        mhl = sb("mhl", [P, S], F32, ml)
        Rm = sb("Rm", [P, H0, S], F32, ml)
        dlt = sb("dlt", [P, H0, P], F32, ml)
        LS = [sb(f"LS{i}", [P, 3 * P], F32, ml) for i in range(2)]
        Qm = [sb(f"Qm{i}", [P, H0, S], F32, ml) for i in range(2)]
        qS = [sb(f"qS{i}", [P, P], F32, ml) for i in range(2)]
        Ks = [sb(f"Ks{i}", [P, P], F32, ml) for i in range(2)]
        stm = sb("stm", [P, H0 * VW], F32, ml)
        tmp = sb("tmp", [P, H0 * VW], F32, ml)
        Dm = [sb(f"Dm{i}", [P, 1024], F32, ml) for i in range(2)]
        Cm = [sb(f"Cm{i}", [P, 1024], F32, ml) for i in range(2)]
        den = sb("den", [P, NT * H0], F32, ml)
        ml.close()

        mo = ExitStack()
        w2 = sb("w2", [P, E0 * F0], F32, mo)
        rt = sb("rt", [P, 8, NT * E0], F32, mo)
        sm = sb("sm", [P, 8, NT], F32, mo)
        ex = sb("ex", [P, 4, E0], F32, mo)
        cmpb = sb("cmpb", [P, NBLK * E0], F32, mo)
        routed = sb("routed", [P, NT * E0], BF16, mo)
        slot = sb("slot", [P, 2, NT], U32, mo)
        share = sb("share", [P, 2, NT], F32, mo)
        bcol = sb("bcol", [1, 2, NBLK], F32, mo)
        boff = sb("boff", [1, NBLK], I32, mo)
        xg = [sb(f"xg{i}", [P, D], F32, mo) for i in range(2)]
        xgh = [sb(f"xgh{i}", [P, P], F32, mo) for i in range(2)]
        xgl = [sb(f"xgl{i}", [P, P], F32, mo) for i in range(2)]
        sg = [sb(f"sg{i}", [P, F0], F32, mo) for i in range(2)]
        hb = [sb(f"hb{i}", [P, F0], F32, mo) for i in range(2)]
        hT = [sb(f"hT{i}", [P, F0], F32, mo) for i in range(2)]
        yb = [sb(f"yb{i}", [P, D], F32, mo) for i in range(2)]
        gy = [sb(f"gy{i}", [P, NT, D], F32, mo) for i in range(2)]
        mo.close()
        ffn.close()

        at3 = ExitStack()
        wqs = sb("wqs", [P, HG * P], F32, at3)
        wks = sb("wks", [P, HG * P], F32, at3)
        we = sb("we", [P, EO, D], F32, at3)
        wem = sb("wem", [P, D], F32, at3)
        bem = sb("bem", [P, 1], F32, at3)
        bemb = sb("bemb", [P, P], F32, at3)
        wc = sb("wc", [P, D], F32, at3)
        cb = sb("cb", [P, D], F32, at3)
        bqs = sb("bqs", [P, HG], F32, at3)
        q32 = sb("q32", [P, HG, S], F32, at3)
        qhi = sb("qhi", [P, HG, S], F32, at3)
        k32 = sb("k32", [P, HG, S], F32, at3)
        khi = sb("khi", [P, HG, S], F32, at3)
        Qs = [sb(f"Qs{i}", [P, HG, S], F32, at3) for i in range(2)]
        Kst = [sb(f"Kst{i}", [P, HG, S], F32, at3) for i in range(2)]
        Q2 = sb("Q2", [P, HG, S], F32, at3)
        Kd = [sb(f"Kd{i}", [P, HG, HJ, S], F32, at3) for i in range(2)]
        Qd = sb("Qd", [P, HG, HJ, S], F32, at3)
        vp = [sb(f"vp{i}", [P, CH, H1, ST], F32, at3) for i in range(2)]
        mx = sb("mx", [P, CH, H1], F32, at3)
        mp = sb("mp", [P, CH, HG, P], F32, at3)
        et3 = [[sb(f"et{i}{c}", [P, HJ, S], F32, at3) for c in range(CH)] for i in range(2)]
        o32 = sb("o32", [P, HG, S], F32, at3)
        rec = sb("rec", [P, CH, H1], F32, at3)
        on = sb("on", [P, CH, D], F32, at3)
        onT = sb("onT", [P, CH, P], F32, at3)
        at3.close()

        m2 = ExitStack()
        graw = sb("graw", [P, 2 * FC1 * P], F32, m2)
        guh = sb("guh", [P, 2 * FC1 * P], F32, m2)
        gul = sb("gul", [P, 2 * FC1 * P], F32, m2)
        dn = sb("dn", [P, FC1, D], F32, m2)
        xTh = sb("xTh", [P, T], F32, m2)
        xTl = sb("xTl", [P, T], F32, m2)
        cT = sb("cT", [P, T], F32, m2)
        ecol = sb("ecol", [P, (FC1 - 1) * P], F32, m2)
        r1 = sb("r1", [P, 6, NT * E1], F32, m2)
        r4 = sb("r4", [P, 12, NT * NG1], F32, m2)
        s4 = sb("s4", [P, 6, NT], F32, m2)
        chl = sb("chl", [P, NT, 2 * E1], F32, m2)
        sg1 = [sb(f"sgb{i}", [P, TT], F32, m2) for i in range(2)]
        h1 = [sb(f"h1{i}", [P, TT], F32, m2) for i in range(2)]
        hT1 = [sb(f"hTb{i}", [P, FC1, TT], F32, m2) for i in range(2)]
        m2.close()

        s_con = sem("constants_loaded")
        s_par = sem("parameters_loaded")
        s_x = sem("x_loaded")
        s_ctx = sem("ctx_loaded")
        s_va = sem("values_loaded")
        s_v = sem("dve_step")
        s_a = sem("act_step")
        s_p = sem("pool_step")
        s_var = sem("ln_variance_ready")
        s_pow = sem("ln_power_ready")
        s_xn = sem("xn_ready")
        s_tr = sem("x_transposed_in_psum")
        s_xT = sem("xT_ready")
        s_gps = sem("gates_in_psum")
        s_gT = sem("gates_copied")
        s_g64 = sem("gates_by_head_row")
        s_z = sem("forget_gate_ready")
        s_sp = sem("softplus_ready")
        s_aM = sem("stabilizers_ready")
        s_t64 = sem("decays_ready")
        s_wps = sem("decays_in_psum")
        s_wT = sem("decay_columns_ready")
        s_bc = sem("mlstm_constants_ready")
        s_free = sem("sequence_matmuls_done")
        s_ct = [sem(f"ctx_columns_{i}_loaded") for i in range(2)]
        s_ls = sem("exponent_operand_ready")
        s_qm = sem("head_queries_ready")
        s_qS = sem("chunk_queries_ready")
        s_E = sem("exponent_in_psum")
        s_D = sem("decay_matrix_ready")
        s_S = sem("scores_in_psum")
        s_C = sem("weighted_scores_ready")
        s_ks = sem("decayed_keys_ready")
        s_st = sem("state_in_psum")
        s_stm = sem("state_copied")
        s_I = sem("state_part_in_psum")
        s_It = sem("state_part_scaled")
        s_PV = sem("head_sums_in_psum")
        s_num = sem("head_sums_copied")
        s_w = [sem(f"weights_{i}_loaded") for i in range(2)]
        s_wh = sem("weights_hi_ready")
        s_wl = sem("weights_lo_ready")
        s_tg = sem("gates_tanh_ready")
        s_x1 = sem("x1_ready")
        s_zero = sem("zero_ready")
        s_clr = sem("scratch_cleared")
        s_out = sem("out_stored")
        s_w2 = sem("w2_loaded")
        s_lg = sem("router_logits_in_psum")
        s_lx = sem("router_logits_less_max")
        s_ex = sem("router_exponentials_ready")
        s_ro = sem("routed_ready")
        s_rk = sem("ranks_in_psum")
        s_sl = sem("slots_ready")
        s_be = sem("block_experts_ready")
        s_sc = sem("tokens_scattered")
        s_xg = [sem(f"block_tokens_{i}_loaded") for i in range(2)]
        s_T = sem("block_tokens_in_psum")
        s_xp = sem("block_tokens_split")
        s_G = sem("hidden_gate_in_psum")
        s_U = sem("hidden_up_in_psum")
        s_sg = sem("silu_ready")
        s_hb = sem("hidden_ready")
        s_H = sem("hidden_transposed_in_psum")
        s_hT = sem("hidden_transposed_copied")
        s_Y = sem("block_out_in_psum")
        s_yb = sem("block_out_copied")
        s_ys = [sem(f"block_out_{i}_stored") for i in range(2)]
        s_gy = [sem(f"tile_{t}_gathered") for t in range(NT)]
        s_x2 = sem("x2_ready")
        c_w = sem("attention_weights_loaded")
        c_wa = sem("mean_expert_ready")
        c_wp = sem("output_weights_in_psum")
        c_wc = sem("output_weights_ready")
        c_z = sem("attention_zeros_ready")
        c_ct = [sem(f"attention_ctx_{i}_loaded") for i in range(2)]
        c_K = sem("keys_in_psum")
        c_k32 = sem("keys_copied")
        c_khi = sem("keys_rounded")
        c_qhi = sem("queries_rounded")
        c_rec = sem("row_sums_inverted")
        c_ks = sem("key_stacks_ready")
        c_kd = [sem(f"key_blocks_{i}_placed") for i in range(2)]
        c_V = sem("values_in_psum")
        c_vp = sem("values_ready")
        c_Q = sem("queries_in_psum")
        c_q32 = sem("queries_copied")
        c_qs = sem("query_stacks_ready")
        c_P1 = sem("scores_for_max_in_psum")
        c_R = sem("max_taken")
        c_mp = sem("max_parts_ready")
        c_MT = sem("max_rows_in_psum")
        c_q2 = sem("queries_with_max_ready")
        c_qd = sem("query_blocks_placed")
        c_P2 = sem("scores_less_max_in_psum")
        c_X = sem("exponentials_ready")
        c_PV = sem("attention_sums_in_psum")
        c_O = sem("attention_sums_copied")
        c_OT = sem("attention_sums_turned")
        c_on = sem("attention_normalized")
        c_nT = sem("attention_turned_in_psum")
        c_nc = sem("attention_turned_copied")
        c_Y = sem("attention_out_in_psum")
        s_x3 = sem("x3_ready")
        d_w = sem("mixture2_weights_loaded")
        d_wh = sem("mixture2_weights_hi_ready")
        d_wl = sem("mixture2_weights_lo_ready")
        d_c = sem("mixture2_constants_ready")
        d_xT = sem("x3_parts_ready")
        d_lg = sem("router2_logits_in_psum")
        d_sg = sem("router2_exponentials_ready")
        d_cm = sem("combine_weights_ready")
        d_cT = sem("combine_rows_in_psum")
        d_cc = sem("combine_rows_ready")
        d_G = sem("mixture2_gate_in_psum")
        d_U = sem("mixture2_up_in_psum")
        d_Us = sem("mixture2_up_matmuls_done")
        d_sl = sem("mixture2_silu_ready")
        d_h1 = sem("mixture2_hidden_ready")
        d_h = sem("mixture2_weighted_hidden_ready")
        d_Y = sem("mixture2_out_in_psum")
        d_x4 = sem("x4_ready")

        block = es.enter_context(nc.Block())

        @block.sync
        def _(sp):
            sp.dma_start(x[:], a["x_nat"].rearrange("p (t d) -> p t d", d=D)).then_inc(s_x, 16)
            sp.dma_start(con[:], a["const"]).then_inc(s_con, 16)
            sp.dma_start(par[:], a["param"]).then_inc(s_par, 16)
            sp.dma_start(ctxT[:], a["ctxT"]).then_inc(s_ctx, 16)
            sp.dma_start(vaug[:], a["vaug"].rearrange("p (t d) -> p t d", d=H0 * VW)).then_inc(s_va, 16)
            sp.wait_ge(s_zero, 1)
            sp.dma_start(scr_x.rearrange("(r p) d -> p r d", p=P),
                         zero[:].unsqueeze(1).broadcast_to([P, NBLK, D])).then_inc(s_clr, 16)
            for b in range(B):
                sp.wait_ge(s_gT, b // 2 + 1)
                for k in range(2):
                    sp.dma_start(g64[b * H0:(b + 1) * H0, k, :],
                                 xn_gates(xn)[k * H0:(k + 1) * H0, b * S:(b + 1) * S]).then_inc(s_g64, 16)
            with sp.Fori(0, B // 2) as it:
                for i in range(2):
                    sp.wait_ge(s_free, it * 2 + (i + 1))
                    sp.dma_start(ctS[i][:], a["ctxT"][:, bass.ds((it * 2 + i) * S, S)]).then_inc(s_ct[i], 16)
                    for u in (2 * i, 2 * i + 1):
                        sp.wait_ge(s_wl, it * 4 + (u + 1))
                        sp.dma_start(wst[u % 2][:], a["w13"][:, bass.ds((it * 4 + u) * F0, F0)])\
                            .then_inc(s_w[u % 2], 16)
            if stage == 1:
                sp.wait_ge(s_x1, 1)
                sp.dma_start(out.rearrange("p (t d) -> p t d", d=D), x[:]).then_inc(s_out, 16)
                sp.wait_ge(s_out, 16)
                sp.wait_ge(s_clr, 16)
                return
            sp.wait_ge(s_x1, 1)
            sp.wait_ge(s_wl, 2 + 2 * E0)
            sp.wait_ge(s_clr, 16)
            sp.dma_start(w2[:], a["w2"]).then_inc(s_w2, 16)
            sp.wait_ge(s_sc, 16 * 2 * NT)

            def load_block(j, i):
                ge(sp, s_T, j - 1)
                sp.dma_start(xg[i][:], scr_x[bass.ds(j * P, P), :]).then_inc(s_xg[i], 16)

            def store_block(j, i):
                sp.wait_ge(s_yb, j + 1)
                sp.dma_start(scr_y[bass.ds(j * P, P), :], yb[i][:]).then_inc(s_ys[i], 16)

            pipelined(sp, NBLK, [(load_block, -1), (store_block, 2)])
            sp.wait_ge(s_x2, NT)
            if stage == 2:
                sp.dma_start(out.rearrange("p (t d) -> p t d", d=D), x[:]).then_inc(s_out, 16)
                sp.wait_ge(s_out, 16)
                return

            for dst, name in ((wqs, "wqs"), (wks, "wks")):
                sp.dma_start(dst[:], a[name]).then_inc(c_w, 16)
            sp.dma_start(we[:], a["we"].rearrange("p (e d) -> p e d", d=D)).then_inc(c_w, 16)
            sp.wait_ge(c_z, 5)

            def load_ctx(b, i):
                ge(sp, c_V, b - 1)
                sp.dma_start(ctS[i][:], a["ctxT"][:, bass.ds(b * S, S)]).then_inc(c_ct[i], 16)

            def place_keys(b, i):
                sp.wait_ge(c_ks, b + 1)
                for j in range(HJ):
                    rows = slice(j * ST, (j + 1) * ST)
                    sp.dma_start(Kd[i][rows, :, j, :], Kst[i][rows, :, :]).then_inc(c_kd[i], 16)

            def place_queries(b, i):
                ge(sp, c_P2, b * 8)
                sp.wait_ge(c_q2, b * 2 + 2)
                for j in range(HJ):
                    rows = slice(j * ST, (j + 1) * ST)
                    sp.dma_start(Qd[rows, :, j, :], Q2[rows, :, :]).then_inc(c_qd, 16)

            pipelined(sp, B, [(load_ctx, -1), (place_keys, -1), (place_queries, 0)])
            sp.wait_ge(s_x3, B)
            if stage == 3:
                sp.dma_start(out.rearrange("p (t d) -> p t d", d=D), x[:]).then_inc(s_out, 16)
                sp.wait_ge(s_out, 16)
                return

            sp.dma_start(graw[:], a["gu"]).then_inc(d_w, 16)
            sp.dma_start(dn[:], a["down"].rearrange("p (c d) -> p c d", d=D)).then_inc(d_w, 16)
            o4 = out.rearrange("p (t d) -> p t d", d=D)
            for t in range(T // TT):
                sp.wait_ge(d_x4, t + 1)
                k = TT // P
                sp.dma_start(o4[:, t * k:(t + 1) * k, :], x[:, t * k:(t + 1) * k, :]).then_inc(s_out, 16)
            sp.wait_ge(s_out, 16 * (T // TT))

        def ln_stats(dve, v, src, k, eps=LN_EPS):
            with dve.Fori(0, NT) as t:
                dve.bn_stats(st[:, t, :], src[:, t, :]).then_inc(v.sem, 1)
            v.n += NT
            dve.wait_ge(v.sem, v.value())
            v.link(dve.tensor_tensor(lnw[:, 0, :], st[:, :, 1], st[:, :, 4], ALU.add))
            v.link(dve.tensor_scalar(lnw[:, 0, :], lnw[:, 0, :], 0.5, None, ALU.mult))
            v.link(dve.tensor_tensor(lnw[:, 1, :], st[:, :, 1], st[:, :, 4], ALU.subtract))
            v.link(dve.tensor_tensor(lnw[:, 1, :], lnw[:, 1, :], lnw[:, 1, :], ALU.mult))
            v.link(dve.tensor_tensor(lnw[:, 2, :], st[:, :, 2], st[:, :, 5], ALU.add))
            v.link(dve.tensor_scalar(lnw[:, 2, :], lnw[:, 2, :], 1.0 / D, eps, ALU.mult, ALU.add))
            dve.scalar_tensor_tensor(out=lnw[:, 3, :], in0=lnw[:, 1, :], scalar=0.25, in1=lnw[:, 2, :],
                                     op0=ALU.mult, op1=ALU.add).then_inc(s_var, 1)
            dve.wait_ge(s_var, k)
            dve.wait_ge(s_pow, k)
            v.link(dve.tensor_tensor(lnw[:, 5, :], lnw[:, 4, :], lnw[:, 4, :], ALU.mult))
            v.link(dve.tensor_tensor(lnw[:, 5, :], lnw[:, 5, :], lnw[:, 3, :], ALU.mult))
            v.link(dve.tensor_scalar(lnw[:, 5, :], lnw[:, 5, :], -0.5, 1.5, ALU.mult, ALU.add))
            v.link(dve.tensor_tensor(lnw[:, 6, :], lnw[:, 5, :], lnw[:, 4, :], ALU.mult))

        def ln_apply(dve, v, dst, src):
            v.link(dve.tensor_tensor(dst, src, lnw[:, 0, :].unsqueeze(2).broadcast_to([P, NT, D]), ALU.subtract))
            return dve.tensor_tensor(dst, dst, lnw[:, 6, :].unsqueeze(2).broadcast_to([P, NT, D]), ALU.mult)

        def ln_power(act, ch, k):
            act.wait_ge(s_var, k)
            ch.link(act.activation(lnw[:, 4, :], lnw[:, 3, :], ACT.Ln))
            act.activation(lnw[:, 4, :], lnw[:, 4, :], ACT.Exp, scale=-0.5).then_inc(s_pow, 1)

        def pick(dve, v, val, eq, sel, top, first, rev, m, n):
            wide = lambda t: t.unsqueeze(2).broadcast_to([P, m, n])
            v.link(dve.tensor_reduce(top, val, AX.X, ALU.max))
            v.link(dve.tensor_tensor(eq, val, wide(top), ALU.is_equal))
            v.link(dve.tensor_tensor(eq, eq, rev.unsqueeze(1).broadcast_to([P, m, n]), ALU.mult))
            v.link(dve.tensor_reduce(first, eq, AX.X, ALU.max))
            v.link(dve.tensor_tensor(sel, eq, wide(first), ALU.is_equal))
            v.link(dve.scalar_tensor_tensor(out=val, in0=sel, scalar=NEG, in1=val, op0=ALU.mult, op1=ALU.add))

        @block.vector
        def _(dve):
            v = Chain(dve, s_v)
            dve.memset(zero[:], 0.0).then_inc(s_zero, 1)
            dve.wait_ge(s_x, 16)
            ln_stats(dve, v, x, 1)
            ln_apply(dve, v, xn[:], x[:]).then_inc(s_xn, 1)
            dve.wait_ge(s_con, 16)
            dve.wait_ge(s_par, 16)
            dve.tensor_copy(ident_bf[:], C("ident")).then_inc(s_bc, 1)
            dve.tensor_copy(future_bf[:], C("future").unsqueeze(1).broadcast_to([P, 4, P])).then_inc(s_bc, 1)
            dve.tensor_copy(rd(dlt[:]), C("of_head").unsqueeze(2).broadcast_to([P, H0, P])).then_inc(s_bc, 1)
            dve.tensor_copy(before_bf[:], C("before")).then_inc(s_bc, 1)
            dve.memset(ones_bf[:], 1.0).then_inc(s_bc, 1)
            dve.memset(ahl[:, 2 * P:], 1.0).then_inc(s_bc, 1)
            dve.tensor_tensor(gwc[:], A("gwk"), A("gwv"), ALU.add).then_inc(s_bc, 1)
            dve.wait_ge(s_tg, 1)
            dve.tensor_scalar(lnsg[:], A("ln_scale"), tg[:, 0:1], None, ALU.mult).then_inc(s_bc, 1)
            dve.wait_ge(s_bc, 8)
            for i in range(4):
                dve.wait_ge(s_tr, i + 1)
                dve.tensor_copy(xT[:, bass.ts(i, 512)], ps[i][:]).then_inc(s_xT, 1)

            IG, FG, AZ, EZ, L, LF, CS, AA, MM, ONE = range(10)
            g = lambda i: g64[:, i, :]
            dve.memset(g(ONE), 1.0).then_inc(s_v, 1)
            v.n += 1
            dve.wait_ge(s_g64, 16 * 2 * B)
            dve.tensor_scalar(g(FG), g(FG), par[0:BH, PARAM["gate_b"][0] + 1:PARAM["gate_b"][1]], None,
                              ALU.add).then_inc(s_z, 1)
            dve.wait_ge(s_z, 1)
            v.link(dve.tensor_scalar(g(LF), g(FG), 0.0, None, ALU.min))
            dve.wait_ge(s_sp, 1)
            v.link(dve.tensor_tensor(g(LF), g(LF), g(L), ALU.subtract))
            v.link(dve.tensor_tensor_scan(g(CS), g(ONE), g(LF), 0.0, ALU.mult, ALU.add))
            v.link(dve.scalar_tensor_tensor(out=g(AA), in0=g(IG), scalar=par[0:BH, PARAM["gate_b"][0]:PARAM["gate_b"][0] + 1],
                                            in1=g(CS), op0=ALU.add, op1=ALU.subtract))
            v.link(dve.tensor_tensor_scan(g(MM), g(ONE), g(AA), LOWEST, ALU.mult, ALU.max))
            v.link(dve.tensor_scalar(negM[:, 0:1], g64[:, MM, P - 1:P], -1.0, None, ALU.mult))
            dve.tensor_tensor(g(CS), g(CS), g(MM), ALU.add).then_inc(s_aM, 1)
            v.link(dve.tensor_copy(rd(ahl[0:BH, 0:S]), g(AA)))
            v.link(dve.tensor_copy(rd(mhl[0:BH, :]), g(MM)))
            v.link(dve.tensor_tensor(rd(ahl[BH:P, 0:S]), g(AA), ahl[0:BH, 0:S], ALU.subtract))
            v.link(dve.tensor_tensor(rd(mhl[BH:P, :]), g(MM), mhl[0:BH, :], ALU.subtract))
            dve.tensor_tensor(rd(Rm[:]), mhl[:].unsqueeze(1).broadcast_to([P, H0, S]),
                              C("neg_of_head").unsqueeze(2).broadcast_to([P, H0, S]), ALU.mult).then_inc(s_bc, 1)
            dve.wait_ge(s_wps, 4)
            dve.tensor_copy(wT[:], ps[0][:, 0:4 * BH].rearrange("p (c r) -> p c r", r=BH)).then_inc(s_wT, 1)
            dve.wait_ge(s_wT, 1)
            dve.wait_ge(s_va, 16)

            vh = lambda t: t.rearrange("p (h w) -> p h w", w=VW)

            def prepare(it, i):
                b = it * 2 + i
                dve.wait_ge(s_free, it * 2 + (i + 1))
                dve.tensor_scalar(rd(LS[i][:]), ahl[:], con[:, bass.ds(CONST["of_seq"][0] + b, 1)], None,
                                  ALU.mult).then_inc(s_ls, 1)
                dve.tensor_tensor(Ks[i][:].rearrange("p (h d) -> p h d", d=DH0),
                                  vh(vaug[:, b * CH, :])[:, :, 0:DH0],
                                  wT[:, 0, bass.ds(b * H0, H0)].unsqueeze(2).broadcast_to([P, H0, DH0]),
                                  ALU.mult).then_inc(s_ks, 1)

            with dve.Fori(0, B // 2) as it:
                for i in range(2):
                    prepare(it, i)
                for u in range(4):
                    i, c = u // 2, u % 2
                    b = it * 2 + i
                    dve.wait_ge(s_S, it * 4 + (u + 1))
                    dve.wait_ge(s_D, it * 4 + (u + 1))
                    dve.wait_ge(s_PV, it * 4 + (u + 1))
                    dve.tensor_tensor(Cm[u % 2][:], pw[1][:], Dm[u % 2][:], ALU.mult).then_inc(s_C, 1)
                    if c == 0:
                        dve.wait_ge(s_st, it * 2 + (i + 1))
                        dve.tensor_tensor(stm[:], ps[1][:, 0:H0 * VW], C("quarter_block"), ALU.mult).then_inc(s_stm, 1)
                        dve.wait_ge(s_PV, it * 4 + (u + 3))
                        dve.tensor_copy(num[:, b * CH, :], ps[0][:, 0:H0 * VW]).then_inc(s_num, 1)
                    else:
                        dve.wait_ge(s_I, it * 2 + (i + 1))
                        dve.tensor_tensor(vh(tmp[:]), vh(ps[1][:, 256:256 + H0 * VW]),
                                          wT[:, 1, bass.ds(b * H0, H0)].unsqueeze(2).broadcast_to([P, H0, VW]),
                                          ALU.mult).then_inc(s_It, 1)
                        dve.wait_ge(s_It, it * 2 + (i + 1))
                        dve.wait_ge(s_PV, it * 4 + (u + 3))
                        dve.tensor_tensor(num[:, b * CH + 1, :], tmp[:], ps[0][:, 0:H0 * VW], ALU.add).then_inc(s_num, 1)
            dve.wait_ge(s_num, NT)

            n4 = num[:].rearrange("p t (h w) -> p (t h) w", w=VW)
            th = lambda t: t.rearrange("p (b c h) -> p b c h", c=CH, h=H0)
            v.link(dve.tensor_scalar(den[:], n4[:, :, DH0], -1.0, None, ALU.mult))
            v.link(dve.tensor_tensor(den[:], den[:], n4[:, :, DH0], ALU.max))
            v.link(dve.tensor_tensor(th(den[:]), th(den[:]), wT[:, 2:4, :].rearrange("p c (b h) -> p b c h", h=H0), ALU.max))
            v.link(dve.tensor_scalar(den[:], den[:], NORM_EPS, None, ALU.add))
            v.link(dve.reciprocal(den[:], den[:]))
            v.link(dve.tensor_tensor(xn[:].rearrange("p t (h d) -> p (t h) d", d=DH0), n4[:, :, 0:DH0],
                                     den[:].unsqueeze(2).broadcast_to([P, NT * H0, DH0]), ALU.mult))
            ln_stats(dve, v, xn, 2)
            v.link(ln_apply(dve, v, xn[:], xn[:]))
            v.link(dve.tensor_tensor(xn[:], xn[:], lnsg[:].unsqueeze(1).broadcast_to([P, NT, D]), ALU.mult))
            dve.tensor_tensor(x[:], x[:], xn[:], ALU.add).then_inc(s_x1, 1)
            dve.wait_ge(s_x1, 1)
            if stage == 1:
                return

            dve.wait_ge(s_wl, 2 + 2 * E0)
            dve.wait_ge(s_clr, 16)
            ln_stats(dve, v, x, 3)
            ln_apply(dve, v, xn[:], x[:]).then_inc(s_xn, 1)
            te = lambda t: t.rearrange("p (t e) -> p t e", e=E0)
            tile1 = lambda t: t.unsqueeze(2).broadcast_to([P, NT, E0])
            pr, eq, s1, s2, tc, inc, pos, one = (rt[:, i, :] for i in range(8))
            dve.memset(one, 1.0).then_inc(s_v, 1)
            v.n += 1
            dve.wait_ge(s_lg, 1)
            lg = pw[0][:, 0:NT * E0]
            v.link(dve.tensor_reduce(sm[:, 0, :], te(lg), AX.X, ALU.max))
            dve.tensor_tensor(te(pr), te(lg), tile1(sm[:, 0, :]), ALU.subtract).then_inc(s_lx, 1)
            dve.wait_ge(s_ex, 1)
            v.link(dve.tensor_reduce(sm[:, 0, :], te(eq), AX.X, ALU.add))
            v.link(dve.reciprocal(sm[:, 1, :], sm[:, 0, :]))
            v.link(dve.tensor_tensor(te(pr), te(eq), tile1(sm[:, 1, :]), ALU.mult))
            pick(dve, v, te(pr), te(eq), te(s1), sm[:, 2, :], sm[:, 4, :], C("rev8"), NT, E0)
            pick(dve, v, te(pr), te(eq), te(s2), sm[:, 3, :], sm[:, 4, :], C("rev8"), NT, E0)
            dve.tensor_tensor(routed[:], s1, s2, ALU.add).then_inc(s_ro, 1)
            v.link(dve.tensor_tensor(sm[:, 4, :], sm[:, 2, :], sm[:, 3, :], ALU.add))
            v.link(dve.reciprocal(sm[:, 5, :], sm[:, 4, :]))
            v.link(dve.tensor_scalar(sm[:, 5, :], sm[:, 5, :], tg[:, 1:2], None, ALU.mult))
            for k in range(2):
                v.link(dve.tensor_tensor(share[:, k, :], sm[:, 2 + k, :], sm[:, 5, :], ALU.mult))
            et = lambda t: t.rearrange("p (e t) -> p e t", t=NT)
            dve.wait_ge(s_rk, 1)
            v.link(dve.tensor_copy(et(tc), ps[0][:, P:2 * P].rearrange("p (t e) -> p e t", e=E0)))
            v.link(dve.tensor_tensor_scan(inc, C("not_first"), tc, 0.0, ALU.mult, ALU.add))
            v.link(dve.tensor_tensor(et(pos), et(inc)[:, :, NT - 1].unsqueeze(2).broadcast_to([P, E0, NT]),
                                     C("block_start").unsqueeze(1).broadcast_to([P, E0, NT]), ALU.is_gt))
            v.link(dve.tensor_reduce(ex[:, 0, :], et(pos), AX.X, ALU.add))
            v.link(dve.tensor_tensor_scan(ex[:, 1, :], one[:, 0:E0], ex[:, 0, :], 0.0, ALU.mult, ALU.add))
            v.link(dve.tensor_tensor(ex[:, 2, :], ex[:, 1, :], ex[:, 0, :], ALU.subtract))
            v.link(dve.tensor_scalar(ex[:, 2, :], ex[:, 2, :], float(P), None, ALU.mult))
            v.link(dve.tensor_tensor(inc, inc, tc, ALU.subtract))
            v.link(dve.tensor_tensor(et(inc), et(inc), ex[:, 2, :].unsqueeze(2).broadcast_to([P, E0, NT]), ALU.add))
            v.link(dve.tensor_tensor(te(pos), te(ps[0][:, 0:P]), inc.rearrange("p (e t) -> p t e", t=NT), ALU.add))
            for k, s in enumerate((s1, s2)):
                v.link(dve.tensor_tensor(eq, s, pos, ALU.mult))
                v.link(dve.tensor_reduce(sm[:, 6 + k, :], te(eq), AX.X, ALU.add))
                dve.tensor_copy(slot[:, k, :], sm[:, 6 + k, :]).then_inc(s_sl, 1)
            b3 = lambda t: t.rearrange("p (j e) -> p j e", e=E0)
            v.link(dve.tensor_tensor(b3(cmpb[0:1, :]), b3(C("block_index")[0:1, :]),
                                     ex[0:1, 1, :].unsqueeze(1).broadcast_to([1, NBLK, E0]), ALU.is_ge))
            v.link(dve.tensor_reduce(bcol[:, 0, :], b3(cmpb[0:1, :]), AX.X, ALU.add))
            v.link(dve.tensor_scalar(bcol[:, 1, :], bcol[:, 0, :], float(E0 - 1), float(F0), ALU.min, ALU.mult))
            dve.tensor_copy(boff[:], bcol[:, 1, :]).then_inc(s_be, 1)

            def split_tokens(j, i):
                dve.wait_ge(s_T, j + 1)
                ge(dve, s_U, j - 1)
                dve.tensor_copy(rd(xgh[i][:]), ps[0][:, 0:P]).then_inc(s_xp, 1)
                dve.wait_ge(s_xp, j * 2 + 1)
                dve.tensor_tensor(rd(xgl[i][:]), ps[0][:, 0:P], xgh[i][:], ALU.subtract).then_inc(s_xp, 1)

            def hidden(j, i):
                dve.wait_ge(s_U, j + 1)
                dve.wait_ge(s_sg, j + 1)
                ge(dve, s_H, j - 1)
                dve.tensor_tensor(hb[i][:], sg[i][:], pw[1][:, i * F0:(i + 1) * F0], ALU.mult).then_inc(s_hb, 1)

            def block_out(j, i):
                dve.wait_ge(s_Y, j + 1)
                if isinstance(j, int):
                    ge(dve, s_ys[i], 16 * (j // 2))
                else:
                    dve.wait_ge(s_ys[i], (j - i) * 8)
                dve.tensor_copy(yb[i][:], ps[3][:, 0:P]).then_inc(s_yb, 1)

            pipelined(dve, NBLK, [(split_tokens, -1), (hidden, 0), (block_out, 2)])
            for t in range(NT):
                dve.wait_ge(s_gy[t], 32)
                dve.scalar_tensor_tensor(out=xn[:, t, :], in0=gy[0][:, t, :], scalar=share[:, 0, t:t + 1],
                                         in1=x[:, t, :], op0=ALU.mult, op1=ALU.add).then_inc(s_v, 1)
                v.n += 1
                dve.wait_ge(s_v, v.value())
                dve.scalar_tensor_tensor(out=x[:, t, :], in0=gy[1][:, t, :], scalar=share[:, 1, t:t + 1],
                                         in1=xn[:, t, :], op0=ALU.mult, op1=ALU.add).then_inc(s_x2, 1)
            dve.wait_ge(s_x2, NT)
            if stage == 2:
                return

            for i in range(2):
                dve.memset(Kd[i][:], 0.0).then_inc(c_z, 1)
                dve.memset(vp[i][:], 0.0).then_inc(c_z, 1)
            dve.memset(Qd[:], 0.0).then_inc(c_z, 1)
            dve.memset(mp[:], 0.0).then_inc(c_z, 1)
            dve.wait_ge(c_z, 6)
            for i in range(2):
                dve.memset(vp[i][:, :, :, DH1:DH1 + 1], 1.0).then_inc(c_z, 1)
            dve.wait_ge(c_z, 8)
            ln_stats(dve, v, x, 4)
            ln_apply(dve, v, xn[:], x[:]).then_inc(s_xn, 1)
            v.link(dve.tensor_scalar(bqs[:], A("bq"), float(DH1) ** -0.5, None, ALU.mult))
            dve.wait_ge(c_w, 48)
            v.link(dve.tensor_reduce(wem[:], we[:].rearrange("p e d -> p d e"), AX.X, ALU.add))
            v.link(dve.tensor_scalar(wem[:], wem[:], tg[:, 2:3], 1.0 / EO, ALU.mult, ALU.mult))
            v.link(dve.tensor_reduce(bem[:], A("be"), AX.X, ALU.add))
            v.link(dve.tensor_scalar(bem[:], bem[:], tg[:, 2:3], 1.0 / EO, ALU.mult, ALU.mult))
            dve.tensor_copy(bemb[:], bem[:, 0:1].broadcast_to([P, P])).then_inc(c_wa, 1)
            dve.wait_ge(c_wp, 1)
            dve.tensor_copy(wc[:], ps[0][:, 0:P]).then_inc(c_wc, 1)
            dve.scalar_tensor_tensor(out=cb[:], in0=A("bo"), scalar=tg[:, 2:3], in1=ps[0][:, P:2 * P],
                                     op0=ALU.mult, op1=ALU.add).then_inc(c_wc, 1)
            dve.wait_ge(c_wc, 2)
            dve.wait_ge(s_xn, 3)
            v.link(dve.tensor_tensor(x[:], x[:], cb[:].unsqueeze(1).broadcast_to([P, NT, D]), ALU.add))

            def take_max(b, i):
                for n in range(8):
                    sc, g = n // HG, n % HG
                    dve.wait_ge(c_P1, b * 8 + (n + 1))
                    if n == 0:
                        ge(dve, c_mp, b * 2)
                    dve.tensor_reduce(mx[:, sc, g * HJ:(g + 1) * HJ], pw[0][:].rearrange("p (j t) -> p j t", t=S),
                                      AX.X, ALU.max).then_inc(c_R, 1)
                dve.wait_ge(c_R, b * 8 + 8)
                ge(dve, c_MT, b)
                col = lambda k: mp[:].rearrange("p c g (j r) -> p c (g j) r", r=ST)[:, :, :, SM + k]
                dve.tensor_scalar(rd(col(0)), mx[:], -1.0, None, ALU.mult).then_inc(c_mp, 1)
                dve.wait_ge(c_mp, b * 2 + 1)
                dve.scalar_tensor_tensor(out=rd(col(1)), in0=mx[:], scalar=-1.0, in1=col(0),
                                         op0=ALU.mult, op1=ALU.subtract).then_inc(c_mp, 1)

            def split_keys(b, i):
                dve.wait_ge(c_k32, b * HG + HG)
                dve.tensor_copy(rd(khi[:]), k32[:]).then_inc(c_khi, 1)
                dve.wait_ge(c_khi, b + 1)
                dve.scalar_tensor_tensor(out=rd(Kst[i][:]), in0=khi[:], scalar=C("key_lo"), in1=k32[:],
                                         op0=ALU.mult, op1=ALU.add).then_inc(c_ks, 1)
                dve.wait_ge(c_V, b + 1)
                dve.tensor_tensor(vp[i][:, :, :, 0:DH1],
                                  ps[2][:, 0:CH * D].rearrange("p (c h d) -> p c h d", h=H1, d=DH1),
                                  A("bv").rearrange("p (h d) -> p h d", d=DH1).unsqueeze(1).broadcast_to([P, CH, H1, DH1]),
                                  ALU.add).then_inc(c_vp, 1)

            def split_queries(b, i):
                dve.wait_ge(c_q32, b * HG + HG)
                dve.tensor_copy(rd(qhi[:]), q32[:]).then_inc(c_qhi, 1)
                dve.wait_ge(c_qhi, b + 1)
                dve.scalar_tensor_tensor(out=rd(Qs[i][:]), in0=qhi[:], scalar=C("query_lo"), in1=q32[:],
                                         op0=ALU.mult, op1=ALU.add).then_inc(c_qs, 1)

            def add_max(b, i):
                dve.wait_ge(c_MT, b + 1)
                dve.wait_ge(c_qs, b + 1)
                if isinstance(b, int):
                    ge(dve, c_qd, 64 * b)
                else:
                    dve.wait_ge(c_qd, b * 64)
                for k in range(2):
                    dve.tensor_tensor(rd(Q2[:, 2 * k:2 * k + 2, :]), Qs[i][:, 2 * k:2 * k + 2, :],
                                      ps[2 + k][:].rearrange("p (g s) -> p g s", s=S), ALU.add).then_inc(c_q2, 1)

            def normalize(b, i):
                dve.wait_ge(c_OT, b + 1)
                for c in range(CH):
                    o = ps[c][:].rearrange("p (h r) -> p h r", r=ST)
                    dve.reciprocal(rec[:, c, :], o[:, :, DH1]).then_inc(c_rec, 1)
                dve.wait_ge(c_rec, b * 2 + 2)
                ge(dve, c_nT, b)
                for c in range(CH):
                    o = ps[c][:].rearrange("p (h r) -> p h r", r=ST)
                    dve.tensor_tensor(on[:, c, :].rearrange("p (h d) -> p h d", d=DH1), o[:, :, 0:DH1],
                                      rec[:, c, :].unsqueeze(2).broadcast_to([P, H1, DH1]), ALU.mult).then_inc(c_on, 1)

            def residual3(b, i):
                dve.wait_ge(c_Y, b + 1)
                dve.tensor_tensor(x[:, bass.ds(b * CH, CH), :], x[:, bass.ds(b * CH, CH), :],
                                  ps[3][:, 0:CH * D].rearrange("p (c d) -> p c d", d=D), ALU.add).then_inc(s_x3, 1)

            pipelined(dve, B, [(take_max, 0), (split_keys, -1), (split_queries, -1), (add_max, 0),
                               (normalize, 1), (residual3, 1)])
            dve.wait_ge(s_x3, B)
            if stage == 3:
                return

            ln_stats(dve, v, x, 5)
            ln_apply(dve, v, xn[:], x[:]).then_inc(s_xn, 1)
            dve.memset(cT[:], 0.0).then_inc(d_c, 1)
            dve.tensor_copy(rd(ecol[:]), C("expert_cols")).then_inc(d_c, 1)
            for i in range(4):
                at = slice(i * 512, (i + 1) * 512)
                dve.wait_ge(s_xT, 13 + i)
                v.link(dve.tensor_copy(rd(xTh[:, at]), xT[:, at]))
                dve.tensor_tensor(rd(xTl[:, at]), xT[:, at], xTh[:, at], ALU.subtract).then_inc(d_xT, 1)
            SC, SB, MK, EQ, SEL, ACC = (r1[:, i, :] for i in range(6))
            te = lambda t: t.rearrange("p (t e) -> p t e", e=E1)
            dve.wait_ge(d_sg, 1)
            v.link(dve.tensor_scalar(SC, SC, 1.0, None, ALU.add))
            v.link(dve.reciprocal(SC, SC))
            v.link(dve.tensor_tensor(te(SB), te(SC), A("e_bias").unsqueeze(1).broadcast_to([P, NT, E1]), ALU.add))
            q4 = SB.rearrange("p (m k) -> p m k", k=NG1)
            W = [r4[:, i, :] for i in range(12)]
            v.link(dve.tensor_tensor(W[0], q4[:, :, 0], q4[:, :, 1], ALU.max))
            v.link(dve.tensor_tensor(W[1], q4[:, :, 0], q4[:, :, 1], ALU.min))
            v.link(dve.tensor_tensor(W[2], q4[:, :, 2], q4[:, :, 3], ALU.max))
            v.link(dve.tensor_tensor(W[3], q4[:, :, 2], q4[:, :, 3], ALU.min))
            v.link(dve.tensor_tensor(W[4], W[0], W[2], ALU.max))
            v.link(dve.tensor_tensor(W[5], W[0], W[2], ALU.min))
            v.link(dve.tensor_tensor(W[6], W[1], W[3], ALU.max))
            v.link(dve.tensor_tensor(W[5], W[5], W[6], ALU.max))
            v.link(dve.tensor_tensor(W[4], W[4], W[5], ALU.add))
            g3 = lambda t: t.rearrange("p (t g) -> p t g", g=NG1)
            rev4 = C("rev8")[:, E0 - NG1:]
            pick(dve, v, g3(W[4]), g3(W[7]), g3(W[8]), s4[:, 0, :], s4[:, 1, :], rev4, NT, NG1)
            pick(dve, v, g3(W[4]), g3(W[7]), g3(W[9]), s4[:, 0, :], s4[:, 1, :], rev4, NT, NG1)
            v.link(dve.tensor_tensor(W[8], W[8], W[9], ALU.add))
            v.link(dve.tensor_tensor(MK.rearrange("p (m k) -> p m k", k=NG1), q4,
                                     W[8].unsqueeze(2).broadcast_to([P, NT * NG1, NG1]), ALU.mult))
            for k in range(K1):
                pick(dve, v, te(MK), te(EQ), te(SEL if k else ACC), s4[:, 0, :], s4[:, 1, :], C("rev16"), NT, E1)
                if k:
                    v.link(dve.tensor_tensor(ACC, ACC, SEL, ALU.add))
            v.link(dve.tensor_tensor(ACC, ACC, SC, ALU.mult))
            v.link(dve.tensor_reduce(s4[:, 2, :], te(ACC), AX.X, ALU.add))
            v.link(dve.tensor_scalar(s4[:, 2, :], s4[:, 2, :], 1e-20, None, ALU.add))
            v.link(dve.reciprocal(s4[:, 3, :], s4[:, 2, :]))
            v.link(dve.tensor_scalar(s4[:, 3, :], s4[:, 3, :], SHARE1, None, ALU.mult))
            v.link(dve.tensor_tensor(te(ACC), te(ACC), s4[:, 3, :].unsqueeze(2).broadcast_to([P, NT, E1]), ALU.mult))
            v.link(dve.tensor_copy(rd(chl[:, :, 0:E1]), te(ACC)))
            dve.tensor_tensor(rd(chl[:, :, E1:]), te(ACC), chl[:, :, 0:E1], ALU.subtract).then_inc(d_cm, 1)
            for i in range(4):
                dve.wait_ge(d_cT, i + 1)
                dve.tensor_copy(rd(cT[0:2 * E1, i * 512:(i + 1) * 512]), ps[i][0:2 * E1, :]).then_inc(d_cc, 1)

            with dve.Fori(0, T // TT // 2) as it:
                for k in range(2):
                    for c in range(FC1):
                        n = k * FC1 + c
                        dve.wait_ge(d_U, it * (2 * FC1) + (n + 1))
                        dve.wait_ge(d_sl, it * (2 * FC1) + (n + 1))
                        if c == 0:
                            dve.wait_ge(d_Y, it * 2 + (k + 1))
                        if c == FC1 - 1:
                            dve.tensor_tensor(hT1[k][:, c, :], sg1[n % 2][:], pw[1][:, n % 2 * TT:(n % 2 + 1) * TT],
                                              ALU.mult).then_inc(d_h1, 1)
                            dve.wait_ge(d_h1, it * (2 * FC1) + (n + 3))
                            continue
                        dve.tensor_tensor(h1[n % 2][:], sg1[n % 2][:], pw[1][:, n % 2 * TT:(n % 2 + 1) * TT],
                                          ALU.mult).then_inc(d_h1, 1)
                        dve.wait_ge(d_h1, it * (2 * FC1) + (n + 3))
                        dve.tensor_tensor(hT1[k][:, c, :], h1[n % 2][:], ps[c % 2][:], ALU.mult).then_inc(d_h, 1)
                    dve.wait_ge(d_Y, it * 2 + (k + 3))
                    at = bass.ds((it * 2 + k) * (TT // P), TT // P)
                    dve.scalar_tensor_tensor(out=x[:, at, :], in0=ps[2 + k][:].rearrange("p (t d) -> p t d", d=D),
                                             scalar=tg[:, 3:4], in1=x[:, at, :], op0=ALU.mult, op1=ALU.add)\
                        .then_inc(d_x4, 1)

        @block.scalar
        def _(act):
            ch = Chain(act, s_a)
            ln_power(act, ch, 1)
            act.wait_ge(s_par, 16)
            act.activation(tg[:], A("gates"), ACT.Tanh).then_inc(s_tg, 1)
            for i in range(4):
                act.wait_ge(s_gps, i + 1)
                bank = (pw[0][:, 0:512], pw[0][:, 512:1024], pw[1][:, 0:512], pw[1][:, 512:1024])[i]
                act.activation(xn_gates(xn)[:, i * 512:(i + 1) * 512], bank[0:2 * H0, :], ACT.Copy).then_inc(s_gT, 1)
            IG, FG, AZ, EZ, L, LF, CS, AA, MM, ONE = range(10)
            g = lambda i: g64[:, i, :]
            act.wait_ge(s_z, 1)
            ch.link(act.activation(g(AZ), g(FG), ACT.Abs))
            ch.link(act.activation(g(EZ), g(AZ), ACT.Exp, scale=-1.0))
            act.activation(g(L), g(EZ), ACT.Ln, bias=1.0).then_inc(s_sp, 1)
            act.wait_ge(s_aM, 1)
            act.activation(t64[:, 0:P], g64[:, AA, 0:P], ACT.Exp, bias=negM[:, 0:1]).then_inc(s_t64, 1)
            act.activation(t64[:, 2 * P:], g(CS), ACT.Exp, scale=-1.0).then_inc(s_t64, 1)
            act.activation(t64[:, P:2 * P], g64[:, MM, P:S], ACT.Exp, bias=g64[:, MM, P - 1:P], scale=-1.0)\
               .then_inc(s_t64, 1)
            with act.Fori(0, B // 2) as it:
                for u in range(4):
                    if u % 2 == 0:
                        act.wait_ge(s_free, it * 2 + (u // 2 + 1))
                        act.activation(qS[u // 2][:], xT[:, bass.ds((it * 2 + u // 2) * S + P, P)], ACT.Copy)\
                            .then_inc(s_qS, 1)
                    act.wait_ge(s_E, it * 4 + (u + 1))
                    act.wait_ge(s_C, it * 4 + (u + 1))
                    act.activation(Dm[u % 2][:], pw[0][:], ACT.Exp).then_inc(s_D, 1)
                    act.wait_ge(s_w[u % 2], it * 32 + (16 * (u // 2 + 1)))
                    act.activation(rd(wh[:, bass.ds((it * 4 + u) * F0, F0)]), wst[u % 2][:], ACT.Copy)\
                        .then_inc(s_wh, 1)
            ln_power(act, ch, 2)
            if stage == 1:
                return

            ln_power(act, ch, 3)
            for i in range(4):
                act.wait_ge(s_tr, 5 + i)
                act.activation(xT[:, i * 512:(i + 1) * 512], ps[i][:], ACT.Copy).then_inc(s_xT, 1)
            act.wait_ge(s_lx, 1)
            act.activation(rt[:, 1, :], rt[:, 0, :], ACT.Exp).then_inc(s_ex, 1)

            def silu(j, i):
                act.wait_ge(s_G, j + 1)
                ge(act, s_hb, j - 1)
                act.activation(sg[i][:], pw[0][:, i * F0:(i + 1) * F0], ACT.Silu).then_inc(s_sg, 1)

            def copy_hidden(j, i):
                act.wait_ge(s_H, j + 1)
                ge(act, s_Y, j - 1)
                act.activation(hT[i][:], ps[1 + i][:], ACT.Copy).then_inc(s_hT, 1)

            pipelined(act, NBLK, [(silu, 0), (copy_hidden, 1)], peel=1)
            if stage == 2:
                return

            ln_power(act, ch, 4)
            for i in range(4):
                act.wait_ge(s_tr, 9 + i)
                act.activation(xT[:, i * 512:(i + 1) * 512], ps[i][:], ACT.Copy).then_inc(s_xT, 1)

            def exponentials(b, i):
                for n in range(8):
                    g, c = n // CH, n % CH
                    act.wait_ge(c_P2, b * 8 + (n + 1))
                    ge(act, c_PV, b * 4 + (g - 1))
                    act.activation(et3[g % 2][c][:], pw[1][:].rearrange("p (j s) -> p j s", s=S), ACT.Exp)\
                        .then_inc(c_X, 1)
                    if n == 5:
                        copy_sums(b, 0)

            def copy_sums(b, k):
                act.wait_ge(c_PV, b * 4 + (2 * k + 2))
                if k == 0:
                    ge(act, c_OT, b)
                act.activation(o32[:, 2 * k:2 * k + 2, :], ps[2 + k][:].rearrange("p (g s) -> p g s", s=S), ACT.Copy)\
                    .then_inc(c_O, 1)

            def copy_keys(b, i):
                act.wait_ge(c_K, b + 1)
                ge(act, c_ks, b)
                for g in range(HG):
                    act.activation(k32[:, g, :], ps[g // 2][:, g % 2 * S:(g % 2 + 1) * S], ACT.Identity,
                                   bias=A("bk")[:, g:g + 1]).then_inc(c_k32, 1)

            def copy_queries(b, i):
                act.wait_ge(c_Q, b + 1)
                ge(act, c_qs, b)
                for g in range(HG):
                    act.activation(q32[:, g, :], ps[g // 2][:, g % 2 * S:(g % 2 + 1) * S], ACT.Identity,
                                   bias=bqs[:, g:g + 1], scale=float(DH1) ** -0.5).then_inc(c_q32, 1)

            def copy_last_sums(b, i):
                copy_sums(b, 1)

            def copy_turned(b, i):
                act.wait_ge(c_nT, b + 1)
                ge(act, c_Y, b)
                act.activation(onT[:], ps[2][:, 0:CH * P].rearrange("p (c s) -> p c s", s=P), ACT.Copy)\
                    .then_inc(c_nc, 1)

            act.wait_ge(c_wc, 2)
            pipelined(act, B, [(exponentials, 1), (copy_last_sums, 1), (copy_keys, -1), (copy_queries, -1),
                               (copy_turned, 1)], peel=1)
            if stage == 3:
                return

            act.wait_ge(s_x3, B)
            ln_power(act, ch, 5)
            for i in range(4):
                act.wait_ge(s_tr, 13 + i)
                act.activation(xT[:, i * 512:(i + 1) * 512], ps[i][:], ACT.Copy).then_inc(s_xT, 1)
            act.wait_ge(d_w, 32)
            for k in range(2):
                at = slice(k * FC1 * P, (k + 1) * FC1 * P)
                act.activation(rd(guh[:, at]), graw[:, at], ACT.Copy).then_inc(d_wh, 1)
            act.wait_ge(d_lg, 1)
            act.activation(r1[:, 0, :], pw[0][:, 0:NT * E1], ACT.Exp, scale=-1.0).then_inc(d_sg, 1)
            with act.Fori(0, T // TT // 2) as it:
                for n in range(2 * FC1):
                    act.wait_ge(d_G, it * (2 * FC1) + (n + 1))
                    act.wait_ge(d_h1, it * (2 * FC1) + (n + 1))
                    act.activation(sg1[n % 2][:], pw[0][:, n % 2 * TT:(n % 2 + 1) * TT], ACT.Silu).then_inc(d_sl, 1)

        @block.gpsimd
        def _(pool):
            pool.sem_inc(s_free, 2)
            pool.sem_inc(s_PV, 2)
            pool.sem_inc(s_C, 2)
            pool.sem_inc(s_wl, 2)
            pool.wait_ge(s_xT, 4)
            with pool.Fori(0, B // 2) as it:
                for i in range(2):
                    b = it * 2 + i
                    pool.wait_ge(s_free, it * 2 + (i + 1))
                    pool.tensor_tensor(Qm[i][:], xT[:, bass.ds(b * S, S)].unsqueeze(1).broadcast_to([P, H0, S]),
                                       C("quarter_of_head").unsqueeze(2).broadcast_to([P, H0, S]), ALU.mult)\
                        .then_inc(s_qm, 1)
                    for u in (2 * i, 2 * i + 1):
                        pool.wait_ge(s_wh, it * 4 + (u + 1))
                        at = bass.ds((it * 4 + u) * F0, F0)
                        pool.tensor_tensor(rd(wl[:, at]), wst[u % 2][:], wh[:, at], ALU.subtract).then_inc(s_wl, 1)

            if stage == 1:
                return
            pool.wait_ge(s_clr, 16)
            pool.wait_ge(s_xn, 2)
            for k in range(2):
                pool.wait_ge(s_sl, k + 1)
                for t in range(NT):
                    pool.indirect_dma_start(out=scr_x, out_offset=bass.IndirectOffsetOnAxis(slot[:, k, t:t + 1], axis=0),
                                            in_=xn[:, t, :], in_offset=None).then_inc(s_sc, 16)
            for i in range(2):
                pool.wait_ge(s_ys[i], 16 * (NBLK // 2))
            for t in range(NT):
                for k in range(2):
                    pool.indirect_dma_start(out=gy[k][:, t, :], out_offset=None, in_=scr_y,
                                            in_offset=bass.IndirectOffsetOnAxis(slot[:, k, t:t + 1], axis=0))\
                        .then_inc(s_gy[t], 16)
            if stage <= 3:
                return
            pool.sem_inc(d_Y, 2)
            pool.sem_inc(d_h1, 2)
            pool.sem_inc(d_h, 2)
            for k in range(2):
                at = slice(k * FC1 * P, (k + 1) * FC1 * P)
                pool.wait_ge(d_wh, k + 1)
                pool.tensor_tensor(rd(gul[:, at]), graw[:, at], guh[:, at], ALU.subtract).then_inc(d_wl, 1)

        @block.tensor
        def _(pe):
            pe.wait_ge(s_con, 16)
            pe.wait_ge(s_xn, 1)
            for i in range(4):
                for k in range(4):
                    ins = pe.transpose(ps[i][:, k * P:(k + 1) * P], xn[:, 4 * i + k, :], C("ident"))
                ins.then_inc(s_tr, 1)
            pe.wait_ge(s_ctx, 16)
            pe.wait_ge(s_bc, 8)
            for i in range(4):
                bank = (pw[0][:, 0:512], pw[0][:, 512:1024], pw[1][:, 0:512], pw[1][:, 512:1024])[i]
                pe.wait_ge(s_xT, i + 1)
                pe.matmul(bank[0:2 * H0, :], A("gwq"), xT[:, i * 512:(i + 1) * 512], start=True, stop=False)
                pe.matmul(bank[0:2 * H0, :], gwc[:], ctxT[:, i * 512:(i + 1) * 512], start=False, stop=True)\
                    .then_inc(s_gps, 1)
            pe.wait_ge(s_t64, 3)
            for k in range(4):
                pe.transpose(ps[0][:, k * BH:(k + 1) * BH], t64[:, k * P:(k + 1) * P], C("ident")[0:BH, 0:BH])\
                    .then_inc(s_wps, 1)
            pe.wait_ge(s_bc, 9)
            pe.wait_ge(s_wT, 1)
            pe.wait_ge(s_gT, 4)

            def exponent(it, u):
                i, c = u // 2, u % 2
                if c == 0:
                    pe.wait_ge(s_ls, it * 2 + (i + 1))
                if u:
                    pe.wait_ge(s_D, it * 4 + u)
                for half in range(2):
                    o = pw[0][:, half * 512:(half + 1) * 512]
                    hs = slice(4 * half, 4 * half + 4)
                    pe.matmul(o, ident_bf[:], future_bf[:], start=True, stop=False)
                    pe.matmul(o, rd(LS[i][:, 2 * P:]), rd(Rm[:, hs, c * P:(c + 1) * P]), start=False, stop=False)
                    ins = pe.matmul(o, rd(LS[i][:, c * P:(c + 1) * P]), rd(dlt[:, hs, :]), start=False, stop=True)
                ins.then_inc(s_E, 1)

            with pe.Fori(0, B // 2) as it:
                exponent(it, 0)
                for u in range(4):
                    i, c = u // 2, u % 2
                    b = it * 2 + i
                    if c == 0:
                        pe.wait_ge(s_ct[i], it * 16 + 16)
                        pe.wait_ge(s_qm, it * 2 + (i + 1))
                    for half in range(2):
                        ins = pe.matmul(pw[1][:, half * 512:(half + 1) * 512], ctS[i][:, c * P:(c + 1) * P],
                                        Qm[i][:, 4 * half:4 * half + 4, c * P:(c + 1) * P], start=True, stop=True)
                    ins.then_inc(s_S, 1)
                    if c == 0:
                        pe.wait_ge(s_ks, it * 2 + (i + 1))
                        if i:
                            pe.wait_ge(s_It, it * 2 + 1)
                        pe.matmul(ps[1][:, 0:H0 * VW], Ks[i][:], vaug[:, b * CH, :], start=True, stop=True)\
                            .then_inc(s_st, 1)
                    if u < 3:
                        exponent(it, u + 1)
                    if c == 1:
                        pe.wait_ge(s_stm, it * 2 + (i + 1))
                        pe.wait_ge(s_qS, it * 2 + (i + 1))
                        pe.matmul(ps[1][:, 256:256 + H0 * VW], qS[i][:], stm[:], start=True, stop=True)\
                            .then_inc(s_I, 1)
                    pe.wait_ge(s_C, it * 4 + (u + 3))
                    if u:
                        pe.wait_ge(s_num, it * 4 + u)
                    for h in range(H0):
                        ins = pe.matmul(ps[0][:, h * VW:(h + 1) * VW], Cm[u % 2][:, h * P:(h + 1) * P],
                                        vaug[:, b * CH + c, h * VW:(h + 1) * VW], start=True, stop=True)
                    ins.then_inc(s_PV, 1)
                    if c == 1:
                        pe.matmul(ps[3][0:32, 0:2], ones_bf[:, 0:32], ones_bf[:, 0:2], start=True, stop=True)\
                            .then_inc(s_free, 1)
                pe.wait_ge(s_num, it * 4 + 4)
            if stage == 1:
                return

            pe.wait_ge(s_xn, 2)
            for i in range(4):
                for k in range(4):
                    ins = pe.transpose(ps[i][:, k * P:(k + 1) * P], xn[:, 4 * i + k, :], C("ident"))
                ins.then_inc(s_tr, 1)
            for t in range(NT):
                if t % 4 == 0:
                    pe.wait_ge(s_xT, 5 + t // 4)
                ins = pe.matmul(pw[0][:, t * E0:(t + 1) * E0], xT[:, t * P:(t + 1) * P], A("router0"),
                                start=True, stop=True)
            ins.then_inc(s_lg, 1)
            pe.wait_ge(s_ro, 1)
            pe.matmul(ps[0][:, 0:P], before_bf[:], routed[:], start=True, stop=True)
            pe.matmul(ps[0][:, P:2 * P], ones_bf[:], routed[:], start=True, stop=True).then_inc(s_rk, 1)
            pe.wait_ge(s_be, 1)
            pe.wait_ge(s_w2, 16)
            pe.wait_ge(s_wl, 2 + 2 * E0)

            def tokens(j, i):
                ge(pe, s_xp, j * 2)
                if isinstance(j, int):
                    pe.wait_ge(s_xg[i], 16 * (j // 2 + 1))
                else:
                    pe.wait_ge(s_xg[i], (j - i) * 8 + 16)
                pe.transpose(ps[0][:, 0:P], xg[i][:], C("ident")).then_inc(s_T, 1)

            def up(j, i):
                at = pe.value_load(boff[0:1, bass.ds(j, 1)], min_val=0, max_val=(E0 - 1) * F0)
                pe.wait_ge(s_xp, j * 2 + 2)
                for bank, m, free, ready in ((pw[0], 0, s_sg, s_G), (pw[1], 1, s_hb, s_U)):
                    o = bank[:, i * F0:(i + 1) * F0]
                    ge(pe, free, j - 1)
                    hi, lo = (w[:, bass.ds(at + m * E0 * F0, F0)] for w in (wh, wl))
                    pe.matmul(o, rd(xgh[i][:]), rd(hi), start=True, stop=False)
                    pe.matmul(o, rd(xgh[i][:]), rd(lo), start=False, stop=False)
                    pe.matmul(o, rd(xgl[i][:]), rd(hi), start=False, stop=True).then_inc(ready, 1)

            def turn_hidden(j, i):
                pe.wait_ge(s_hb, j + 1)
                ge(pe, s_hT, j - 1)
                for c in range(FC0):
                    ins = pe.transpose(ps[1 + i][:, c * P:(c + 1) * P], hb[i][:, c * P:(c + 1) * P], C("ident"))
                ins.then_inc(s_H, 1)

            def down(j, i):
                at = pe.value_load(boff[0:1, bass.ds(j, 1)], min_val=0, max_val=(E0 - 1) * F0)
                pe.wait_ge(s_hT, j + 1)
                ge(pe, s_yb, j)
                for c in range(FC0):
                    ins = pe.matmul(ps[3][:, 0:P], hT[i][:, c * P:(c + 1) * P], w2[:, bass.ds(at + c * D, D)],
                                    start=(c == 0), stop=(c == FC0 - 1))
                ins.then_inc(s_Y, 1)

            pipelined(pe, NBLK, [(up, 0), (tokens, -1), (turn_hidden, 1), (down, 2)])
            if stage == 2:
                return

            pe.wait_ge(s_xn, 3)
            pe.wait_ge(s_yb, NBLK)
            for i in range(4):
                for k in range(4):
                    ins = pe.transpose(ps[i][:, k * P:(k + 1) * P], xn[:, 4 * i + k, :], C("ident"))
                ins.then_inc(s_tr, 1)
            pe.wait_ge(c_wa, 1)
            pe.wait_ge(s_xT, 12)
            pe.matmul(ps[0][:, 0:P], wem[:], A("wo"), start=True, stop=True)
            pe.matmul(ps[0][:, P:2 * P], bemb[:], A("wo"), start=True, stop=True).then_inc(c_wp, 1)
            pe.wait_ge(c_wc, 2)

            def scores(b, i):
                for n in range(10):
                    if n < 8:
                        scores_for_max(b, i, n)
                    if n >= 2:
                        scores_less_max(b - 1, 1 - i, n - 2)
                    if n >= 4 and n % 2 == 0:
                        weighted_sums(b - 1, 1 - i, n // 2 - 2)

            def scores_for_max(b, i, n):
                sc, g = n // HG, n % HG
                if n == 0:
                    pe.wait_ge(c_qs, b + 1)
                    pe.wait_ge(c_kd[i], 64 * (b // 2 + 1) if isinstance(b, int) else (b - i) * 32 + 64)
                ge(pe, c_R, b * 8 + n)
                for k in range(2):
                    ins = pe.matmul(pw[0][:, k * 512:(k + 1) * 512], rd(Qs[i][:, g, sc * P:(sc + 1) * P]),
                                    rd(Kd[i][:, g, 2 * k:2 * k + 2, :]), start=True, stop=True)
                ins.then_inc(c_P1, 1)

            def scores_less_max(b, i, n):
                g, c = n // CH, n % CH
                if n == 0:
                    pe.wait_ge(c_qd, b * 64 + 64)
                ge(pe, c_X, b * 8 + n)
                for k in range(2):
                    ins = pe.matmul(pw[1][:, k * 512:(k + 1) * 512], rd(Kst[i][:, g, c * P:(c + 1) * P]),
                                    rd(Qd[:, g, 2 * k:2 * k + 2, :]), start=True, stop=True)
                ins.then_inc(c_P2, 1)

            def weighted_sums(b, i, g):
                pe.wait_ge(c_X, b * 8 + (2 * g + 2))
                if g == 0:
                    pe.wait_ge(c_q2, b * 2 + 2)
                    ge(pe, s_x3, b)
                for c in range(CH):
                    for j in range(HJ):
                        ins = pe.matmul(ps[2 + g // 2][j * ST:(j + 1) * ST, g % 2 * S:(g % 2 + 1) * S],
                                        vp[i][:, c, HJ * g + j, :], et3[g % 2][c][:, j, :],
                                        start=(c == 0), stop=(c == CH - 1), skip_group_check=True)
                ins.then_inc(c_PV, 1)

            def last_sums(b, i):
                weighted_sums(b, i, 3)

            def keys_values(b, i):
                pe.wait_ge(c_ct[i], 16 * (b // 2 + 1) if isinstance(b, int) else (b - i) * 8 + 16)
                ge(pe, c_on, (b - 1) * 2 - 2)
                for g in range(HG):
                    ins = pe.matmul(ps[g // 2][:, g % 2 * S:(g % 2 + 1) * S], wks[:, g * P:(g + 1) * P],
                                    ctxT[:, bass.ds(b * S, S)], start=True, stop=True)
                ins.then_inc(c_K, 1)
                ge(pe, c_O, (b - 1) * 2 - 1)
                for c in range(CH):
                    ins = pe.matmul(ps[2][:, c * D:(c + 1) * D], ctS[i][:, c * P:(c + 1) * P], A("wv"),
                                    start=True, stop=True)
                ins.then_inc(c_V, 1)

            def queries(b, i):
                pe.wait_ge(c_k32, b * HG + HG)
                for g in range(HG):
                    ins = pe.matmul(ps[g // 2][:, g % 2 * S:(g % 2 + 1) * S], wqs[:, g * P:(g + 1) * P],
                                    xT[:, bass.ds(b * S, S)], start=True, stop=True)
                ins.then_inc(c_Q, 1)

            def max_rows(b, i):
                pe.wait_ge(c_mp, b * 2 + 2)
                if isinstance(b, int) and b == B - 1:
                    pe.wait_ge(c_vp, B)
                else:
                    pe.wait_ge(c_vp, b + 2)
                ge(pe, c_O, b * 2)
                for g in range(HG):
                    for c in range(CH):
                        at = g % 2 * S + c * P
                        ins = pe.transpose(ps[2 + g // 2][:, at:at + P], mp[:, c, g, :], C("ident"))
                ins.then_inc(c_MT, 1)

            def turn_sums(b, i):
                pe.wait_ge(c_O, b * 2 + 2)
                if isinstance(b, int) and b >= B - 2:
                    pe.wait_ge(c_q32, B * HG)
                else:
                    pe.wait_ge(c_q32, b * HG + 3 * HG)
                for c in range(CH):
                    for g in range(HG):
                        ins = pe.transpose(ps[c][:, g * P:(g + 1) * P], o32[:, g, c * P:(c + 1) * P], C("ident"))
                ins.then_inc(c_OT, 1)

            def attention_out(b, i):
                pe.wait_ge(c_on, b * 2 + 2)
                pe.wait_ge(c_q2, (min(b + 1, B - 1) if isinstance(b, int) else b + 1) * 2 + 2)
                for c in range(CH):
                    ins = pe.transpose(ps[2][:, c * P:(c + 1) * P], on[:, c, :], C("ident"))
                ins.then_inc(c_nT, 1)
                pe.wait_ge(c_nc, b + 1)
                for c in range(CH):
                    ins = pe.matmul(ps[3][:, c * D:(c + 1) * D], onT[:, c, :], wc[:], start=True, stop=True)
                ins.then_inc(c_Y, 1)

            def first_scores(b, i):
                for n in range(8):
                    scores_for_max(b, i, n)

            def last_scores(b, i):
                for n in range(10):
                    if n < 8:
                        scores_less_max(b, i, n)
                    if n >= 2 and n % 2 == 0 and n < 8:
                        weighted_sums(b, i, n // 2 - 1)

            def both_scores(b, i):
                if isinstance(b, int) and b == 0:
                    first_scores(b, i)
                elif isinstance(b, int) and b == B:
                    last_scores(b - 1, 1 - i)
                else:
                    scores(b, i)

            pipelined(pe, B, [(both_scores, 0), (last_sums, 1), (keys_values, -1), (queries, -1),
                              (max_rows, 0), (turn_sums, 1), (attention_out, 1)], extra=both_scores)
            if stage == 3:
                return

            pe.wait_ge(s_xn, 4)
            for i in range(4):
                for k in range(4):
                    ins = pe.transpose(ps[i][:, k * P:(k + 1) * P], xn[:, 4 * i + k, :], C("ident"))
                ins.then_inc(s_tr, 1)
            for t in range(NT):
                if t % 4 == 0:
                    pe.wait_ge(s_xT, 13 + t // 4)
                ins = pe.matmul(pw[0][:, t * E1:(t + 1) * E1], xT[:, t * P:(t + 1) * P], A("router1"),
                                start=True, stop=True)
            ins.then_inc(d_lg, 1)
            pe.wait_ge(d_cm, 1)
            for i in range(4):
                for k in range(4):
                    ins = pe.transpose(ps[i][0:2 * E1, k * P:(k + 1) * P], chl[:, 4 * i + k, :], C("ident"))
                ins.then_inc(d_cT, 1)
            pe.wait_ge(d_cc, 4)
            pe.wait_ge(d_wl, 2)
            pe.wait_ge(d_c, 2)
            pe.wait_ge(d_xT, 4)

            def hidden_units(it, k, c):
                n = k * FC1 + c
                t = bass.ds((it * 2 + k) * TT, TT)
                half = slice(n % 2 * TT, (n % 2 + 1) * TT)
                for m, (bank, free, ready) in enumerate(((pw[0], d_sl, d_G), (pw[1], d_h1, d_U))):
                    if n >= 2:
                        pe.wait_ge(free, it * (2 * FC1) + (n - 1 + 2 * m))
                    f = slice((m * FC1 + c) * P, (m * FC1 + c + 1) * P)
                    pe.matmul(bank[:, half], rd(guh[:, f]), rd(xTh[:, t]), start=True, stop=False)
                    pe.matmul(bank[:, half], rd(gul[:, f]), rd(xTh[:, t]), start=False, stop=False)
                    ins = pe.matmul(bank[:, half], rd(guh[:, f]), rd(xTl[:, t]), start=False, stop=True)
                    if m == 0:
                        ins.then_inc(ready, 1)
                if c < FC1 - 1:
                    ins.then_inc(d_Us, 1)
                    pe.wait_ge(d_h, it * (2 * (FC1 - 1)) + (k * (FC1 - 1) + c + 1))
                    ins = pe.matmul(ps[c % 2][:], rd(ecol[:, c * P:(c + 1) * P]), rd(cT[:, t]), start=True, stop=True)
                ins.then_inc(ready, 1)

            def down2(it, k):
                pe.wait_ge(d_h1, it * (2 * FC1) + (k * FC1 + FC1 + 2))
                pe.wait_ge(d_h, it * (2 * (FC1 - 1)) + ((k + 1) * (FC1 - 1) + 2))
                for q in range(TT // P):
                    for c in range(FC1):
                        ins = pe.matmul(ps[2 + k][:, q * D:(q + 1) * D], hT1[k][:, c, q * P:(q + 1) * P], dn[:, c, :],
                                        start=(c == 0), stop=(c == FC1 - 1))
                ins.then_inc(d_Y, 1)

            with pe.Fori(0, T // TT // 2) as it:
                for c in range(FC1):
                    hidden_units(it, 0, c)
                for c in range(FC1):
                    hidden_units(it, 1, c)
                    if c == 1:
                        down2(it, 0)
                down2(it, 1)


def xn_gates(xn):
    return xn[0:2 * H0, :, :].rearrange("p t d -> p (t d)")


def kernel(**inputs):
    import numpy as np
    import concourse.bacc as bacc
    from concourse.bass_utils import run_bass_kernel_spmd as run

    nc = bacc.Bacc("TRN2", target_bir_lowering=False, num_devices=1)
    arrays = lay_out(np, {k: np.asarray(v) for k, v in inputs.items()})
    aps = {}
    for name, arr in arrays.items():
        aps[name] = nc.dram_tensor("in_" + name, arr.shape, mybir.dt.from_np(arr.dtype), kind="ExternalInput").ap()
    out = nc.dram_tensor("out", (P, NT * D), F32, kind="ExternalOutput").ap()
    scr_x = nc.dram_tensor("scratch_x", (NBLK * P, D), F32).ap()
    scr_y = nc.dram_tensor("scratch_y", (NBLK * P, D), F32).ap()
    build(nc, aps, scr_x, scr_y, out)
    r = run(nc, [{"in_" + n: t for n, t in arrays.items()}], core_ids=[0])
    got = r.results[0]["out"]
    return np.ascontiguousarray(got.reshape(P, NT, D).transpose(1, 0, 2).reshape(B, S, D))


def lay_out(np, v):
    f = np.float32

    def tiles(t):
        return t.reshape(NT, P, D).transpose(1, 0, 2)

    x, ctx = v["x"].reshape(T, D), v["ctx_1024"].reshape(T, D)
    va = np.ones((P, NT, H0, VW), f)
    va[..., :DH0] = tiles(ctx).reshape(P, NT, H0, DH0)

    r = np.arange(P)
    con = np.zeros((P, NCONST), f)
    c = {k: con[:, s:e] for k, (s, e) in CONST.items()}
    c["ident"][:] = np.eye(P)
    c["future"][:] = np.where(r[:, None] > r[None, :], NEG, 0.0)
    c["before"][:] = r[:, None] < r[None, :]
    c["of_seq"][:] = (r[:, None] % BH) // H0 == np.arange(B)
    c["of_head"][:] = r[:, None] % H0 == np.arange(H0)
    c["neg_of_head"][:] = -1.0 * (r[:, None] % H0 == np.arange(H0))
    c["quarter_of_head"][:] = 0.25 * (r[:, None] // DH0 == np.arange(H0))
    c["quarter_block"][:] = np.repeat(0.25 * (r[:, None] // DH0 == np.arange(H0)), VW, 1)
    c["block_start"][:] = P * np.arange(NT)
    c["not_first"][:] = np.arange(P) % NT != 0
    c["block_index"][:] = np.repeat(np.arange(NBLK), E0)
    c["rev8"][:] = E0 - np.arange(E0)
    c["rev16"][:] = E1 - np.arange(E1)
    c["query_lo"][:, 0] = -1.0 * (r % ST // DH1 == 2)
    c["key_lo"][:, 0] = -1.0 * (r % ST // DH1 == 1)
    for e in range(E1):
        for row in (e, E1 + e):
            c["expert_cols"][row, I1 * e:I1 * (e + 1)] = 1.0
    par = np.zeros((P, NPARAM), f)
    q = {k: par[:, s:e] for k, (s, e) in PARAM.items()}
    iw, fw = v["L0_xattn_igate_w"], v["L0_xattn_fgate_w"]
    for k, name in enumerate(("gwq", "gwk", "gwv")):
        q[name][:, :H0] = iw[:, k * D:(k + 1) * D].T
        q[name][:, H0:] = fw[:, k * D:(k + 1) * D].T
    q["gate_b"][:BH, 0] = np.tile(v["L0_xattn_igate_b"], B)
    q["gate_b"][:BH, 1] = np.tile(v["L0_xattn_fgate_b"], B)
    q["ln_scale"][:] = v["L0_xattn_ln_scale"]
    q["gates"][:, 0], q["gates"][:, 1] = v["g_xattn"][0], v["g_ffn"][0]
    q["gates"][:, 2], q["gates"][:, 3] = v["g_xattn"][1], v["g_ffn"][1]
    q["router0"][:] = v["L0_ffn_gate_w"]
    q["router1"][:] = v["L1_ffn_router_weight"].T
    q["e_bias"][:] = v["L1_ffn_e_bias"]
    wqs, wks = np.zeros((P, HG, HJ, ST), f), np.zeros((P, HG, HJ, ST), f)
    for w, wt, bias in ((wqs, "L1_xattn_Wq", "bq"), (wks, "L1_xattn_Wk", "bk")):
        b4 = v["L1_xattn_" + bias].reshape(HG, HJ, DH1)
        for k in range(3):
            at = slice(k * DH1, (k + 1) * DH1)
            w[:, :, :, at] = v[wt].T.reshape(P, HG, HJ, DH1)
            q[bias].reshape(HJ, ST, HG)[:, at, :] = b4.transpose(1, 2, 0)
    for j in range(HJ):
        q["bk"][j * ST + SM:j * ST + SM + 2] = 1.0
    q["bv"][:] = v["L1_xattn_bv"]
    q["wv"][:] = v["L1_xattn_Wv"].T
    q["wo"][:] = v["L1_xattn_Wo"].T
    q["be"][:] = v["L1_xattn_be"].T
    q["bo"][:] = v["L1_xattn_bo"]
    gu = np.zeros((P, 2, FC1 * P), f)
    for m, (routed, shared) in enumerate((("L1_ffn_gate_w", "L1_ffn_sh_gate_w"), ("L1_ffn_up_w", "L1_ffn_sh_up_w"))):
        gu[:, m, :E1 * I1] = v[routed].transpose(2, 0, 1).reshape(P, E1 * I1)
        gu[:, m, E1 * I1:] = v[shared].T
    down = np.zeros((P, FC1, D), f)
    down[:, :FC1 - 1] = v["L1_ffn_down_w"].transpose(0, 2, 1).reshape(FC1 - 1, P, D).transpose(1, 0, 2)
    down[:, FC1 - 1] = v["L1_ffn_sh_down_w"].T
    w13 = np.zeros((P, 2 * E0 * F0), f)
    w13[:, :E0 * F0] = v["L0_ffn_w1"].transpose(1, 0, 2).reshape(P, E0 * F0)
    w13[:, E0 * F0:2 * E0 * F0] = v["L0_ffn_w3"].transpose(1, 0, 2).reshape(P, E0 * F0)
    arrays = {
        "x_nat": tiles(x).reshape(P, NT * D), "ctxT": ctx.T, "vaug": va.reshape(P, NT * H0 * VW),
        "const": con, "param": par, "w13": w13,
        "wqs": wqs.reshape(P, HG * P), "wks": wks.reshape(P, HG * P),
        "we": v["L1_xattn_We"].transpose(1, 0, 2).reshape(P, EO * D),
        "gu": gu.reshape(P, 2 * FC1 * P), "down": down.reshape(P, FC1 * D),
        "w2": v["L0_ffn_w2"].reshape(E0, FC0, P, D).transpose(2, 0, 1, 3).reshape(P, E0 * F0),
    }
    return {k: np.ascontiguousarray(t) for k, t in arrays.items()}
```

```python
from contextlib import ExitStack

import concourse.bass as bass
from concourse import mybir

P = 128
B, S, D = 8, 256, 128
T = B * S
NT = T // P
CH = S // P
H0, DH0 = 8, 16
VW = DH0 + 1
BH = B * H0
E0, F0 = 8, 512
FC0 = F0 // P
NBLK = (2 * T + E0 * (P - 1)) // P
NBLK += NBLK % 2
H1, DH1 = 16, 8
HG, HJ = 4, 4
ST = P // HJ
NU = 2 * CH * HG
SM = 3 * DH1
EO = 8
E1, I1, K1 = 16, 64, 4
SHARE1 = 2.5
NG1 = 4
FC1 = E1 * I1 // P + 1
TT = 512
LN_EPS = 1e-5
NORM_EPS = 1e-6
NEG = -1.0e30
LOWEST = -3.0e38

ALU = mybir.AluOpType
ACT = mybir.ActivationFunctionType
AX = mybir.AxisListType
F32 = mybir.dt.float32
F32R = mybir.dt.float32r
BF16 = mybir.dt.bfloat16
I32 = mybir.dt.int32
U32 = mybir.dt.uint32


def layout(widths):
    at, out = 0, {}
    for name, w in widths:
        out[name] = (at, at + w)
        at += w
    return out, at


CONST, NCONST = layout([
    ("ident", P), ("future", P), ("before", P), ("of_seq", B), ("neg_of_head", H0),
    ("of_head", H0), ("quarter_of_head", H0), ("quarter_block", H0 * VW), ("block_start", NT),
    ("not_first", P), ("block_index", NBLK * E0), ("rev8", E0), ("rev16", E1),
    ("query_lo", 1), ("key_lo", 1), ("expert_cols", (FC1 - 1) * P),
])
PARAM, NPARAM = layout([
    ("gwq", 2 * H0), ("gwk", 2 * H0), ("gwv", 2 * H0), ("gate_b", 2), ("ln_scale", D), ("gates", 4),
    ("router0", E0), ("router1", E1), ("e_bias", E1), ("bq", HG), ("bk", HG), ("bv", D),
    ("wv", D), ("wo", D), ("be", EO), ("bo", D),
])


def rd(ap):
    return ap.bitcast(F32R)


class Chain:

    def __init__(self, eng, sem):
        self.eng, self.sem, self.base, self.n, self.turn, self.per = eng, sem, 0, 0, None, 0

    def enter(self, turn, per):
        self.base, self.n, self.turn, self.per = self.base + self.n, 0, turn, per

    def leave(self, turns):
        assert self.n == self.per, (self.n, self.per)
        self.base, self.n, self.turn = self.base + turns * self.per, 0, None

    def value(self):
        return self.base + self.n if self.turn is None else self.turn * self.per + (self.base + self.n)

    def link(self, ins):
        ins.then_inc(self.sem, 1)
        self.n += 1
        self.eng.wait_ge(self.sem, self.value())


def ge(eng, sem, value):
    if not (isinstance(value, int) and value <= 0):
        eng.wait_ge(sem, value)


def pipelined(eng, n, stages, extra=None, peel=0):
    least, most = min(lag for _, lag in stages), max(lag for _, lag in stages)
    first = most + peel

    def turn(k, parity):
        for stage, lag in stages:
            if not isinstance(k, int) or 0 <= k - lag < n + (stage is extra):
                stage(k - lag, (parity - lag) % 2)

    passes = (n + least - first) // 2
    for k in range(least, first):
        turn(k, k % 2)
    with eng.Fori(0, passes) as it:
        for i in range(2):
            turn(it * 2 + (first + i), (first + i) % 2)
    for k in range(first + 2 * passes, n + most):
        turn(k, k % 2)


def turns(eng, n, ahead, behind, peel, turn):
    first = behind + peel
    passes = (n - ahead - first) // 2
    for k in range(-ahead, first):
        turn(k, k % 2)
    with eng.Fori(0, passes) as it:
        for i in range(2):
            turn(it * 2 + (first + i), (first + i) % 2)
    for k in range(first + 2 * passes, n + behind):
        turn(k, k % 2)


def among(b, n):
    return not isinstance(b, int) or 0 <= b < n


def loads(b, i, units):
    return units * (b // 2 + 1) if isinstance(b, int) else (b - i) * (units // 2) + units


def build(nc, a, scr_x, scr_y, out, stage=9):
    es = ExitStack()
    with es:
        def sb(name, shape, dt=F32, stack=es):
            return stack.enter_context(nc.sbuf_tensor(name, shape, dt))

        def sem(name):
            return es.enter_context(nc.semaphore(name))

        ps = [es.enter_context(nc.psum_tensor(f"bank{i}", [P, 512], F32)) for i in range(4)]
        pw = [es.enter_context(nc.psum_tensor(f"wide{i}", [P, 1024], F32)) for i in range(2)]

        con = sb("con", [P, NCONST])
        par = sb("par", [P, NPARAM])
        x = sb("x", [P, NT, D])
        xn = sb("xn", [P, NT, D])
        xT = sb("xT", [P, T])
        ctxT = sb("ctxT", [P, T])
        st = sb("st", [P, NT, 6])
        lnw = sb("lnw", [P, 8, NT])
        tg = sb("tg", [P, 4])
        ctS = [sb(f"ctS{i}", [P, S]) for i in range(2)]
        before_bf = sb("before_bf", [P, P], BF16)
        ones_bf = sb("ones_bf", [P, P], BF16)

        def C(name):
            return con[:, CONST[name][0]:CONST[name][1]]

        def A(name):
            return par[:, PARAM[name][0]:PARAM[name][1]]

        ffn = ExitStack()
        wh = sb("w13h", [P, 2 * E0 * F0], F32, ffn)
        wl = sb("w13l", [P, 2 * E0 * F0], F32, ffn)

        ml = ExitStack()
        wst = [sb(f"wst{i}", [P, F0], F32, ml) for i in range(2)]
        zero = sb("zero", [P, P], F32, ml)
        vaug = sb("vaug", [P, NT, H0 * VW], F32, ml)
        num = sb("num", [P, NT, H0 * VW], F32, ml)
        gwc = sb("gwc", [P, 2 * H0], F32, ml)
        lnsg = sb("lnsg", [P, D], F32, ml)
        ident_bf = sb("ident_bf", [P, P], BF16, ml)
        future_bf = sb("future_bf", [P, 4, P], BF16, ml)
        g64 = sb("g64", [BH, 10, S], F32, ml)
        negM = sb("negM", [BH, 2], F32, ml)
        t64 = sb("t64", [BH, 4 * P], F32, ml)
        wT = sb("wT", [P, 4, BH], F32, ml)
        ahl = sb("ahl", [P, 3 * P], F32, ml)
        mhl = sb("mhl", [P, S], F32, ml)
        Rm = sb("Rm", [P, H0, S], F32, ml)
        dlt = sb("dlt", [P, H0, P], F32, ml)
        LS = [sb(f"LS{i}", [P, 3 * P], F32, ml) for i in range(2)]
        Qm = [sb(f"Qm{i}", [P, H0, S], F32, ml) for i in range(2)]
        qS = [sb(f"qS{i}", [P, P], F32, ml) for i in range(2)]
        Ks = [sb(f"Ks{i}", [P, P], F32, ml) for i in range(2)]
        stm = sb("stm", [P, H0 * VW], F32, ml)
        tmp = sb("tmp", [P, H0 * VW], F32, ml)
        Dm = [sb(f"Dm{i}", [P, 1024], F32, ml) for i in range(2)]
        Cm = [sb(f"Cm{i}", [P, 1024], F32, ml) for i in range(2)]
        den = sb("den", [P, NT * H0], F32, ml)
        ml.close()

        mo = ExitStack()
        w2 = sb("w2", [P, E0 * F0], F32, mo)
        rt = sb("rt", [P, 8, NT * E0], F32, mo)
        sm = sb("sm", [P, 8, NT], F32, mo)
        ex = sb("ex", [P, 4, E0], F32, mo)
        cmpb = sb("cmpb", [P, NBLK * E0], F32, mo)
        routed = sb("routed", [P, NT * E0], BF16, mo)
        slot = sb("slot", [P, 2, NT], U32, mo)
        share = sb("share", [P, 2, NT], F32, mo)
        bcol = sb("bcol", [1, 2, NBLK], F32, mo)
        boff = sb("boff", [1, NBLK], I32, mo)
        xg = [sb(f"xg{i}", [P, D], F32, mo) for i in range(2)]
        xgh = [sb(f"xgh{i}", [P, P], F32, mo) for i in range(2)]
        xgl = [sb(f"xgl{i}", [P, P], F32, mo) for i in range(2)]
        sg = [sb(f"sg{i}", [P, F0], F32, mo) for i in range(2)]
        hb = [sb(f"hb{i}", [P, F0], F32, mo) for i in range(2)]
        hT = [sb(f"hT{i}", [P, F0], F32, mo) for i in range(2)]
        yb = [sb(f"yb{i}", [P, D], F32, mo) for i in range(2)]
        gy = [sb(f"gy{i}", [P, NT, D], F32, mo) for i in range(2)]
        mo.close()
        ffn.close()

        at3 = ExitStack()
        wqs = sb("wqs", [P, HG * P], F32, at3)
        wks = sb("wks", [P, HG * P], F32, at3)
        we = sb("we", [P, EO, D], F32, at3)
        wem = sb("wem", [P, D], F32, at3)
        bem = sb("bem", [P, 1], F32, at3)
        bemb = sb("bemb", [P, P], F32, at3)
        wc = sb("wc", [P, D], F32, at3)
        cb = sb("cb", [P, D], F32, at3)
        bqs = sb("bqs", [P, HG], F32, at3)
        q32 = sb("q32", [P, HG, S], F32, at3)
        qhi = sb("qhi", [P, HG, S], F32, at3)
        k32 = sb("k32", [P, HG, S], F32, at3)
        khi = sb("khi", [P, HG, S], F32, at3)
        Qs = [sb(f"Qs{i}", [P, HG, S], F32, at3) for i in range(2)]
        Kst = [sb(f"Kst{i}", [P, HG, S], F32, at3) for i in range(2)]
        Kn = sb("Kn", [P, HG, S], F32, at3)
        Q2 = sb("Q2", [P, HG, S], F32, at3)
        Kd = [sb(f"Kd{i}", [P, HG, HJ, S], F32, at3) for i in range(2)]
        Qd = sb("Qd", [P, HG, HJ, S], F32, at3)
        vp = [sb(f"vp{i}", [P, CH, H1, ST], F32, at3) for i in range(2)]
        mx = sb("mx", [P, CH, H1], F32, at3)
        mp = sb("mp", [P, CH, HG, P], F32, at3)
        et3 = [[sb(f"et{i}{c}", [P, HJ, S], F32, at3) for c in range(CH)] for i in range(2)]
        o32 = sb("o32", [P, HG, S], F32, at3)
        rec = sb("rec", [P, CH, H1], F32, at3)
        on = sb("on", [P, CH, D], F32, at3)
        onT = sb("onT", [P, CH, P], F32, at3)
        at3.close()

        m2 = ExitStack()
        graw = sb("graw", [P, 2 * FC1 * P], F32, m2)
        guh = sb("guh", [P, 2 * FC1 * P], F32, m2)
        gul = sb("gul", [P, 2 * FC1 * P], F32, m2)
        dn = sb("dn", [P, FC1, D], F32, m2)
        xTh = sb("xTh", [P, T], F32, m2)
        xTl = sb("xTl", [P, T], F32, m2)
        cT = sb("cT", [P, T], F32, m2)
        ecol = sb("ecol", [P, (FC1 - 1) * P], F32, m2)
        r1 = sb("r1", [P, 6, NT * E1], F32, m2)
        r4 = sb("r4", [P, 12, NT * NG1], F32, m2)
        s4 = sb("s4", [P, 6, NT], F32, m2)
        chl = sb("chl", [P, NT, 2 * E1], F32, m2)
        sg1 = [sb(f"sgb{i}", [P, TT], F32, m2) for i in range(2)]
        h1 = [sb(f"h1{i}", [P, TT], F32, m2) for i in range(2)]
        hT1 = [sb(f"hTb{i}", [P, FC1, TT], F32, m2) for i in range(2)]
        m2.close()

        s_con = sem("constants_loaded")
        s_par = sem("parameters_loaded")
        s_x = sem("x_loaded")
        s_ctx = sem("ctx_loaded")
        s_va = sem("values_loaded")
        s_v = sem("dve_step")
        s_a = sem("act_step")
        s_p = sem("pool_step")
        s_var = sem("ln_variance_ready")
        s_pow = sem("ln_power_ready")
        s_xn = sem("xn_ready")
        s_tr = sem("x_transposed_in_psum")
        s_xT = sem("xT_ready")
        s_gps = sem("gates_in_psum")
        s_gT = sem("gates_copied")
        s_g64 = sem("gates_by_head_row")
        s_z = sem("forget_gate_ready")
        s_sp = sem("softplus_ready")
        s_aM = sem("stabilizers_ready")
        s_t64 = sem("decays_ready")
        s_wps = sem("decays_in_psum")
        s_wT = sem("decay_columns_ready")
        s_bc = sem("mlstm_constants_ready")
        s_free = sem("sequence_matmuls_done")
        s_ct = [sem(f"ctx_columns_{i}_loaded") for i in range(2)]
        s_ls = sem("exponent_operand_ready")
        s_qm = sem("head_queries_ready")
        s_qS = sem("chunk_queries_ready")
        s_E = sem("exponent_in_psum")
        s_D = sem("decay_matrix_ready")
        s_S = sem("scores_in_psum")
        s_C = sem("weighted_scores_ready")
        s_ks = sem("decayed_keys_ready")
        s_st = sem("state_in_psum")
        s_stm = sem("state_copied")
        s_I = sem("state_part_in_psum")
        s_It = sem("state_part_scaled")
        s_PV = sem("head_sums_in_psum")
        s_num = sem("head_sums_copied")
        s_w = [sem(f"weights_{i}_loaded") for i in range(2)]
        s_wh = sem("weights_hi_ready")
        s_wl = sem("weights_lo_ready")
        s_tg = sem("gates_tanh_ready")
        s_x1 = sem("x1_ready")
        s_zero = sem("zero_ready")
        s_clr = sem("scratch_cleared")
        s_out = sem("out_stored")
        s_w2 = sem("w2_loaded")
        s_lg = sem("router_logits_in_psum")
        s_lx = sem("router_logits_less_max")
        s_ex = sem("router_exponentials_ready")
        s_ro = sem("routed_ready")
        s_rk = sem("ranks_in_psum")
        s_sl = sem("slots_ready")
        s_be = sem("block_experts_ready")
        s_sc = sem("tokens_scattered")
        s_xg = [sem(f"block_tokens_{i}_loaded") for i in range(2)]
        s_T = sem("block_tokens_in_psum")
        s_xp = sem("block_tokens_split")
        s_G = sem("hidden_gate_in_psum")
        s_U = sem("hidden_up_in_psum")
        s_sg = sem("silu_ready")
        s_hb = sem("hidden_ready")
        s_H = sem("hidden_transposed_in_psum")
        s_hT = sem("hidden_transposed_copied")
        s_Y = sem("block_out_in_psum")
        s_yb = sem("block_out_copied")
        s_ys = [sem(f"block_out_{i}_stored") for i in range(2)]
        s_gy = [sem(f"tile_{t}_gathered") for t in range(NT)]
        s_x2 = sem("x2_ready")
        c_w = sem("attention_weights_loaded")
        c_wa = sem("mean_expert_ready")
        c_wp = sem("output_weights_in_psum")
        c_wc = sem("output_weights_ready")
        c_z = sem("attention_zeros_ready")
        c_ct = [sem(f"attention_ctx_{i}_loaded") for i in range(2)]
        c_K = sem("keys_in_psum")
        c_k32 = sem("keys_copied")
        c_khi = sem("keys_rounded")
        c_qhi = sem("queries_rounded")
        c_rec = sem("row_sums_inverted")
        c_ks = sem("key_stacks_ready")
        c_kd = [sem(f"key_blocks_{i}_placed") for i in range(2)]
        c_kst = [sem(f"key_stacks_{i}_copied") for i in range(2)]
        c_V = sem("values_in_psum")
        c_vp = sem("values_ready")
        c_Q = sem("queries_in_psum")
        c_q32 = sem("queries_copied")
        c_qs = sem("query_stacks_ready")
        c_P1 = sem("scores_for_max_in_psum")
        c_R = sem("max_taken")
        c_mp = sem("max_parts_ready")
        c_MT = sem("max_rows_in_psum")
        c_q2 = sem("queries_with_max_ready")
        c_qd = sem("query_blocks_placed")
        c_P2 = sem("scores_less_max_in_psum")
        c_X = sem("exponentials_ready")
        c_PV = sem("attention_sums_in_psum")
        c_O = sem("attention_sums_copied")
        c_OT = sem("attention_sums_turned")
        c_on = sem("attention_normalized")
        c_nT = sem("attention_turned_in_psum")
        c_nc = sem("attention_turned_copied")
        c_Y = sem("attention_out_in_psum")
        s_x3 = sem("x3_ready")
        d_w = sem("mixture2_weights_loaded")
        d_wh = sem("mixture2_weights_hi_ready")
        d_wl = sem("mixture2_weights_lo_ready")
        d_c = sem("mixture2_constants_ready")
        d_xT = sem("x3_parts_ready")
        d_lg = sem("router2_logits_in_psum")
        d_sg = sem("router2_exponentials_ready")
        d_cm = sem("combine_weights_ready")
        d_cT = sem("combine_rows_in_psum")
        d_cc = sem("combine_rows_ready")
        d_G = sem("mixture2_gate_in_psum")
        d_U = sem("mixture2_up_in_psum")
        d_Us = sem("mixture2_up_matmuls_done")
        d_sl = sem("mixture2_silu_ready")
        d_h1 = sem("mixture2_hidden_ready")
        d_h = sem("mixture2_weighted_hidden_ready")
        d_Y = sem("mixture2_out_in_psum")
        d_x4 = sem("x4_ready")

        block = es.enter_context(nc.Block())

        @block.sync
        def _(sp):
            sp.dma_start(x[:], a["x_nat"].rearrange("p (t d) -> p t d", d=D)).then_inc(s_x, 16)
            sp.dma_start(con[:], a["const"]).then_inc(s_con, 16)
            sp.dma_start(par[:], a["param"]).then_inc(s_par, 16)
            sp.dma_start(ctxT[:], a["ctxT"]).then_inc(s_ctx, 16)
            sp.dma_start(vaug[:], a["vaug"].rearrange("p (t d) -> p t d", d=H0 * VW)).then_inc(s_va, 16)
            sp.wait_ge(s_zero, 1)
            sp.dma_start(scr_x.rearrange("(r p) d -> p r d", p=P),
                         zero[:].unsqueeze(1).broadcast_to([P, NBLK, D])).then_inc(s_clr, 16)
            for b in range(B):
                sp.wait_ge(s_gT, b // 2 + 1)
                for k in range(2):
                    sp.dma_start(g64[b * H0:(b + 1) * H0, k, :],
                                 xn_gates(xn)[k * H0:(k + 1) * H0, b * S:(b + 1) * S]).then_inc(s_g64, 16)
            with sp.Fori(0, B // 2) as it:
                for i in range(2):
                    sp.wait_ge(s_free, it * 2 + (i + 1))
                    sp.dma_start(ctS[i][:], a["ctxT"][:, bass.ds((it * 2 + i) * S, S)]).then_inc(s_ct[i], 16)
                    for u in (2 * i, 2 * i + 1):
                        sp.wait_ge(s_wl, it * 4 + (u + 1))
                        sp.dma_start(wst[u % 2][:], a["w13"][:, bass.ds((it * 4 + u) * F0, F0)])\
                            .then_inc(s_w[u % 2], 16)
            if stage == 1:
                sp.wait_ge(s_x1, 1)
                sp.dma_start(out.rearrange("p (t d) -> p t d", d=D), x[:]).then_inc(s_out, 16)
                sp.wait_ge(s_out, 16)
                sp.wait_ge(s_clr, 16)
                return
            sp.wait_ge(s_x1, 1)
            sp.wait_ge(s_wl, 2 + 2 * E0)
            sp.wait_ge(s_clr, 16)
            sp.dma_start(w2[:], a["w2"]).then_inc(s_w2, 16)
            sp.wait_ge(s_sc, 16 * 2 * NT)

            def load_block(j, i):
                ge(sp, s_T, j - 1)
                sp.dma_start(xg[i][:], scr_x[bass.ds(j * P, P), :]).then_inc(s_xg[i], 16)

            pipelined(sp, NBLK, [(load_block, 0)], peel=2)
            sp.wait_ge(s_x2, NT)
            if stage == 2:
                sp.dma_start(out.rearrange("p (t d) -> p t d", d=D), x[:]).then_inc(s_out, 16)
                sp.wait_ge(s_out, 16)
                return

            for dst, name in ((wqs, "wqs"), (wks, "wks")):
                sp.dma_start(dst[:], a[name]).then_inc(c_w, 16)
            sp.dma_start(we[:], a["we"].rearrange("p (e d) -> p e d", d=D)).then_inc(c_w, 16)
            sp.wait_ge(c_z, 5)

            def place(k, i):
                if among(k + 1, B):
                    ge(sp, c_V, k)
                    sp.dma_start(ctS[1 - i][:], a["ctxT"][:, bass.ds((k + 1) * S, S)]).then_inc(c_ct[1 - i], 16)
                    sp.wait_ge(c_ks, k + 2)
                    for j in range(HJ):
                        rows = slice(j * ST, (j + 1) * ST)
                        sp.dma_start(Kd[1 - i][rows, :, j, :], Kn[rows, :, :]).then_inc(c_kd[1 - i], 16)
                ge(sp, c_P2, k * NU)
                if among(k + 1, B):
                    sp.dma_start(Kst[1 - i][:], Kn[:]).then_inc(c_kst[1 - i], 16)
                if among(k, B):
                    sp.wait_ge(c_q2, k * 2 + 2)
                    for j in range(HJ):
                        rows = slice(j * ST, (j + 1) * ST)
                        sp.dma_start(Qd[rows, :, j, :], Q2[rows, :, :]).then_inc(c_qd, 16)

            turns(sp, B, 1, 0, 2, place)
            sp.wait_ge(s_x3, B)
            if stage == 3:
                sp.dma_start(out.rearrange("p (t d) -> p t d", d=D), x[:]).then_inc(s_out, 16)
                sp.wait_ge(s_out, 16)
                return

            sp.dma_start(graw[:], a["gu"]).then_inc(d_w, 16)
            sp.dma_start(dn[:], a["down"].rearrange("p (c d) -> p c d", d=D)).then_inc(d_w, 16)
            o4 = out.rearrange("p (t d) -> p t d", d=D)
            for t in range(T // TT):
                sp.wait_ge(d_x4, t + 1)
                k = TT // P
                sp.dma_start(o4[:, t * k:(t + 1) * k, :], x[:, t * k:(t + 1) * k, :]).then_inc(s_out, 16)
            sp.wait_ge(s_out, 16 * (T // TT))

        def ln_stats(dve, v, src, k, eps=LN_EPS):
            with dve.Fori(0, NT) as t:
                dve.bn_stats(st[:, t, :], src[:, t, :]).then_inc(v.sem, 1)
            v.n += NT
            dve.wait_ge(v.sem, v.value())
            v.link(dve.tensor_tensor(lnw[:, 0, :], st[:, :, 1], st[:, :, 4], ALU.add))
            v.link(dve.tensor_scalar(lnw[:, 0, :], lnw[:, 0, :], 0.5, None, ALU.mult))
            v.link(dve.tensor_tensor(lnw[:, 1, :], st[:, :, 1], st[:, :, 4], ALU.subtract))
            v.link(dve.tensor_tensor(lnw[:, 1, :], lnw[:, 1, :], lnw[:, 1, :], ALU.mult))
            v.link(dve.tensor_tensor(lnw[:, 2, :], st[:, :, 2], st[:, :, 5], ALU.add))
            v.link(dve.tensor_scalar(lnw[:, 2, :], lnw[:, 2, :], 1.0 / D, eps, ALU.mult, ALU.add))
            dve.scalar_tensor_tensor(out=lnw[:, 3, :], in0=lnw[:, 1, :], scalar=0.25, in1=lnw[:, 2, :],
                                     op0=ALU.mult, op1=ALU.add).then_inc(s_var, 1)
            dve.wait_ge(s_var, k)
            dve.wait_ge(s_pow, k)
            v.link(dve.tensor_tensor(lnw[:, 5, :], lnw[:, 4, :], lnw[:, 4, :], ALU.mult))
            v.link(dve.tensor_tensor(lnw[:, 5, :], lnw[:, 5, :], lnw[:, 3, :], ALU.mult))
            v.link(dve.tensor_scalar(lnw[:, 5, :], lnw[:, 5, :], -0.5, 1.5, ALU.mult, ALU.add))
            v.link(dve.tensor_tensor(lnw[:, 6, :], lnw[:, 5, :], lnw[:, 4, :], ALU.mult))

        def ln_apply(dve, v, dst, src):
            v.link(dve.tensor_tensor(dst, src, lnw[:, 0, :].unsqueeze(2).broadcast_to([P, NT, D]), ALU.subtract))
            return dve.tensor_tensor(dst, dst, lnw[:, 6, :].unsqueeze(2).broadcast_to([P, NT, D]), ALU.mult)

        def ln_power(act, ch, k):
            act.wait_ge(s_var, k)
            ch.link(act.activation(lnw[:, 4, :], lnw[:, 3, :], ACT.Ln))
            act.activation(lnw[:, 4, :], lnw[:, 4, :], ACT.Exp, scale=-0.5).then_inc(s_pow, 1)

        def pick(dve, v, val, eq, sel, top, first, rev, m, n):
            wide = lambda t: t.unsqueeze(2).broadcast_to([P, m, n])
            v.link(dve.tensor_reduce(top, val, AX.X, ALU.max))
            v.link(dve.tensor_tensor(eq, val, wide(top), ALU.is_equal))
            v.link(dve.tensor_tensor(eq, eq, rev.unsqueeze(1).broadcast_to([P, m, n]), ALU.mult))
            v.link(dve.tensor_reduce(first, eq, AX.X, ALU.max))
            v.link(dve.tensor_tensor(sel, eq, wide(first), ALU.is_equal))
            v.link(dve.scalar_tensor_tensor(out=val, in0=sel, scalar=NEG, in1=val, op0=ALU.mult, op1=ALU.add))

        @block.vector
        def _(dve):
            v = Chain(dve, s_v)
            dve.memset(zero[:], 0.0).then_inc(s_zero, 1)
            dve.wait_ge(s_x, 16)
            ln_stats(dve, v, x, 1)
            ln_apply(dve, v, xn[:], x[:]).then_inc(s_xn, 1)
            dve.wait_ge(s_con, 16)
            dve.wait_ge(s_par, 16)
            dve.tensor_copy(ident_bf[:], C("ident")).then_inc(s_bc, 1)
            dve.tensor_copy(future_bf[:], C("future").unsqueeze(1).broadcast_to([P, 4, P])).then_inc(s_bc, 1)
            dve.tensor_copy(rd(dlt[:]), C("of_head").unsqueeze(2).broadcast_to([P, H0, P])).then_inc(s_bc, 1)
            dve.tensor_copy(before_bf[:], C("before")).then_inc(s_bc, 1)
            dve.memset(ones_bf[:], 1.0).then_inc(s_bc, 1)
            dve.memset(ahl[:, 2 * P:], 1.0).then_inc(s_bc, 1)
            dve.tensor_tensor(gwc[:], A("gwk"), A("gwv"), ALU.add).then_inc(s_bc, 1)
            dve.wait_ge(s_tg, 1)
            dve.tensor_scalar(lnsg[:], A("ln_scale"), tg[:, 0:1], None, ALU.mult).then_inc(s_bc, 1)
            dve.wait_ge(s_bc, 8)
            for i in range(4):
                dve.wait_ge(s_tr, i + 1)
                dve.tensor_copy(xT[:, bass.ts(i, 512)], ps[i][:]).then_inc(s_xT, 1)

            IG, FG, AZ, EZ, L, LF, CS, AA, MM, ONE = range(10)
            g = lambda i: g64[:, i, :]
            dve.memset(g(ONE), 1.0).then_inc(s_v, 1)
            v.n += 1
            dve.wait_ge(s_g64, 16 * 2 * B)
            dve.tensor_scalar(g(FG), g(FG), par[0:BH, PARAM["gate_b"][0] + 1:PARAM["gate_b"][1]], None,
                              ALU.add).then_inc(s_z, 1)
            dve.wait_ge(s_z, 1)
            v.link(dve.tensor_scalar(g(LF), g(FG), 0.0, None, ALU.min))
            dve.wait_ge(s_sp, 1)
            v.link(dve.tensor_tensor(g(LF), g(LF), g(L), ALU.subtract))
            v.link(dve.tensor_tensor_scan(g(CS), g(ONE), g(LF), 0.0, ALU.mult, ALU.add))
            v.link(dve.scalar_tensor_tensor(out=g(AA), in0=g(IG), scalar=par[0:BH, PARAM["gate_b"][0]:PARAM["gate_b"][0] + 1],
                                            in1=g(CS), op0=ALU.add, op1=ALU.subtract))
            v.link(dve.tensor_tensor_scan(g(MM), g(ONE), g(AA), LOWEST, ALU.mult, ALU.max))
            v.link(dve.tensor_scalar(negM[:, 0:1], g64[:, MM, P - 1:P], -1.0, None, ALU.mult))
            dve.tensor_tensor(g(CS), g(CS), g(MM), ALU.add).then_inc(s_aM, 1)
            v.link(dve.tensor_copy(rd(ahl[0:BH, 0:S]), g(AA)))
            v.link(dve.tensor_copy(rd(mhl[0:BH, :]), g(MM)))
            v.link(dve.tensor_tensor(rd(ahl[BH:P, 0:S]), g(AA), ahl[0:BH, 0:S], ALU.subtract))
            v.link(dve.tensor_tensor(rd(mhl[BH:P, :]), g(MM), mhl[0:BH, :], ALU.subtract))
            dve.tensor_tensor(rd(Rm[:]), mhl[:].unsqueeze(1).broadcast_to([P, H0, S]),
                              C("neg_of_head").unsqueeze(2).broadcast_to([P, H0, S]), ALU.mult).then_inc(s_bc, 1)
            dve.wait_ge(s_wps, 4)
            dve.tensor_copy(wT[:], ps[0][:, 0:4 * BH].rearrange("p (c r) -> p c r", r=BH)).then_inc(s_wT, 1)
            dve.wait_ge(s_wT, 1)
            dve.wait_ge(s_va, 16)

            vh = lambda t: t.rearrange("p (h w) -> p h w", w=VW)

            def prepare(it, i):
                b = it * 2 + i
                dve.wait_ge(s_free, it * 2 + (i + 1))
                dve.tensor_scalar(rd(LS[i][:]), ahl[:], con[:, bass.ds(CONST["of_seq"][0] + b, 1)], None,
                                  ALU.mult).then_inc(s_ls, 1)
                dve.tensor_tensor(Ks[i][:].rearrange("p (h d) -> p h d", d=DH0),
                                  vh(vaug[:, b * CH, :])[:, :, 0:DH0],
                                  wT[:, 0, bass.ds(b * H0, H0)].unsqueeze(2).broadcast_to([P, H0, DH0]),
                                  ALU.mult).then_inc(s_ks, 1)

            with dve.Fori(0, B // 2) as it:
                for i in range(2):
                    prepare(it, i)
                for u in range(4):
                    i, c = u // 2, u % 2
                    b = it * 2 + i
                    dve.wait_ge(s_S, it * 4 + (u + 1))
                    dve.wait_ge(s_D, it * 4 + (u + 1))
                    dve.wait_ge(s_PV, it * 4 + (u + 1))
                    dve.tensor_tensor(Cm[u % 2][:], pw[1][:], Dm[u % 2][:], ALU.mult).then_inc(s_C, 1)
                    if c == 0:
                        dve.wait_ge(s_st, it * 2 + (i + 1))
                        dve.tensor_tensor(stm[:], ps[1][:, 0:H0 * VW], C("quarter_block"), ALU.mult).then_inc(s_stm, 1)
                        dve.wait_ge(s_PV, it * 4 + (u + 3))
                        dve.tensor_copy(num[:, b * CH, :], ps[0][:, 0:H0 * VW]).then_inc(s_num, 1)
                    else:
                        dve.wait_ge(s_I, it * 2 + (i + 1))
                        dve.tensor_tensor(vh(tmp[:]), vh(ps[1][:, 256:256 + H0 * VW]),
                                          wT[:, 1, bass.ds(b * H0, H0)].unsqueeze(2).broadcast_to([P, H0, VW]),
                                          ALU.mult).then_inc(s_It, 1)
                        dve.wait_ge(s_It, it * 2 + (i + 1))
                        dve.wait_ge(s_PV, it * 4 + (u + 3))
                        dve.tensor_tensor(num[:, b * CH + 1, :], tmp[:], ps[0][:, 0:H0 * VW], ALU.add).then_inc(s_num, 1)
            dve.wait_ge(s_num, NT)

            n4 = num[:].rearrange("p t (h w) -> p (t h) w", w=VW)
            th = lambda t: t.rearrange("p (b c h) -> p b c h", c=CH, h=H0)
            v.link(dve.tensor_scalar(den[:], n4[:, :, DH0], -1.0, None, ALU.mult))
            v.link(dve.tensor_tensor(den[:], den[:], n4[:, :, DH0], ALU.max))
            v.link(dve.tensor_tensor(th(den[:]), th(den[:]), wT[:, 2:4, :].rearrange("p c (b h) -> p b c h", h=H0), ALU.max))
            v.link(dve.tensor_scalar(den[:], den[:], NORM_EPS, None, ALU.add))
            v.link(dve.reciprocal(den[:], den[:]))
            v.link(dve.tensor_tensor(xn[:].rearrange("p t (h d) -> p (t h) d", d=DH0), n4[:, :, 0:DH0],
                                     den[:].unsqueeze(2).broadcast_to([P, NT * H0, DH0]), ALU.mult))
            ln_stats(dve, v, xn, 2)
            v.link(ln_apply(dve, v, xn[:], xn[:]))
            v.link(dve.tensor_tensor(xn[:], xn[:], lnsg[:].unsqueeze(1).broadcast_to([P, NT, D]), ALU.mult))
            dve.tensor_tensor(x[:], x[:], xn[:], ALU.add).then_inc(s_x1, 1)
            dve.wait_ge(s_x1, 1)
            if stage == 1:
                return

            dve.wait_ge(s_wl, 2 + 2 * E0)
            dve.wait_ge(s_clr, 16)
            ln_stats(dve, v, x, 3)
            ln_apply(dve, v, xn[:], x[:]).then_inc(s_xn, 1)
            te = lambda t: t.rearrange("p (t e) -> p t e", e=E0)
            tile1 = lambda t: t.unsqueeze(2).broadcast_to([P, NT, E0])
            pr, eq, s1, s2, tc, inc, pos, one = (rt[:, i, :] for i in range(8))
            dve.memset(one, 1.0).then_inc(s_v, 1)
            v.n += 1
            dve.wait_ge(s_lg, 1)
            lg = pw[0][:, 0:NT * E0]
            v.link(dve.tensor_reduce(sm[:, 0, :], te(lg), AX.X, ALU.max))
            dve.tensor_tensor(te(pr), te(lg), tile1(sm[:, 0, :]), ALU.subtract).then_inc(s_lx, 1)
            dve.wait_ge(s_ex, 1)
            v.link(dve.tensor_reduce(sm[:, 0, :], te(eq), AX.X, ALU.add))
            v.link(dve.reciprocal(sm[:, 1, :], sm[:, 0, :]))
            v.link(dve.tensor_tensor(te(pr), te(eq), tile1(sm[:, 1, :]), ALU.mult))
            pick(dve, v, te(pr), te(eq), te(s1), sm[:, 2, :], sm[:, 4, :], C("rev8"), NT, E0)
            pick(dve, v, te(pr), te(eq), te(s2), sm[:, 3, :], sm[:, 4, :], C("rev8"), NT, E0)
            dve.tensor_tensor(routed[:], s1, s2, ALU.add).then_inc(s_ro, 1)
            v.link(dve.tensor_tensor(sm[:, 4, :], sm[:, 2, :], sm[:, 3, :], ALU.add))
            v.link(dve.reciprocal(sm[:, 5, :], sm[:, 4, :]))
            v.link(dve.tensor_scalar(sm[:, 5, :], sm[:, 5, :], tg[:, 1:2], None, ALU.mult))
            for k in range(2):
                v.link(dve.tensor_tensor(share[:, k, :], sm[:, 2 + k, :], sm[:, 5, :], ALU.mult))
            et = lambda t: t.rearrange("p (e t) -> p e t", t=NT)
            dve.wait_ge(s_rk, 1)
            v.link(dve.tensor_copy(et(tc), ps[0][:, P:2 * P].rearrange("p (t e) -> p e t", e=E0)))
            v.link(dve.tensor_tensor_scan(inc, C("not_first"), tc, 0.0, ALU.mult, ALU.add))
            v.link(dve.tensor_tensor(et(pos), et(inc)[:, :, NT - 1].unsqueeze(2).broadcast_to([P, E0, NT]),
                                     C("block_start").unsqueeze(1).broadcast_to([P, E0, NT]), ALU.is_gt))
            v.link(dve.tensor_reduce(ex[:, 0, :], et(pos), AX.X, ALU.add))
            v.link(dve.tensor_tensor_scan(ex[:, 1, :], one[:, 0:E0], ex[:, 0, :], 0.0, ALU.mult, ALU.add))
            v.link(dve.tensor_tensor(ex[:, 2, :], ex[:, 1, :], ex[:, 0, :], ALU.subtract))
            v.link(dve.tensor_scalar(ex[:, 2, :], ex[:, 2, :], float(P), None, ALU.mult))
            v.link(dve.tensor_tensor(inc, inc, tc, ALU.subtract))
            v.link(dve.tensor_tensor(et(inc), et(inc), ex[:, 2, :].unsqueeze(2).broadcast_to([P, E0, NT]), ALU.add))
            v.link(dve.tensor_tensor(te(pos), te(ps[0][:, 0:P]), inc.rearrange("p (e t) -> p t e", t=NT), ALU.add))
            for k, s in enumerate((s1, s2)):
                v.link(dve.tensor_tensor(eq, s, pos, ALU.mult))
                v.link(dve.tensor_reduce(sm[:, 6 + k, :], te(eq), AX.X, ALU.add))
                dve.tensor_copy(slot[:, k, :], sm[:, 6 + k, :]).then_inc(s_sl, 1)
            b3 = lambda t: t.rearrange("p (j e) -> p j e", e=E0)
            v.link(dve.tensor_tensor(b3(cmpb[0:1, :]), b3(C("block_index")[0:1, :]),
                                     ex[0:1, 1, :].unsqueeze(1).broadcast_to([1, NBLK, E0]), ALU.is_ge))
            v.link(dve.tensor_reduce(bcol[:, 0, :], b3(cmpb[0:1, :]), AX.X, ALU.add))
            v.link(dve.tensor_scalar(bcol[:, 1, :], bcol[:, 0, :], float(E0 - 1), float(F0), ALU.min, ALU.mult))
            dve.tensor_copy(boff[:], bcol[:, 1, :]).then_inc(s_be, 1)

            def split_tokens(j, i):
                dve.wait_ge(s_T, j + 1)
                ge(dve, s_U, j - 1)
                dve.tensor_copy(rd(xgh[i][:]), ps[0][:, 0:P]).then_inc(s_xp, 1)
                dve.wait_ge(s_xp, j * 2 + 1)
                dve.tensor_tensor(rd(xgl[i][:]), ps[0][:, 0:P], xgh[i][:], ALU.subtract).then_inc(s_xp, 1)

            def hidden(j, i):
                dve.wait_ge(s_U, j + 1)
                dve.wait_ge(s_sg, j + 1)
                ge(dve, s_H, j - 1)
                dve.tensor_tensor(hb[i][:], sg[i][:], pw[1][:, i * F0:(i + 1) * F0], ALU.mult).then_inc(s_hb, 1)

            def block_out(j, i):
                dve.wait_ge(s_Y, j + 1)
                if isinstance(j, int):
                    ge(dve, s_ys[i], 16 * (j // 2))
                else:
                    dve.wait_ge(s_ys[i], (j - i) * 8)
                dve.tensor_copy(yb[i][:], ps[3][:, 0:P]).then_inc(s_yb, 1)

            pipelined(dve, NBLK, [(split_tokens, -1), (hidden, 0), (block_out, 2)], peel=2)
            for t in range(NT):
                dve.wait_ge(s_gy[t], 32)
                dve.scalar_tensor_tensor(out=xn[:, t, :], in0=gy[0][:, t, :], scalar=share[:, 0, t:t + 1],
                                         in1=x[:, t, :], op0=ALU.mult, op1=ALU.add).then_inc(s_v, 1)
                v.n += 1
                dve.wait_ge(s_v, v.value())
                dve.scalar_tensor_tensor(out=x[:, t, :], in0=gy[1][:, t, :], scalar=share[:, 1, t:t + 1],
                                         in1=xn[:, t, :], op0=ALU.mult, op1=ALU.add).then_inc(s_x2, 1)
            dve.wait_ge(s_x2, NT)
            if stage == 2:
                return

            for i in range(2):
                dve.memset(Kd[i][:], 0.0).then_inc(c_z, 1)
                dve.memset(vp[i][:], 0.0).then_inc(c_z, 1)
            dve.memset(Qd[:], 0.0).then_inc(c_z, 1)
            dve.memset(mp[:], 0.0).then_inc(c_z, 1)
            dve.wait_ge(c_z, 6)
            for i in range(2):
                dve.memset(vp[i][:, :, :, DH1:DH1 + 1], 1.0).then_inc(c_z, 1)
            dve.wait_ge(c_z, 8)
            ln_stats(dve, v, x, 4)
            ln_apply(dve, v, xn[:], x[:]).then_inc(s_xn, 1)
            v.link(dve.tensor_scalar(bqs[:], A("bq"), float(DH1) ** -0.5, None, ALU.mult))
            dve.wait_ge(c_w, 48)
            v.link(dve.tensor_reduce(wem[:], we[:].rearrange("p e d -> p d e"), AX.X, ALU.add))
            v.link(dve.tensor_scalar(wem[:], wem[:], tg[:, 2:3], 1.0 / EO, ALU.mult, ALU.mult))
            v.link(dve.tensor_reduce(bem[:], A("be"), AX.X, ALU.add))
            v.link(dve.tensor_scalar(bem[:], bem[:], tg[:, 2:3], 1.0 / EO, ALU.mult, ALU.mult))
            dve.tensor_copy(bemb[:], bem[:, 0:1].broadcast_to([P, P])).then_inc(c_wa, 1)
            dve.wait_ge(c_wp, 1)
            dve.tensor_copy(wc[:], ps[0][:, 0:P]).then_inc(c_wc, 1)
            dve.scalar_tensor_tensor(out=cb[:], in0=A("bo"), scalar=tg[:, 2:3], in1=ps[0][:, P:2 * P],
                                     op0=ALU.mult, op1=ALU.add).then_inc(c_wc, 1)
            dve.wait_ge(c_wc, 2)
            dve.wait_ge(s_xn, 3)
            v.link(dve.tensor_tensor(x[:], x[:], cb[:].unsqueeze(1).broadcast_to([P, NT, D]), ALU.add))

            def take_max(b, n):
                c, g, half = n // 8, n // 2 % 4, n % 2
                dve.wait_ge(c_P1, b * NU + (n + 1))
                h = g * HJ + half * 2
                dve.tensor_reduce(mx[:, c, h:h + 2], pw[0][:, half * 512:(half + 1) * 512]
                                  .rearrange("p (j t) -> p j t", t=S), AX.X, ALU.max).then_inc(c_R, 1)

            def split_max(b):
                dve.wait_ge(c_R, b * NU + NU)
                ge(dve, c_MT, b)
                col = lambda k: mp[:].rearrange("p c g (j r) -> p c (g j) r", r=ST)[:, :, :, SM + k]
                dve.tensor_scalar(rd(col(0)), mx[:], -1.0, None, ALU.mult).then_inc(c_mp, 1)
                dve.wait_ge(c_mp, b * 2 + 1)
                dve.scalar_tensor_tensor(out=rd(col(1)), in0=mx[:], scalar=-1.0, in1=col(0),
                                         op0=ALU.mult, op1=ALU.subtract).then_inc(c_mp, 1)

            def add_values(b, i):
                dve.wait_ge(c_V, b + 1)
                ge(dve, c_PV, (b - 1) * HG)
                dve.tensor_tensor(vp[i][:, :, :, 0:DH1],
                                  ps[0][:, 0:CH * D].rearrange("p (c h d) -> p c h d", h=H1, d=DH1),
                                  A("bv").rearrange("p (h d) -> p h d", d=DH1).unsqueeze(1).broadcast_to([P, CH, H1, DH1]),
                                  ALU.add).then_inc(c_vp, 1)

            def add_max(b, i):
                dve.wait_ge(c_MT, b + 1)
                dve.wait_ge(c_qs, b + 1)
                ge(dve, c_qd, b * 64)
                for k in range(2):
                    dve.tensor_tensor(rd(Q2[:, 2 * k:2 * k + 2, :]), Qs[i][:, 2 * k:2 * k + 2, :],
                                      ps[k][:].rearrange("p (g s) -> p g s", s=S), ALU.add).then_inc(c_q2, 1)

            def normalize(b, i):
                dve.wait_ge(c_OT, b + 1)
                for c in range(CH):
                    o = ps[2 + c][:].rearrange("p (h r) -> p h r", r=ST)
                    dve.reciprocal(rec[:, c, :], o[:, :, DH1]).then_inc(c_rec, 1)
                dve.wait_ge(c_rec, b * 2 + 2)
                ge(dve, c_nT, b)
                for c in range(CH):
                    o = ps[2 + c][:].rearrange("p (h r) -> p h r", r=ST)
                    dve.tensor_tensor(on[:, c, :].rearrange("p (h d) -> p h d", d=DH1), o[:, :, 0:DH1],
                                      rec[:, c, :].unsqueeze(2).broadcast_to([P, H1, DH1]), ALU.mult).then_inc(c_on, 1)

            def residual3(b, i):
                dve.wait_ge(c_Y, b + 1)
                dve.tensor_tensor(x[:, bass.ds(b * CH, CH), :], x[:, bass.ds(b * CH, CH), :],
                                  ps[3][:, 0:CH * D].rearrange("p (c d) -> p c d", d=D), ALU.add).then_inc(s_x3, 1)

            def attend(k, i):
                for n in range(NU):
                    if among(k, B):
                        take_max(k, n)
                    if n == 3 and among(k - 2, B):
                        normalize(k - 2, i)
                    if n == 8 and among(k - 2, B):
                        residual3(k - 2, i)
                    if n == 13 and among(k, B):
                        add_values(k, i)
                if among(k, B):
                    split_max(k)
                    add_max(k, i)

            turns(dve, B, 1, 2, 1, attend)
            dve.wait_ge(s_x3, B)
            if stage == 3:
                return

            ln_stats(dve, v, x, 5)
            ln_apply(dve, v, xn[:], x[:]).then_inc(s_xn, 1)
            dve.memset(cT[:], 0.0).then_inc(d_c, 1)
            dve.tensor_copy(rd(ecol[:]), C("expert_cols")).then_inc(d_c, 1)
            for i in range(4):
                at = slice(i * 512, (i + 1) * 512)
                dve.wait_ge(s_xT, 13 + i)
                v.link(dve.tensor_copy(rd(xTh[:, at]), xT[:, at]))
                dve.tensor_tensor(rd(xTl[:, at]), xT[:, at], xTh[:, at], ALU.subtract).then_inc(d_xT, 1)
            SC, SB, MK, EQ, SEL, ACC = (r1[:, i, :] for i in range(6))
            te = lambda t: t.rearrange("p (t e) -> p t e", e=E1)
            dve.wait_ge(d_sg, 1)
            v.link(dve.tensor_scalar(SC, SC, 1.0, None, ALU.add))
            v.link(dve.reciprocal(SC, SC))
            v.link(dve.tensor_tensor(te(SB), te(SC), A("e_bias").unsqueeze(1).broadcast_to([P, NT, E1]), ALU.add))
            q4 = SB.rearrange("p (m k) -> p m k", k=NG1)
            W = [r4[:, i, :] for i in range(12)]
            v.link(dve.tensor_tensor(W[0], q4[:, :, 0], q4[:, :, 1], ALU.max))
            v.link(dve.tensor_tensor(W[1], q4[:, :, 0], q4[:, :, 1], ALU.min))
            v.link(dve.tensor_tensor(W[2], q4[:, :, 2], q4[:, :, 3], ALU.max))
            v.link(dve.tensor_tensor(W[3], q4[:, :, 2], q4[:, :, 3], ALU.min))
            v.link(dve.tensor_tensor(W[4], W[0], W[2], ALU.max))
            v.link(dve.tensor_tensor(W[5], W[0], W[2], ALU.min))
            v.link(dve.tensor_tensor(W[6], W[1], W[3], ALU.max))
            v.link(dve.tensor_tensor(W[5], W[5], W[6], ALU.max))
            v.link(dve.tensor_tensor(W[4], W[4], W[5], ALU.add))
            g3 = lambda t: t.rearrange("p (t g) -> p t g", g=NG1)
            rev4 = C("rev8")[:, E0 - NG1:]
            pick(dve, v, g3(W[4]), g3(W[7]), g3(W[8]), s4[:, 0, :], s4[:, 1, :], rev4, NT, NG1)
            pick(dve, v, g3(W[4]), g3(W[7]), g3(W[9]), s4[:, 0, :], s4[:, 1, :], rev4, NT, NG1)
            v.link(dve.tensor_tensor(W[8], W[8], W[9], ALU.add))
            v.link(dve.tensor_tensor(MK.rearrange("p (m k) -> p m k", k=NG1), q4,
                                     W[8].unsqueeze(2).broadcast_to([P, NT * NG1, NG1]), ALU.mult))
            for k in range(K1):
                pick(dve, v, te(MK), te(EQ), te(SEL if k else ACC), s4[:, 0, :], s4[:, 1, :], C("rev16"), NT, E1)
                if k:
                    v.link(dve.tensor_tensor(ACC, ACC, SEL, ALU.add))
            v.link(dve.tensor_tensor(ACC, ACC, SC, ALU.mult))
            v.link(dve.tensor_reduce(s4[:, 2, :], te(ACC), AX.X, ALU.add))
            v.link(dve.tensor_scalar(s4[:, 2, :], s4[:, 2, :], 1e-20, None, ALU.add))
            v.link(dve.reciprocal(s4[:, 3, :], s4[:, 2, :]))
            v.link(dve.tensor_scalar(s4[:, 3, :], s4[:, 3, :], SHARE1, None, ALU.mult))
            v.link(dve.tensor_tensor(te(ACC), te(ACC), s4[:, 3, :].unsqueeze(2).broadcast_to([P, NT, E1]), ALU.mult))
            v.link(dve.tensor_copy(rd(chl[:, :, 0:E1]), te(ACC)))
            dve.tensor_tensor(rd(chl[:, :, E1:]), te(ACC), chl[:, :, 0:E1], ALU.subtract).then_inc(d_cm, 1)
            for i in range(4):
                dve.wait_ge(d_cT, i + 1)
                dve.tensor_copy(rd(cT[0:2 * E1, i * 512:(i + 1) * 512]), ps[i][0:2 * E1, :]).then_inc(d_cc, 1)

            with dve.Fori(0, T // TT // 2) as it:
                for k in range(2):
                    for c in range(FC1):
                        n = k * FC1 + c
                        dve.wait_ge(d_U, it * (2 * FC1) + (n + 1))
                        dve.wait_ge(d_sl, it * (2 * FC1) + (n + 1))
                        if c == 0:
                            dve.wait_ge(d_Y, it * 2 + (k + 1))
                        if c == FC1 - 1:
                            dve.tensor_tensor(hT1[k][:, c, :], sg1[n % 2][:], pw[1][:, n % 2 * TT:(n % 2 + 1) * TT],
                                              ALU.mult).then_inc(d_h1, 1)
                            dve.wait_ge(d_h1, it * (2 * FC1) + (n + 3))
                            continue
                        dve.tensor_tensor(h1[n % 2][:], sg1[n % 2][:], pw[1][:, n % 2 * TT:(n % 2 + 1) * TT],
                                          ALU.mult).then_inc(d_h1, 1)
                        dve.wait_ge(d_h1, it * (2 * FC1) + (n + 3))
                        dve.tensor_tensor(hT1[k][:, c, :], h1[n % 2][:], ps[c % 2][:], ALU.mult).then_inc(d_h, 1)
                    dve.wait_ge(d_Y, it * 2 + (k + 3))
                    at = bass.ds((it * 2 + k) * (TT // P), TT // P)
                    dve.scalar_tensor_tensor(out=x[:, at, :], in0=ps[2 + k][:].rearrange("p (t d) -> p t d", d=D),
                                             scalar=tg[:, 3:4], in1=x[:, at, :], op0=ALU.mult, op1=ALU.add)\
                        .then_inc(d_x4, 1)

        @block.scalar
        def _(act):
            ch = Chain(act, s_a)
            ln_power(act, ch, 1)
            act.wait_ge(s_par, 16)
            act.activation(tg[:], A("gates"), ACT.Tanh).then_inc(s_tg, 1)
            for i in range(4):
                act.wait_ge(s_gps, i + 1)
                bank = (pw[0][:, 0:512], pw[0][:, 512:1024], pw[1][:, 0:512], pw[1][:, 512:1024])[i]
                act.activation(xn_gates(xn)[:, i * 512:(i + 1) * 512], bank[0:2 * H0, :], ACT.Copy).then_inc(s_gT, 1)
            IG, FG, AZ, EZ, L, LF, CS, AA, MM, ONE = range(10)
            g = lambda i: g64[:, i, :]
            act.wait_ge(s_z, 1)
            ch.link(act.activation(g(AZ), g(FG), ACT.Abs))
            ch.link(act.activation(g(EZ), g(AZ), ACT.Exp, scale=-1.0))
            act.activation(g(L), g(EZ), ACT.Ln, bias=1.0).then_inc(s_sp, 1)
            act.wait_ge(s_aM, 1)
            act.activation(t64[:, 0:P], g64[:, AA, 0:P], ACT.Exp, bias=negM[:, 0:1]).then_inc(s_t64, 1)
            act.activation(t64[:, 2 * P:], g(CS), ACT.Exp, scale=-1.0).then_inc(s_t64, 1)
            act.activation(t64[:, P:2 * P], g64[:, MM, P:S], ACT.Exp, bias=g64[:, MM, P - 1:P], scale=-1.0)\
               .then_inc(s_t64, 1)
            with act.Fori(0, B // 2) as it:
                for u in range(4):
                    if u % 2 == 0:
                        act.wait_ge(s_free, it * 2 + (u // 2 + 1))
                        act.activation(qS[u // 2][:], xT[:, bass.ds((it * 2 + u // 2) * S + P, P)], ACT.Copy)\
                            .then_inc(s_qS, 1)
                    act.wait_ge(s_E, it * 4 + (u + 1))
                    act.wait_ge(s_C, it * 4 + (u + 1))
                    act.activation(Dm[u % 2][:], pw[0][:], ACT.Exp).then_inc(s_D, 1)
                    act.wait_ge(s_w[u % 2], it * 32 + (16 * (u // 2 + 1)))
                    act.activation(rd(wh[:, bass.ds((it * 4 + u) * F0, F0)]), wst[u % 2][:], ACT.Copy)\
                        .then_inc(s_wh, 1)
            ln_power(act, ch, 2)
            if stage == 1:
                return

            ln_power(act, ch, 3)
            for i in range(4):
                act.wait_ge(s_tr, 5 + i)
                act.activation(xT[:, i * 512:(i + 1) * 512], ps[i][:], ACT.Copy).then_inc(s_xT, 1)
            act.wait_ge(s_lx, 1)
            act.activation(rt[:, 1, :], rt[:, 0, :], ACT.Exp).then_inc(s_ex, 1)

            def silu(j, i):
                act.wait_ge(s_G, j + 1)
                ge(act, s_hb, j - 1)
                act.activation(sg[i][:], pw[0][:, i * F0:(i + 1) * F0], ACT.Silu).then_inc(s_sg, 1)

            def copy_hidden(j, i):
                act.wait_ge(s_H, j + 1)
                ge(act, s_Y, j - 1)
                act.activation(hT[i][:], ps[1 + i][:], ACT.Copy).then_inc(s_hT, 1)

            pipelined(act, NBLK, [(silu, 0), (copy_hidden, 1)], peel=2)
            if stage == 2:
                return

            ln_power(act, ch, 4)
            for i in range(4):
                act.wait_ge(s_tr, 9 + i)
                act.activation(xT[:, i * 512:(i + 1) * 512], ps[i][:], ACT.Copy).then_inc(s_xT, 1)

            def exponentials(b, n):
                g, c, half = n // 4, n // 2 % 2, n % 2
                act.wait_ge(c_P2, b * NU + (n + 1))
                if n % 4 == 0:
                    ge(act, c_PV, b * HG + (g - 1))
                act.activation(et3[g % 2][c][:, 2 * half:2 * half + 2, :],
                               pw[1][:, half * 512:(half + 1) * 512].rearrange("p (j s) -> p j s", s=S), ACT.Exp)\
                    .then_inc(c_X, 1)

            def copy_sums(b, k):
                act.wait_ge(c_PV, b * HG + (2 * k + 2))
                if k == 0:
                    ge(act, c_OT, b)
                act.activation(o32[:, 2 * k:2 * k + 2, :], ps[2 + k][:].rearrange("p (g s) -> p g s", s=S), ACT.Copy)\
                    .then_inc(c_O, 1)

            def copy_keys(b):
                act.wait_ge(c_K, b + 1)
                ge(act, c_ks, b)
                for g in range(HG):
                    act.activation(k32[:, g, :], ps[g // 2][:, g % 2 * S:(g % 2 + 1) * S], ACT.Identity,
                                   bias=A("bk")[:, g:g + 1]).then_inc(c_k32, 1)
                act.wait_ge(c_k32, b * HG + HG)
                act.activation(rd(khi[:]), k32[:], ACT.Copy, scale=C("key_lo")).then_inc(c_khi, 1)

            def copy_queries(b):
                act.wait_ge(c_Q, b + 1)
                ge(act, c_qs, b)
                for g in range(HG):
                    act.activation(q32[:, g, :], ps[g // 2][:, g % 2 * S:(g % 2 + 1) * S], ACT.Identity,
                                   bias=bqs[:, g:g + 1], scale=float(DH1) ** -0.5).then_inc(c_q32, 1)
                act.wait_ge(c_q32, b * HG + HG)
                act.activation(rd(qhi[:]), q32[:], ACT.Copy, scale=C("query_lo")).then_inc(c_qhi, 1)

            def copy_turned(b):
                act.wait_ge(c_nT, b + 1)
                ge(act, c_Y, b)
                act.activation(onT[:], ps[2][:, 0:CH * P].rearrange("p (c s) -> p c s", s=P), ACT.Copy)\
                    .then_inc(c_nc, 1)

            def attend(k, i):
                if among(k + 1, B):
                    copy_keys(k + 1)
                for n in range(NU):
                    if among(k - 1, B):
                        exponentials(k - 1, n)
                    if n == 1 and among(k - 2, B):
                        copy_turned(k - 2)
                    if n == 3 and among(k + 1, B):
                        copy_queries(k + 1)
                    if n == 11 and among(k - 1, B):
                        copy_sums(k - 1, 0)
                if among(k - 1, B):
                    copy_sums(k - 1, 1)

            act.wait_ge(c_wc, 2)
            turns(act, B, 1, 2, 1, attend)
            if stage == 3:
                return

            act.wait_ge(s_x3, B)
            ln_power(act, ch, 5)
            for i in range(4):
                act.wait_ge(s_tr, 13 + i)
                act.activation(xT[:, i * 512:(i + 1) * 512], ps[i][:], ACT.Copy).then_inc(s_xT, 1)
            act.wait_ge(d_w, 32)
            for k in range(2):
                at = slice(k * FC1 * P, (k + 1) * FC1 * P)
                act.activation(rd(guh[:, at]), graw[:, at], ACT.Copy).then_inc(d_wh, 1)
            act.wait_ge(d_lg, 1)
            act.activation(r1[:, 0, :], pw[0][:, 0:NT * E1], ACT.Exp, scale=-1.0).then_inc(d_sg, 1)
            with act.Fori(0, T // TT // 2) as it:
                for n in range(2 * FC1):
                    act.wait_ge(d_G, it * (2 * FC1) + (n + 1))
                    act.wait_ge(d_h1, it * (2 * FC1) + (n + 1))
                    act.activation(sg1[n % 2][:], pw[0][:, n % 2 * TT:(n % 2 + 1) * TT], ACT.Silu).then_inc(d_sl, 1)

        @block.gpsimd
        def _(pool):
            pool.sem_inc(s_free, 2)
            pool.sem_inc(s_PV, 2)
            pool.sem_inc(s_C, 2)
            pool.sem_inc(s_wl, 2)
            pool.wait_ge(s_xT, 4)
            with pool.Fori(0, B // 2) as it:
                for i in range(2):
                    b = it * 2 + i
                    pool.wait_ge(s_free, it * 2 + (i + 1))
                    pool.tensor_tensor(Qm[i][:], xT[:, bass.ds(b * S, S)].unsqueeze(1).broadcast_to([P, H0, S]),
                                       C("quarter_of_head").unsqueeze(2).broadcast_to([P, H0, S]), ALU.mult)\
                        .then_inc(s_qm, 1)
                    for u in (2 * i, 2 * i + 1):
                        pool.wait_ge(s_wh, it * 4 + (u + 1))
                        at = bass.ds((it * 4 + u) * F0, F0)
                        pool.tensor_tensor(rd(wl[:, at]), wst[u % 2][:], wh[:, at], ALU.subtract).then_inc(s_wl, 1)

            if stage == 1:
                return
            pool.wait_ge(s_clr, 16)
            pool.wait_ge(s_xn, 2)
            for k in range(2):
                pool.wait_ge(s_sl, k + 1)
                for t in range(NT):
                    pool.indirect_dma_start(out=scr_x, out_offset=bass.IndirectOffsetOnAxis(slot[:, k, t:t + 1], axis=0),
                                            in_=xn[:, t, :], in_offset=None).then_inc(s_sc, 16)
            def store_block(j, i):
                pool.wait_ge(s_yb, j + 1)
                pool.dma_start(scr_y[bass.ds(j * P, P), :], yb[i][:]).then_inc(s_ys[i], 16)

            pipelined(pool, NBLK, [(store_block, 0)])
            for i in range(2):
                pool.wait_ge(s_ys[i], 16 * (NBLK // 2))
            for t in range(NT):
                for k in range(2):
                    pool.indirect_dma_start(out=gy[k][:, t, :], out_offset=None, in_=scr_y,
                                            in_offset=bass.IndirectOffsetOnAxis(slot[:, k, t:t + 1], axis=0))\
                        .then_inc(s_gy[t], 16)
            if stage == 2:
                return

            def split(k, i):
                if not among(k + 1, B):
                    return
                pool.wait_ge(c_khi, k + 2)
                if among(k, B):
                    pool.wait_ge(c_kd[i], loads(k, i, 64))
                    pool.wait_ge(c_kst[i], loads(k, i, 16))
                pool.tensor_tensor(rd(Kn[:]), k32[:], khi[:], ALU.subtract).then_inc(c_ks, 1)
                pool.wait_ge(c_qhi, k + 2)
                ge(pool, c_q2, k * 2)
                pool.tensor_tensor(rd(Qs[1 - i][:]), q32[:], qhi[:], ALU.subtract).then_inc(c_qs, 1)

            turns(pool, B, 1, 0, 3, split)
            if stage == 3:
                return

            pool.sem_inc(d_Y, 2)
            pool.sem_inc(d_h1, 2)
            pool.sem_inc(d_h, 2)
            for k in range(2):
                at = slice(k * FC1 * P, (k + 1) * FC1 * P)
                pool.wait_ge(d_wh, k + 1)
                pool.tensor_tensor(rd(gul[:, at]), graw[:, at], guh[:, at], ALU.subtract).then_inc(d_wl, 1)

        @block.tensor
        def _(pe):
            pe.wait_ge(s_con, 16)
            pe.wait_ge(s_xn, 1)
            for i in range(4):
                for k in range(4):
                    ins = pe.transpose(ps[i][:, k * P:(k + 1) * P], xn[:, 4 * i + k, :], C("ident"))
                ins.then_inc(s_tr, 1)
            pe.wait_ge(s_ctx, 16)
            pe.wait_ge(s_bc, 8)
            for i in range(4):
                bank = (pw[0][:, 0:512], pw[0][:, 512:1024], pw[1][:, 0:512], pw[1][:, 512:1024])[i]
                pe.wait_ge(s_xT, i + 1)
                pe.matmul(bank[0:2 * H0, :], A("gwq"), xT[:, i * 512:(i + 1) * 512], start=True, stop=False)
                pe.matmul(bank[0:2 * H0, :], gwc[:], ctxT[:, i * 512:(i + 1) * 512], start=False, stop=True)\
                    .then_inc(s_gps, 1)
            pe.wait_ge(s_t64, 3)
            for k in range(4):
                pe.transpose(ps[0][:, k * BH:(k + 1) * BH], t64[:, k * P:(k + 1) * P], C("ident")[0:BH, 0:BH])\
                    .then_inc(s_wps, 1)
            pe.wait_ge(s_bc, 9)
            pe.wait_ge(s_wT, 1)
            pe.wait_ge(s_gT, 4)

            def exponent(it, u):
                i, c = u // 2, u % 2
                if c == 0:
                    pe.wait_ge(s_ls, it * 2 + (i + 1))
                if u:
                    pe.wait_ge(s_D, it * 4 + u)
                for half in range(2):
                    o = pw[0][:, half * 512:(half + 1) * 512]
                    hs = slice(4 * half, 4 * half + 4)
                    pe.matmul(o, ident_bf[:], future_bf[:], start=True, stop=False)
                    pe.matmul(o, rd(LS[i][:, 2 * P:]), rd(Rm[:, hs, c * P:(c + 1) * P]), start=False, stop=False)
                    ins = pe.matmul(o, rd(LS[i][:, c * P:(c + 1) * P]), rd(dlt[:, hs, :]), start=False, stop=True)
                ins.then_inc(s_E, 1)

            with pe.Fori(0, B // 2) as it:
                exponent(it, 0)
                for u in range(4):
                    i, c = u // 2, u % 2
                    b = it * 2 + i
                    if c == 0:
                        pe.wait_ge(s_ct[i], it * 16 + 16)
                        pe.wait_ge(s_qm, it * 2 + (i + 1))
                    for half in range(2):
                        ins = pe.matmul(pw[1][:, half * 512:(half + 1) * 512], ctS[i][:, c * P:(c + 1) * P],
                                        Qm[i][:, 4 * half:4 * half + 4, c * P:(c + 1) * P], start=True, stop=True)
                    ins.then_inc(s_S, 1)
                    if c == 0:
                        pe.wait_ge(s_ks, it * 2 + (i + 1))
                        if i:
                            pe.wait_ge(s_It, it * 2 + 1)
                        pe.matmul(ps[1][:, 0:H0 * VW], Ks[i][:], vaug[:, b * CH, :], start=True, stop=True)\
                            .then_inc(s_st, 1)
                    if u < 3:
                        exponent(it, u + 1)
                    if c == 1:
                        pe.wait_ge(s_stm, it * 2 + (i + 1))
                        pe.wait_ge(s_qS, it * 2 + (i + 1))
                        pe.matmul(ps[1][:, 256:256 + H0 * VW], qS[i][:], stm[:], start=True, stop=True)\
                            .then_inc(s_I, 1)
                    pe.wait_ge(s_C, it * 4 + (u + 3))
                    if u:
                        pe.wait_ge(s_num, it * 4 + u)
                    for h in range(H0):
                        ins = pe.matmul(ps[0][:, h * VW:(h + 1) * VW], Cm[u % 2][:, h * P:(h + 1) * P],
                                        vaug[:, b * CH + c, h * VW:(h + 1) * VW], start=True, stop=True)
                    ins.then_inc(s_PV, 1)
                    if c == 1:
                        pe.matmul(ps[3][0:32, 0:2], ones_bf[:, 0:32], ones_bf[:, 0:2], start=True, stop=True)\
                            .then_inc(s_free, 1)
                pe.wait_ge(s_num, it * 4 + 4)
            if stage == 1:
                return

            pe.wait_ge(s_xn, 2)
            for i in range(4):
                for k in range(4):
                    ins = pe.transpose(ps[i][:, k * P:(k + 1) * P], xn[:, 4 * i + k, :], C("ident"))
                ins.then_inc(s_tr, 1)
            for t in range(NT):
                if t % 4 == 0:
                    pe.wait_ge(s_xT, 5 + t // 4)
                ins = pe.matmul(pw[0][:, t * E0:(t + 1) * E0], xT[:, t * P:(t + 1) * P], A("router0"),
                                start=True, stop=True)
            ins.then_inc(s_lg, 1)
            pe.wait_ge(s_ro, 1)
            pe.matmul(ps[0][:, 0:P], before_bf[:], routed[:], start=True, stop=True)
            pe.matmul(ps[0][:, P:2 * P], ones_bf[:], routed[:], start=True, stop=True).then_inc(s_rk, 1)
            pe.wait_ge(s_be, 1)
            pe.wait_ge(s_w2, 16)
            pe.wait_ge(s_wl, 2 + 2 * E0)

            def tokens(j, i):
                ge(pe, s_xp, j * 2)
                if isinstance(j, int):
                    pe.wait_ge(s_xg[i], 16 * (j // 2 + 1))
                else:
                    pe.wait_ge(s_xg[i], (j - i) * 8 + 16)
                pe.transpose(ps[0][:, 0:P], xg[i][:], C("ident")).then_inc(s_T, 1)

            def up(j, i):
                at = pe.value_load(boff[0:1, bass.ds(j, 1)], min_val=0, max_val=(E0 - 1) * F0)
                pe.wait_ge(s_xp, j * 2 + 2)
                for bank, m, free, ready in ((pw[0], 0, s_sg, s_G), (pw[1], 1, s_hb, s_U)):
                    o = bank[:, i * F0:(i + 1) * F0]
                    ge(pe, free, j - 1)
                    hi, lo = (w[:, bass.ds(at + m * E0 * F0, F0)] for w in (wh, wl))
                    pe.matmul(o, rd(xgh[i][:]), rd(hi), start=True, stop=False)
                    pe.matmul(o, rd(xgh[i][:]), rd(lo), start=False, stop=False)
                    pe.matmul(o, rd(xgl[i][:]), rd(hi), start=False, stop=True).then_inc(ready, 1)

            def turn_hidden(j, i):
                pe.wait_ge(s_hb, j + 1)
                ge(pe, s_hT, j - 1)
                for c in range(FC0):
                    ins = pe.transpose(ps[1 + i][:, c * P:(c + 1) * P], hb[i][:, c * P:(c + 1) * P], C("ident"))
                ins.then_inc(s_H, 1)

            def down(j, i):
                at = pe.value_load(boff[0:1, bass.ds(j, 1)], min_val=0, max_val=(E0 - 1) * F0)
                pe.wait_ge(s_hT, j + 1)
                ge(pe, s_yb, j)
                for c in range(FC0):
                    ins = pe.matmul(ps[3][:, 0:P], hT[i][:, c * P:(c + 1) * P], w2[:, bass.ds(at + c * D, D)],
                                    start=(c == 0), stop=(c == FC0 - 1))
                ins.then_inc(s_Y, 1)

            pipelined(pe, NBLK, [(up, 0), (tokens, -1), (turn_hidden, 1), (down, 2)], peel=2)
            if stage == 2:
                return

            pe.wait_ge(s_xn, 3)
            pe.wait_ge(s_yb, NBLK)
            for i in range(4):
                for k in range(4):
                    ins = pe.transpose(ps[i][:, k * P:(k + 1) * P], xn[:, 4 * i + k, :], C("ident"))
                ins.then_inc(s_tr, 1)
            pe.wait_ge(c_wa, 1)
            pe.wait_ge(s_xT, 12)
            pe.matmul(ps[0][:, 0:P], wem[:], A("wo"), start=True, stop=True)
            pe.matmul(ps[0][:, P:2 * P], bemb[:], A("wo"), start=True, stop=True).then_inc(c_wp, 1)
            pe.wait_ge(c_wc, 2)

            def scores_for_max(b, i, n):
                c, g, half = n // 8, n // 2 % 4, n % 2
                if n == 0:
                    pe.wait_ge(c_qs, b + 1)
                    pe.wait_ge(c_kd[i], loads(b, i, 64))
                ge(pe, c_R, b * NU + (n - 1) if n else (b - 1) * NU + (NU - 1))
                pe.matmul(pw[0][:, half * 512:(half + 1) * 512], rd(Qs[i][:, g, c * P:(c + 1) * P]),
                          rd(Kd[i][:, g, 2 * half:2 * half + 2, :]), start=True, stop=True).then_inc(c_P1, 1)

            def scores_less_max(b, i, n):
                g, c, half = n // 4, n // 2 % 2, n % 2
                if n == 0:
                    pe.wait_ge(c_qd, b * 64 + 64)
                    pe.wait_ge(c_kst[i], loads(b, i, 16))
                ge(pe, c_X, b * NU + (n - 1) if n else (b - 1) * NU + (NU - 1))
                pe.matmul(pw[1][:, half * 512:(half + 1) * 512], rd(Kst[i][:, g, c * P:(c + 1) * P]),
                          rd(Qd[:, g, 2 * half:2 * half + 2, :]), start=True, stop=True).then_inc(c_P2, 1)

            def weighted_sums(b, i, g):
                pe.wait_ge(c_X, b * NU + (4 * g + 4))
                if g == 0:
                    pe.wait_ge(c_vp, b + 1)
                    ge(pe, c_nc, b)
                if g == 2:
                    ge(pe, s_x3, b)
                for c in range(CH):
                    for j in range(HJ):
                        ins = pe.matmul(ps[2 + g // 2][j * ST:(j + 1) * ST, g % 2 * S:(g % 2 + 1) * S],
                                        vp[i][:, c, HJ * g + j, :], et3[g % 2][c][:, j, :],
                                        start=(c == 0), stop=(c == CH - 1), skip_group_check=True)
                ins.then_inc(c_PV, 1)

            def keys(b):
                ge(pe, c_q2, (b - 1) * 2)
                for g in range(HG):
                    ins = pe.matmul(ps[g // 2][:, g % 2 * S:(g % 2 + 1) * S], wks[:, g * P:(g + 1) * P],
                                    ctxT[:, bass.ds(b * S, S)], start=True, stop=True)
                ins.then_inc(c_K, 1)

            def queries(b):
                pe.wait_ge(c_k32, b * HG + HG)
                for g in range(HG):
                    ins = pe.matmul(ps[g // 2][:, g % 2 * S:(g % 2 + 1) * S], wqs[:, g * P:(g + 1) * P],
                                    xT[:, bass.ds(b * S, S)], start=True, stop=True)
                ins.then_inc(c_Q, 1)

            def values(b, i):
                pe.wait_ge(c_ct[i], loads(b, i, 16))
                pe.wait_ge(c_q32, min(b + 2, B) * HG if isinstance(b, int) else b * HG + 2 * HG)
                for c in range(CH):
                    ins = pe.matmul(ps[0][:, c * D:(c + 1) * D], ctS[i][:, c * P:(c + 1) * P], A("wv"),
                                    start=True, stop=True)
                ins.then_inc(c_V, 1)

            def max_rows(b):
                pe.wait_ge(c_mp, b * 2 + 2)
                pe.wait_ge(c_vp, b + 1)
                for g in range(HG):
                    for c in range(CH):
                        at = g % 2 * S + c * P
                        ins = pe.transpose(ps[g // 2][:, at:at + P], mp[:, c, g, :], C("ident"))
                ins.then_inc(c_MT, 1)

            def turn_sums(b):
                pe.wait_ge(c_O, b * 2 + 2)
                for c in range(CH):
                    for g in range(HG):
                        ins = pe.transpose(ps[2 + c][:, g * P:(g + 1) * P], o32[:, g, c * P:(c + 1) * P], C("ident"))
                ins.then_inc(c_OT, 1)

            def turn_attention(b):
                pe.wait_ge(c_on, b * 2 + 2)
                for c in range(CH):
                    ins = pe.transpose(ps[2][:, c * P:(c + 1) * P], on[:, c, :], C("ident"))
                ins.then_inc(c_nT, 1)

            def attention_out(b):
                pe.wait_ge(c_nc, b + 1)
                for c in range(CH):
                    ins = pe.matmul(ps[3][:, c * D:(c + 1) * D], onT[:, c, :], wc[:], start=True, stop=True)
                ins.then_inc(c_Y, 1)

            def attend(k, i):
                for n in range(NU + 4):
                    if n < NU and among(k, B):
                        scores_for_max(k, i, n)
                    if n == 1 and among(k + 1, B):
                        keys(k + 1)
                    if n == 2 and among(k - 2, B):
                        turn_sums(k - 2)
                    if n >= 4 and among(k - 1, B):
                        scores_less_max(k - 1, 1 - i, n - 4)
                    if n == 5 and among(k - 2, B):
                        turn_attention(k - 2)
                    if n == 6 and among(k + 1, B):
                        queries(k + 1)
                    if n == 8 and among(k - 2, B):
                        attention_out(k - 2)
                    if n in (10, 14, 18) and among(k - 1, B):
                        weighted_sums(k - 1, 1 - i, (n - 10) // 4)
                    if n == 12 and among(k, B):
                        values(k, i)
                    if n == 19 and among(k, B):
                        max_rows(k)
                if among(k - 1, B):
                    weighted_sums(k - 1, 1 - i, 3)

            turns(pe, B, 1, 2, 1, attend)
            if stage == 3:
                return

            pe.wait_ge(s_xn, 4)
            for i in range(4):
                for k in range(4):
                    ins = pe.transpose(ps[i][:, k * P:(k + 1) * P], xn[:, 4 * i + k, :], C("ident"))
                ins.then_inc(s_tr, 1)
            for t in range(NT):
                if t % 4 == 0:
                    pe.wait_ge(s_xT, 13 + t // 4)
                ins = pe.matmul(pw[0][:, t * E1:(t + 1) * E1], xT[:, t * P:(t + 1) * P], A("router1"),
                                start=True, stop=True)
            ins.then_inc(d_lg, 1)
            pe.wait_ge(d_cm, 1)
            for i in range(4):
                for k in range(4):
                    ins = pe.transpose(ps[i][0:2 * E1, k * P:(k + 1) * P], chl[:, 4 * i + k, :], C("ident"))
                ins.then_inc(d_cT, 1)
            pe.wait_ge(d_cc, 4)
            pe.wait_ge(d_wl, 2)
            pe.wait_ge(d_c, 2)
            pe.wait_ge(d_xT, 4)

            def hidden_units(it, k, c):
                n = k * FC1 + c
                t = bass.ds((it * 2 + k) * TT, TT)
                half = slice(n % 2 * TT, (n % 2 + 1) * TT)
                for m, (bank, free, ready) in enumerate(((pw[0], d_sl, d_G), (pw[1], d_h1, d_U))):
                    if n >= 2:
                        pe.wait_ge(free, it * (2 * FC1) + (n - 1 + 2 * m))
                    f = slice((m * FC1 + c) * P, (m * FC1 + c + 1) * P)
                    pe.matmul(bank[:, half], rd(guh[:, f]), rd(xTh[:, t]), start=True, stop=False)
                    pe.matmul(bank[:, half], rd(gul[:, f]), rd(xTh[:, t]), start=False, stop=False)
                    ins = pe.matmul(bank[:, half], rd(guh[:, f]), rd(xTl[:, t]), start=False, stop=True)
                    if m == 0:
                        ins.then_inc(ready, 1)
                if c < FC1 - 1:
                    ins.then_inc(d_Us, 1)
                    pe.wait_ge(d_h, it * (2 * (FC1 - 1)) + (k * (FC1 - 1) + c + 1))
                    ins = pe.matmul(ps[c % 2][:], rd(ecol[:, c * P:(c + 1) * P]), rd(cT[:, t]), start=True, stop=True)
                ins.then_inc(ready, 1)

            def down2(it, k):
                pe.wait_ge(d_h1, it * (2 * FC1) + (k * FC1 + FC1 + 2))
                pe.wait_ge(d_h, it * (2 * (FC1 - 1)) + ((k + 1) * (FC1 - 1) + 2))
                for q in range(TT // P):
                    for c in range(FC1):
                        ins = pe.matmul(ps[2 + k][:, q * D:(q + 1) * D], hT1[k][:, c, q * P:(q + 1) * P], dn[:, c, :],
                                        start=(c == 0), stop=(c == FC1 - 1))
                ins.then_inc(d_Y, 1)

            with pe.Fori(0, T // TT // 2) as it:
                for c in range(FC1):
                    hidden_units(it, 0, c)
                for c in range(FC1):
                    hidden_units(it, 1, c)
                    if c == 1:
                        down2(it, 0)
                down2(it, 1)


def xn_gates(xn):
    return xn[0:2 * H0, :, :].rearrange("p t d -> p (t d)")


def kernel(**inputs):
    import numpy as np
    import concourse.bacc as bacc
    from concourse.bass_utils import run_bass_kernel_spmd as run

    nc = bacc.Bacc("TRN2", target_bir_lowering=False, num_devices=1)
    arrays = lay_out(np, {k: np.asarray(v) for k, v in inputs.items()})
    aps = {}
    for name, arr in arrays.items():
        aps[name] = nc.dram_tensor("in_" + name, arr.shape, mybir.dt.from_np(arr.dtype), kind="ExternalInput").ap()
    out = nc.dram_tensor("out", (P, NT * D), F32, kind="ExternalOutput").ap()
    scr_x = nc.dram_tensor("scratch_x", (NBLK * P, D), F32).ap()
    scr_y = nc.dram_tensor("scratch_y", (NBLK * P, D), F32).ap()
    build(nc, aps, scr_x, scr_y, out)
    r = run(nc, [{"in_" + n: t for n, t in arrays.items()}], core_ids=[0])
    got = r.results[0]["out"]
    return np.ascontiguousarray(got.reshape(P, NT, D).transpose(1, 0, 2).reshape(B, S, D))


def lay_out(np, v):
    f = np.float32

    def tiles(t):
        return t.reshape(NT, P, D).transpose(1, 0, 2)

    x, ctx = v["x"].reshape(T, D), v["ctx_1024"].reshape(T, D)
    va = np.ones((P, NT, H0, VW), f)
    va[..., :DH0] = tiles(ctx).reshape(P, NT, H0, DH0)

    r = np.arange(P)
    con = np.zeros((P, NCONST), f)
    c = {k: con[:, s:e] for k, (s, e) in CONST.items()}
    c["ident"][:] = np.eye(P)
    c["future"][:] = np.where(r[:, None] > r[None, :], NEG, 0.0)
    c["before"][:] = r[:, None] < r[None, :]
    c["of_seq"][:] = (r[:, None] % BH) // H0 == np.arange(B)
    c["of_head"][:] = r[:, None] % H0 == np.arange(H0)
    c["neg_of_head"][:] = -1.0 * (r[:, None] % H0 == np.arange(H0))
    c["quarter_of_head"][:] = 0.25 * (r[:, None] // DH0 == np.arange(H0))
    c["quarter_block"][:] = np.repeat(0.25 * (r[:, None] // DH0 == np.arange(H0)), VW, 1)
    c["block_start"][:] = P * np.arange(NT)
    c["not_first"][:] = np.arange(P) % NT != 0
    c["block_index"][:] = np.repeat(np.arange(NBLK), E0)
    c["rev8"][:] = E0 - np.arange(E0)
    c["rev16"][:] = E1 - np.arange(E1)
    c["query_lo"][:, 0] = 1.0 * (r % ST // DH1 == 2)
    c["key_lo"][:, 0] = 1.0 * (r % ST // DH1 == 1)
    for e in range(E1):
        for row in (e, E1 + e):
            c["expert_cols"][row, I1 * e:I1 * (e + 1)] = 1.0
    par = np.zeros((P, NPARAM), f)
    q = {k: par[:, s:e] for k, (s, e) in PARAM.items()}
    iw, fw = v["L0_xattn_igate_w"], v["L0_xattn_fgate_w"]
    for k, name in enumerate(("gwq", "gwk", "gwv")):
        q[name][:, :H0] = iw[:, k * D:(k + 1) * D].T
        q[name][:, H0:] = fw[:, k * D:(k + 1) * D].T
    q["gate_b"][:BH, 0] = np.tile(v["L0_xattn_igate_b"], B)
    q["gate_b"][:BH, 1] = np.tile(v["L0_xattn_fgate_b"], B)
    q["ln_scale"][:] = v["L0_xattn_ln_scale"]
    q["gates"][:, 0], q["gates"][:, 1] = v["g_xattn"][0], v["g_ffn"][0]
    q["gates"][:, 2], q["gates"][:, 3] = v["g_xattn"][1], v["g_ffn"][1]
    q["router0"][:] = v["L0_ffn_gate_w"]
    q["router1"][:] = v["L1_ffn_router_weight"].T
    q["e_bias"][:] = v["L1_ffn_e_bias"]
    wqs, wks = np.zeros((P, HG, HJ, ST), f), np.zeros((P, HG, HJ, ST), f)
    for w, wt, bias in ((wqs, "L1_xattn_Wq", "bq"), (wks, "L1_xattn_Wk", "bk")):
        b4 = v["L1_xattn_" + bias].reshape(HG, HJ, DH1)
        for k in range(3):
            at = slice(k * DH1, (k + 1) * DH1)
            w[:, :, :, at] = v[wt].T.reshape(P, HG, HJ, DH1)
            q[bias].reshape(HJ, ST, HG)[:, at, :] = b4.transpose(1, 2, 0)
    for j in range(HJ):
        q["bk"][j * ST + SM:j * ST + SM + 2] = 1.0
    q["bv"][:] = v["L1_xattn_bv"]
    q["wv"][:] = v["L1_xattn_Wv"].T
    q["wo"][:] = v["L1_xattn_Wo"].T
    q["be"][:] = v["L1_xattn_be"].T
    q["bo"][:] = v["L1_xattn_bo"]
    gu = np.zeros((P, 2, FC1 * P), f)
    for m, (routed, shared) in enumerate((("L1_ffn_gate_w", "L1_ffn_sh_gate_w"), ("L1_ffn_up_w", "L1_ffn_sh_up_w"))):
        gu[:, m, :E1 * I1] = v[routed].transpose(2, 0, 1).reshape(P, E1 * I1)
        gu[:, m, E1 * I1:] = v[shared].T
    down = np.zeros((P, FC1, D), f)
    down[:, :FC1 - 1] = v["L1_ffn_down_w"].transpose(0, 2, 1).reshape(FC1 - 1, P, D).transpose(1, 0, 2)
    down[:, FC1 - 1] = v["L1_ffn_sh_down_w"].T
    w13 = np.zeros((P, 2 * E0 * F0), f)
    w13[:, :E0 * F0] = v["L0_ffn_w1"].transpose(1, 0, 2).reshape(P, E0 * F0)
    w13[:, E0 * F0:2 * E0 * F0] = v["L0_ffn_w3"].transpose(1, 0, 2).reshape(P, E0 * F0)
    arrays = {
        "x_nat": tiles(x).reshape(P, NT * D), "ctxT": ctx.T, "vaug": va.reshape(P, NT * H0 * VW),
        "const": con, "param": par, "w13": w13,
        "wqs": wqs.reshape(P, HG * P), "wks": wks.reshape(P, HG * P),
        "we": v["L1_xattn_We"].transpose(1, 0, 2).reshape(P, EO * D),
        "gu": gu.reshape(P, 2 * FC1 * P), "down": down.reshape(P, FC1 * D),
        "w2": v["L0_ffn_w2"].reshape(E0, FC0, P, D).transpose(2, 0, 1, 3).reshape(P, E0 * F0),
    }
    return {k: np.ascontiguousarray(t) for k, t in arrays.items()}
```

```python
from contextlib import ExitStack

import concourse.bass as bass
from concourse import mybir

P = 128
B, S, D = 8, 256, 128
T = B * S
NT = T // P
CH = S // P
H0, DH0 = 8, 16
VW = DH0 + 1
BH = B * H0
E0, F0 = 8, 512
FC0 = F0 // P
NBLK = (2 * T + E0 * (P - 1)) // P
NBLK += NBLK % 2
H1, DH1 = 16, 8
HG, HJ = 4, 4
ST = P // HJ
NU = 2 * CH * HG
SM = 3 * DH1
EO = 8
E1, I1, K1 = 16, 64, 4
SHARE1 = 2.5
NG1 = 4
FC1 = E1 * I1 // P + 1
TT = 512
LN_EPS = 1e-5
NORM_EPS = 1e-6
NEG = -1.0e30
LOWEST = -3.0e38
ROOT_GUESS = 0x5f3759df

ALU = mybir.AluOpType
ACT = mybir.ActivationFunctionType
AX = mybir.AxisListType
F32 = mybir.dt.float32
F32R = mybir.dt.float32r
BF16 = mybir.dt.bfloat16
I32 = mybir.dt.int32
U32 = mybir.dt.uint32


def layout(widths):
    at, out = 0, {}
    for name, w in widths:
        out[name] = (at, at + w)
        at += w
    return out, at


CONST, NCONST = layout([
    ("ident", P), ("future", P), ("before", P), ("of_seq", B), ("neg_of_head", H0),
    ("of_head", H0), ("quarter_of_head", H0), ("quarter_block", H0 * VW), ("block_start", NT), ("result_row", NT), ("spare_row", NBLK),
    ("not_first", P), ("block_index", NBLK * E0), ("rev8", E0),
    ("query_lo", 1), ("key_lo", 1), ("expert_cols", (FC1 - 1) * P),
])
PARAM, NPARAM = layout([
    ("gwq", 2 * H0), ("gwk", 2 * H0), ("gwv", 2 * H0), ("gate_b", 2), ("ln_scale", D), ("gates", 4),
    ("router0", E0), ("router1", E1), ("e_bias", E1), ("bq", HG), ("bk", HG), ("bv", D),
    ("wv", D), ("wo", D), ("be", EO), ("bo", D),
])


def rd(ap):
    return ap.bitcast(F32R)


class Chain:

    def __init__(self, eng, sem):
        self.eng, self.sem, self.base, self.n, self.turn, self.per = eng, sem, 0, 0, None, 0

    def enter(self, turn, per):
        self.base, self.n, self.turn, self.per = self.base + self.n, 0, turn, per

    def leave(self, turns):
        assert self.n == self.per, (self.n, self.per)
        self.base, self.n, self.turn = self.base + turns * self.per, 0, None

    def value(self):
        return self.base + self.n if self.turn is None else self.turn * self.per + (self.base + self.n)

    def send(self, ins):
        ins.then_inc(self.sem, 1)
        self.n += 1

    def link(self, ins):
        self.send(ins)
        self.eng.wait_ge(self.sem, self.value())


def ge(eng, sem, value):
    if not (isinstance(value, int) and value <= 0):
        eng.wait_ge(sem, value)


def pipelined(eng, n, stages, peel=0, width=4):
    least, most = min(lag for _, lag in stages), max(lag for _, lag in stages)
    first = most + peel

    def turn(k, parity):
        for stage, lag in stages:
            if not isinstance(k, int) or 0 <= k - lag < n:
                stage(k - lag, (parity - lag) % 2)

    passes = (n + least - first) // width
    for k in range(least, first):
        turn(k, k % 2)
    with eng.Fori(0, passes) as it:
        for i in range(width):
            turn(it * width + (first + i), (first + i) % 2)
    for k in range(first + width * passes, n + most):
        turn(k, k % 2)


def loop_pairs(eng, pair):
    with eng.Fori(0, B // 2 - 1) as it:
        pair(it, False)
    pair(B // 2 - 1, True)


def turns(eng, n, ahead, behind, peel, turn):
    first = behind + peel
    passes = (n - ahead - first) // 2
    for k in range(-ahead, first):
        turn(k, k % 2)
    with eng.Fori(0, passes) as it:
        for i in range(2):
            turn(it * 2 + (first + i), (first + i) % 2)
    for k in range(first + 2 * passes, n + behind):
        turn(k, k % 2)


def among(b, n):
    return not isinstance(b, int) or 0 <= b < n


def loads(b, i, units):
    return units * (b // 2 + 1) if isinstance(b, int) else (b - i) * (units // 2) + units


def build(nc, a, scr_x, scr_y, out):
    es = ExitStack()
    with es:
        def sb(name, shape, dt=F32, stack=es):
            return stack.enter_context(nc.sbuf_tensor(name, shape, dt))

        def sem(name):
            return es.enter_context(nc.semaphore(name))

        ps = [es.enter_context(nc.psum_tensor(f"bank{i}", [P, 512], F32)) for i in range(4)]
        pw = [es.enter_context(nc.psum_tensor(f"wide{i}", [P, 1024], F32)) for i in range(2)]

        con = sb("con", [P, NCONST])
        par = sb("par", [P, NPARAM])
        x = sb("x", [P, NT, D])
        xn = sb("xn", [P, NT, D])
        xT = sb("xT", [P, T])
        ctxT = sb("ctxT", [P, T])
        st = sb("st", [P, NT, 6])
        lnw = sb("lnw", [P, 8, NT])
        tg = sb("tg", [P, 4])
        ctS = [sb(f"ctS{i}", [P, S]) for i in range(2)]
        before_bf = sb("before_bf", [P, P], BF16)
        ones_bf = sb("ones_bf", [P, P], BF16)

        def C(name):
            return con[:, CONST[name][0]:CONST[name][1]]

        def A(name):
            return par[:, PARAM[name][0]:PARAM[name][1]]

        ffn = ExitStack()
        wh = sb("w13h", [P, 2 * E0 * F0], F32, ffn)
        wl = sb("w13l", [P, 2 * E0 * F0], F32, ffn)

        ml = ExitStack()
        wst = [sb(f"wst{i}", [P, F0], F32, ml) for i in range(2)]
        zero = sb("zero", [P, D + 2], F32, ml)
        vaug = sb("vaug", [P, NT, H0 * VW], F32, ml)
        num = sb("num", [P, NT, H0 * VW], F32, ml)
        gwc = sb("gwc", [P, 2 * H0], F32, ml)
        lnsg = sb("lnsg", [P, D], F32, ml)
        ident_bf = sb("ident_bf", [P, P], BF16, ml)
        future_bf = sb("future_bf", [P, 4, P], BF16, ml)
        g64 = sb("g64", [BH, 10, S], F32, ml)
        negM = sb("negM", [BH, 2], F32, ml)
        t64 = sb("t64", [BH, 4 * P], F32, ml)
        wT = sb("wT", [P, 4, BH], F32, ml)
        ahl = sb("ahl", [P, 3 * P], F32, ml)
        mhl = sb("mhl", [P, S], F32, ml)
        Rm = sb("Rm", [P, H0, S], F32, ml)
        dlt = sb("dlt", [P, H0, P], F32, ml)
        LS = [sb(f"LS{i}", [P, 3 * P], F32, ml) for i in range(2)]
        Qm = [sb(f"Qm{i}", [P, H0, S], F32, ml) for i in range(2)]
        qS = [sb(f"qS{i}", [P, P], F32, ml) for i in range(2)]
        Ks = [sb(f"Ks{i}", [P, P], F32, ml) for i in range(2)]
        stm = sb("stm", [P, H0 * VW], F32, ml)
        tmp = sb("tmp", [P, H0 * VW], F32, ml)
        Dm = [sb(f"Dm{i}", [P, 1024], F32, ml) for i in range(2)]
        Cm = [sb(f"Cm{i}", [P, 1024], F32, ml) for i in range(2)]
        den = sb("den", [P, NT * H0], F32, ml)
        ml.close()

        mo = ExitStack()
        w2 = sb("w2", [P, E0 * F0], F32, mo)
        rt = sb("rt", [P, 8, NT * E0], F32, mo)
        sm = sb("sm", [P, 8, NT], F32, mo)
        ex = sb("ex", [P, 4, E0], F32, mo)
        cmpb = sb("cmpb", [P, NBLK * E0], F32, mo)
        routed = sb("routed", [P, NT * E0], BF16, mo)
        slot = sb("slot", [P, 2, NT], U32, mo)
        bcol = sb("bcol", [1, 2, NBLK], F32, mo)
        boff = sb("boff", [1, NBLK], I32, mo)
        xg = [sb(f"xg{i}", [P, D], F32, mo) for i in range(2)]
        xgh = [sb(f"xgh{i}", [P, P], F32, mo) for i in range(2)]
        xgl = [sb(f"xgl{i}", [P, P], F32, mo) for i in range(2)]
        sg = [sb(f"sg{i}", [P, F0], F32, mo) for i in range(2)]
        hb = [sb(f"hb{i}", [P, F0], F32, mo) for i in range(2)]
        hT = [sb(f"hT{i}", [P, F0], F32, mo) for i in range(2)]
        yb = [sb(f"yb{i}", [P, D], F32, mo) for i in range(2)]
        xa = [sb(f"xa{i}", [P, NT, D + 2], F32, mo) for i in range(2)]
        dw = sb("dw", [P, NBLK, 2], F32, mo)
        rows = sb("rows", [P, NBLK], U32, mo)
        row = [sb(f"row{i}", [P, 1], U32, mo) for i in range(2)]
        wt = [sb(f"wt{i}", [P, 1], F32, mo) for i in range(2)]
        mo.close()
        ffn.close()

        at3 = ExitStack()
        Kd = [sb(f"Kd{i}", [P, HG, HJ, S], F32, at3) for i in range(2)]
        Qd = sb("Qd", [P, HG, HJ, S], F32, at3)
        vp = [sb(f"vp{i}", [P, CH, H1, ST], F32, at3) for i in range(2)]
        mp = sb("mp", [P, CH, HG, P], F32, at3)
        wqs = sb("wqs", [P, HG * P], F32, at3)
        wks = sb("wks", [P, HG * P], F32, at3)
        we = sb("we", [P, EO, D], F32, at3)
        wem = sb("wem", [P, D], F32, at3)
        bem = sb("bem", [P, 1], F32, at3)
        bemb = sb("bemb", [P, P], F32, at3)
        wc = sb("wc", [P, D], F32, at3)
        cb = sb("cb", [P, D], F32, at3)
        bqs = sb("bqs", [P, HG], F32, at3)
        q32 = sb("q32", [P, HG, S], F32, at3)
        qhi = sb("qhi", [P, HG, S], F32, at3)
        k32 = sb("k32", [P, HG, S], F32, at3)
        khi = sb("khi", [P, HG, S], F32, at3)
        Kn = sb("Kn", [P, HG, S], F32, at3)
        Kst = [sb(f"Kst{i}", [P, HG, S], F32, at3) for i in range(2)]
        Qs = [sb(f"Qs{i}", [P, HG, S], F32, at3) for i in range(2)]
        Q2 = sb("Q2", [P, HG, S], F32, at3)
        mx = sb("mx", [P, CH, H1], F32, at3)
        et3 = [[sb(f"et{i}{c}", [P, HJ, S], F32, at3) for c in range(CH)] for i in range(2)]
        o32 = sb("o32", [P, HG, S], F32, at3)
        rec = sb("rec", [P, CH, H1], F32, at3)
        on = sb("on", [P, CH, D], F32, at3)
        onT = sb("onT", [P, CH, P], F32, at3)
        at3.close()

        m2 = ExitStack()
        graw = sb("graw", [P, 2 * FC1 * P], F32, m2)
        guh = sb("guh", [P, 2 * FC1 * P], F32, m2)
        gul = sb("gul", [P, 2 * FC1 * P], F32, m2)
        dn = sb("dn", [P, FC1, D], F32, m2)
        xTh = sb("xTh", [P, T], F32, m2)
        xTl = sb("xTl", [P, T], F32, m2)
        cT = sb("cT", [P, T], F32, m2)
        ecol = sb("ecol", [P, (FC1 - 1) * P], F32, m2)
        r1 = sb("r1", [P, 3, NT * E1], F32, m2)
        mk = sb("mk", [P, NT, E1 + 8 - K1], F32, m2)
        mrep = sb("mrep", [P, NT, E1 + 8 - K1], F32, m2)
        top8 = sb("top8", [P, NT, 8], F32, m2)
        r4 = sb("r4", [P, 12, NT * NG1], F32, m2)
        s4 = sb("s4", [P, 6, NT], F32, m2)
        chl = sb("chl", [P, NT, 2 * E1], F32, m2)
        sg1 = [sb(f"sgb{i}", [P, TT], F32, m2) for i in range(2)]
        h1 = [sb(f"h1{i}", [P, TT], F32, m2) for i in range(2)]
        hT1 = [sb(f"hTb{i}", [P, FC1, TT], F32, m2) for i in range(2)]
        m2.close()

        s_con = sem("constants_loaded")
        s_par = sem("parameters_loaded")
        s_x = sem("x_loaded")
        s_ctx = sem("ctx_loaded")
        s_va = sem("values_loaded")
        s_v = sem("dve_step")
        s_a = sem("act_step")
        s_xn = sem("xn_ready")
        s_tr = sem("x_transposed_in_psum")
        s_xT = sem("xT_ready")
        s_gps = sem("gates_in_psum")
        s_gT = sem("gates_copied")
        s_g64 = sem("gates_by_head_row")
        s_z = sem("forget_gate_ready")
        s_sp = sem("softplus_ready")
        s_aM = sem("stabilizers_ready")
        s_t64 = sem("decays_ready")
        s_wps = sem("decays_in_psum")
        s_wT = sem("decay_columns_ready")
        s_bc = sem("mlstm_constants_ready")
        s_free = sem("sequence_matmuls_done")
        s_ct = [sem(f"ctx_columns_{i}_loaded") for i in range(2)]
        s_ls = sem("exponent_operand_ready")
        s_qm = sem("head_queries_ready")
        s_qS = sem("chunk_queries_ready")
        s_E = sem("exponent_in_psum")
        s_D = sem("decay_matrix_ready")
        s_S = sem("scores_in_psum")
        s_C = sem("weighted_scores_ready")
        s_ks = sem("decayed_keys_ready")
        s_st = sem("state_in_psum")
        s_stm = sem("state_copied")
        s_I = sem("state_part_in_psum")
        s_It = sem("state_part_scaled")
        s_PV = sem("head_sums_in_psum")
        s_num = sem("head_sums_copied")
        s_w = [sem(f"weights_{i}_loaded") for i in range(2)]
        s_wh = sem("weights_hi_ready")
        s_wl = sem("weights_lo_ready")
        s_tg = sem("gates_tanh_ready")
        s_x1 = sem("x1_ready")
        s_zero = sem("zero_ready")
        s_clr = sem("scratch_cleared")
        s_out = sem("out_stored")
        s_w2 = sem("w2_loaded")
        s_lg = sem("router_logits_in_psum")
        s_lx = sem("router_logits_less_max")
        s_ex = sem("router_exponentials_ready")
        s_ro = sem("routed_ready")
        s_rk = sem("ranks_in_psum")
        s_sl = sem("slots_ready")
        s_be = sem("block_experts_ready")
        s_sc = sem("tokens_scattered")
        s_xg = [sem(f"block_tokens_{i}_loaded") for i in range(2)]
        s_T = sem("block_tokens_in_psum")
        s_xp = sem("block_tokens_split")
        s_G = sem("hidden_gate_in_psum")
        s_U = sem("hidden_up_in_psum")
        s_sg = sem("silu_ready")
        s_hb = sem("hidden_ready")
        s_H = sem("hidden_transposed_in_psum")
        s_hT = sem("hidden_transposed_copied")
        s_Y = sem("block_out_in_psum")
        s_yb = sem("block_out_copied")
        s_ys = [sem(f"block_out_{i}_stored") for i in range(2)]
        s_xa = sem("tokens_copied")
        s_seen = sem("block_out_seen_by_gpsimd")
        s_dw = sem("slot_rows_and_weights_loaded")
        s_rw = sem("block_rows_and_weights_ready")
        s_y2 = [sem(f"results_{t}_loaded") for t in range(4)]
        s_x2 = sem("x2_ready")
        c_w = sem("attention_weights_loaded")
        c_wa = sem("mean_expert_ready")
        c_wp = sem("output_weights_in_psum")
        c_wc = sem("output_weights_ready")
        c_z = sem("attention_zeros_ready")
        c_zk = sem("block_diagonals_zeroed")
        c_ct = [sem(f"attention_ctx_{i}_loaded") for i in range(2)]
        c_K = sem("keys_in_psum")
        c_k32 = sem("keys_copied")
        c_khi = sem("keys_rounded")
        c_qhi = sem("queries_rounded")
        c_rec = sem("row_sums_inverted")
        c_ks = sem("key_stacks_ready")
        c_kd = [sem(f"key_blocks_{i}_placed") for i in range(2)]
        c_kst = [sem(f"key_stacks_{i}_copied") for i in range(2)]
        c_V = sem("values_in_psum")
        c_vp = sem("values_ready")
        c_Q = sem("queries_in_psum")
        c_q32 = sem("queries_copied")
        c_qs = sem("query_stacks_ready")
        c_P1 = sem("scores_for_max_in_psum")
        c_R = sem("max_taken")
        c_mp = sem("max_parts_ready")
        c_MT = sem("max_rows_in_psum")
        c_q2 = sem("queries_with_max_ready")
        c_qd = sem("query_blocks_placed")
        c_P2 = sem("scores_less_max_in_psum")
        c_X = sem("exponentials_ready")
        c_PV = sem("attention_sums_in_psum")
        c_O = sem("attention_sums_copied")
        c_OT = sem("attention_sums_turned")
        c_on = sem("attention_normalized")
        c_nT = sem("attention_turned_in_psum")
        c_nc = sem("attention_turned_copied")
        c_Y = sem("attention_out_in_psum")
        s_x3 = sem("x3_ready")
        d_w = sem("mixture2_weights_loaded")
        d_wh = sem("mixture2_weights_hi_ready")
        d_wl = sem("mixture2_weights_lo_ready")
        d_c = sem("mixture2_constants_ready")
        d_xh = sem("x3_rounded")
        d_xT = sem("x3_parts_ready")
        d_lg = sem("router2_logits_in_psum")
        d_sg = sem("router2_exponentials_ready")
        d_cm = sem("combine_weights_ready")
        d_cT = sem("combine_rows_in_psum")
        d_cc = sem("combine_rows_ready")
        d_G = sem("mixture2_gate_in_psum")
        d_U = sem("mixture2_up_in_psum")
        d_sl = sem("mixture2_silu_ready")
        d_h1 = sem("mixture2_hidden_ready")
        d_h = sem("mixture2_weighted_hidden_ready")
        d_Y = sem("mixture2_out_in_psum")
        d_x4 = sem("x4_ready")

        wide = [pw[i // 2][:, i % 2 * 512:(i % 2 + 1) * 512] for i in range(4)]
        block = es.enter_context(nc.Block())

        @block.sync
        def _(sp):
            sp.dma_start(x[:], a["x_nat"].rearrange("p (t d) -> p t d", d=D)).then_inc(s_x, 16)
            sp.dma_start(con[:], a["const"]).then_inc(s_con, 16)
            sp.dma_start(par[:], a["param"]).then_inc(s_par, 16)
            sp.dma_start(ctxT[:], a["ctxT"]).then_inc(s_ctx, 16)
            sp.dma_start(vaug[:], a["vaug"].rearrange("p (t d) -> p t d", d=H0 * VW)).then_inc(s_va, 16)
            sp.wait_ge(s_zero, 1)
            sp.dma_start(scr_x.rearrange("(r p) d -> p r d", p=P),
                         zero[:].unsqueeze(1).broadcast_to([P, NBLK, D + 2])).then_inc(s_clr, 16)
            for b in range(B):
                sp.wait_ge(s_gT, b // 2 + 1)
                for k in range(2):
                    sp.dma_start(g64[b * H0:(b + 1) * H0, k, :],
                                 xn_gates(xn)[k * H0:(k + 1) * H0, b * S:(b + 1) * S]).then_inc(s_g64, 16)
            with sp.Fori(0, B // 2) as it:
                for i in range(2):
                    sp.wait_ge(s_free, it * 2 + (i + 1))
                    sp.dma_start(ctS[i][:], a["ctxT"][:, bass.ds((it * 2 + i) * S, S)]).then_inc(s_ct[i], 16)
                    for u in (2 * i, 2 * i + 1):
                        sp.wait_ge(s_wl, it * 4 + (u + 1))
                        sp.dma_start(wst[u % 2][:], a["w13"][:, bass.ds((it * 4 + u) * F0, F0)])\
                            .then_inc(s_w[u % 2], 16)
            sp.wait_ge(s_x1, 1)
            sp.wait_ge(s_wl, 2 + 2 * E0)
            sp.wait_ge(s_clr, 16)
            sp.dma_start(w2[:], a["w2"]).then_inc(s_w2, 16)
            sp.wait_ge(s_sc, 16 * 2 * NT)

            def load_block(j, i):
                ge(sp, s_T, j - 1)
                sp.dma_start(xg[i][:], scr_x[bass.ds(j * P, P), 0:D]).then_inc(s_xg[i], 16)
                if isinstance(j, int) and j == 1:
                    sp.dma_start(dw[:], scr_x[:, D:D + 2].rearrange("(j p) w -> p j w", p=P)).then_inc(s_dw, 16)

            pipelined(sp, NBLK, [(load_block, 0)], peel=2)
            sp.wait_ge(s_yb, NBLK)
            for dst, name in ((wqs, "wqs"), (wks, "wks")):
                sp.dma_start(dst[:], a[name]).then_inc(c_w, 16)
            sp.dma_start(we[:], a["we"].rearrange("p (e d) -> p e d", d=D)).then_inc(c_w, 16)
            for i in range(2):
                sp.wait_ge(s_ys[i], 16 * (NBLK // 2))
            for q in range(4):
                for k in range(2):
                    at = slice(1 + k * T + q * 4 * P, 1 + k * T + (q + 1) * 4 * P)
                    sp.dma_start(xa[k][:, 4 * q:4 * q + 4, 0:D], scr_y[at, :].rearrange("(t p) d -> p t d", p=P))\
                        .then_inc(s_y2[q], 16)

            sp.wait_ge(c_zk, 3)

            def place(k, i):
                if among(k + 1, B):
                    ge(sp, c_V, k)
                    sp.dma_start(ctS[1 - i][:], a["ctxT"][:, bass.ds((k + 1) * S, S)]).then_inc(c_ct[1 - i], 16)
                    sp.wait_ge(c_ks, k + 2)
                    for j in range(HJ):
                        rows = slice(j * ST, (j + 1) * ST)
                        sp.dma_start(Kd[1 - i][rows, :, j, :], Kn[rows, :, :]).then_inc(c_kd[1 - i], 16)
                ge(sp, c_P2, k * NU)
                if among(k + 1, B):
                    sp.dma_start(Kst[1 - i][:], Kn[:]).then_inc(c_kst[1 - i], 16)
                if among(k, B):
                    sp.wait_ge(c_q2, k * 2 + 2)
                    for j in range(HJ):
                        rows = slice(j * ST, (j + 1) * ST)
                        sp.dma_start(Qd[rows, :, j, :], Q2[rows, :, :]).then_inc(c_qd, 16)

            turns(sp, B, 1, 0, 2, place)
            sp.wait_ge(s_x3, B)

            sp.dma_start(graw[:], a["gu"]).then_inc(d_w, 16)
            sp.dma_start(dn[:], a["down"].rearrange("p (c d) -> p c d", d=D)).then_inc(d_w, 16)
            o4 = out.rearrange("p (t d) -> p t d", d=D)
            for t in range(T // TT):
                sp.wait_ge(d_x4, t + 1)
                k = TT // P
                sp.dma_start(o4[:, t * k:(t + 1) * k, :], x[:, t * k:(t + 1) * k, :]).then_inc(s_out, 16)
            sp.wait_ge(s_out, 16 * (T // TT))

        def ln_stats(dve, v, src, tiles=range(NT), eps=LN_EPS):
            for t in tiles:
                dve.bn_stats(st[:, t, :], src[:, t, :]).then_inc(v.sem, 1)
            v.n += len(tiles)
            dve.wait_ge(v.sem, v.value())
            w = lambda r: lnw[:, r, tiles[0]:tiles[-1] + 1]
            b = lambda r: st[:, tiles[0]:tiles[-1] + 1, r]
            v.send(dve.tensor_tensor(w(0), b(1), b(4), ALU.add))
            v.send(dve.tensor_tensor(w(1), b(1), b(4), ALU.subtract))
            v.link(dve.tensor_tensor(w(2), b(2), b(5), ALU.add))
            v.send(dve.tensor_scalar(w(0), w(0), 0.5, None, ALU.mult))
            v.send(dve.tensor_tensor(w(1), w(1), w(1), ALU.mult))
            v.link(dve.tensor_scalar(w(2), w(2), 1.0 / D, eps, ALU.mult, ALU.add))
            v.link(dve.scalar_tensor_tensor(out=w(3), in0=w(1), scalar=0.25, in1=w(2), op0=ALU.mult, op1=ALU.add))
            inverse_root(dve, v, w(6), w(3), w(5), w(4))

        def inverse_root(dve, v, y, var, half, t):
            v.send(dve.tensor_scalar(half, var, -0.5, None, ALU.mult))
            v.link(dve.tensor_scalar(t.bitcast(I32), var.bitcast(I32), 1, None, ALU.arith_shift_right))
            v.link(dve.tensor_scalar(y.bitcast(I32), t.bitcast(I32), -1, ROOT_GUESS, ALU.mult, ALU.add))
            for _ in range(3):
                v.link(dve.tensor_tensor(t, y, y, ALU.mult))
                v.link(dve.tensor_tensor(t, t, half, ALU.mult))
                v.link(dve.scalar_tensor_tensor(out=y, in0=t, scalar=1.5, in1=y, op0=ALU.add, op1=ALU.mult))

        def ln_apply(dve, dst, src, sem, tiles=range(NT)):
            for t in tiles:
                dve.tensor_scalar(dst[:, t, :], src[:, t, :], lnw[:, 0, t:t + 1], lnw[:, 6, t:t + 1],
                                  ALU.subtract, ALU.mult).then_inc(sem, 1)

        def pick(dve, v, val, eq, sel, top, first, rev, m, n):
            wide = lambda t: t.unsqueeze(2).broadcast_to([P, m, n])
            v.link(dve.tensor_reduce(top, val, AX.X, ALU.max))
            v.link(dve.tensor_tensor(eq, val, wide(top), ALU.is_equal))
            v.link(dve.tensor_tensor(eq, eq, rev.unsqueeze(1).broadcast_to([P, m, n]), ALU.mult))
            v.link(dve.tensor_reduce(first, eq, AX.X, ALU.max))
            v.link(dve.tensor_tensor(sel, eq, wide(first), ALU.is_equal))
            v.link(dve.scalar_tensor_tensor(out=val, in0=sel, scalar=NEG, in1=val, op0=ALU.mult, op1=ALU.add))

        @block.vector
        def _(dve):
            v = Chain(dve, s_v)
            dve.memset(zero[:], 0.0).then_inc(s_zero, 1)
            dve.wait_ge(s_x, 16)
            ln_stats(dve, v, x)
            ln_apply(dve, xn, x, s_xn)
            dve.wait_ge(s_con, 16)
            dve.wait_ge(s_par, 16)
            dve.tensor_copy(ident_bf[:], C("ident")).then_inc(s_bc, 1)
            dve.tensor_copy(future_bf[:], C("future").unsqueeze(1).broadcast_to([P, 4, P])).then_inc(s_bc, 1)
            dve.tensor_copy(rd(dlt[:]), C("of_head").unsqueeze(2).broadcast_to([P, H0, P])).then_inc(s_bc, 1)
            dve.tensor_copy(before_bf[:], C("before")).then_inc(s_bc, 1)
            dve.memset(ones_bf[:], 1.0).then_inc(s_bc, 1)
            dve.memset(ahl[:, 2 * P:], 1.0).then_inc(s_bc, 1)
            dve.tensor_tensor(gwc[:], A("gwk"), A("gwv"), ALU.add).then_inc(s_bc, 1)
            dve.wait_ge(s_tg, 1)
            dve.tensor_scalar(lnsg[:], A("ln_scale"), tg[:, 0:1], None, ALU.mult).then_inc(s_bc, 1)
            dve.wait_ge(s_bc, 8)
            for i in range(4):
                dve.wait_ge(s_tr, i + 1)
                dve.tensor_copy(xT[:, bass.ts(i, 512)], ps[i][:]).then_inc(s_xT, 1)

            IG, FG, AZ, EZ, L, LF, CS, AA, MM, ONE = range(10)
            g = lambda i: g64[:, i, :]
            dve.memset(g(ONE), 1.0).then_inc(s_v, 1)
            v.n += 1
            dve.wait_ge(s_g64, 16 * 2 * B)
            dve.tensor_scalar(g(FG), g(FG), par[0:BH, PARAM["gate_b"][0] + 1:PARAM["gate_b"][1]], None,
                              ALU.add).then_inc(s_z, 1)
            dve.wait_ge(s_z, 1)
            v.link(dve.tensor_scalar(g(LF), g(FG), 0.0, None, ALU.min))
            dve.wait_ge(s_sp, 1)
            v.link(dve.tensor_tensor(g(LF), g(LF), g(L), ALU.subtract))
            v.link(dve.tensor_tensor_scan(g(CS), g(ONE), g(LF), 0.0, ALU.mult, ALU.add))
            v.link(dve.scalar_tensor_tensor(out=g(AA), in0=g(IG), scalar=par[0:BH, PARAM["gate_b"][0]:PARAM["gate_b"][0] + 1],
                                            in1=g(CS), op0=ALU.add, op1=ALU.subtract))
            v.link(dve.tensor_tensor_scan(g(MM), g(ONE), g(AA), LOWEST, ALU.mult, ALU.max))
            v.link(dve.tensor_scalar(negM[:, 0:1], g64[:, MM, P - 1:P], -1.0, None, ALU.mult))
            dve.tensor_tensor(g(CS), g(CS), g(MM), ALU.add).then_inc(s_aM, 1)
            v.send(dve.tensor_copy(rd(ahl[0:BH, 0:S]), g(AA)))
            v.link(dve.tensor_copy(rd(mhl[0:BH, :]), g(MM)))
            v.send(dve.tensor_tensor(rd(ahl[BH:P, 0:S]), g(AA), ahl[0:BH, 0:S], ALU.subtract))
            v.link(dve.tensor_tensor(rd(mhl[BH:P, :]), g(MM), mhl[0:BH, :], ALU.subtract))
            dve.tensor_tensor(rd(Rm[:]), mhl[:].unsqueeze(1).broadcast_to([P, H0, S]),
                              C("neg_of_head").unsqueeze(2).broadcast_to([P, H0, S]), ALU.mult).then_inc(s_bc, 1)
            dve.wait_ge(s_wps, 4)
            dve.tensor_copy(wT[:], ps[0][:, 0:4 * BH].rearrange("p (c r) -> p c r", r=BH)).then_inc(s_wT, 1)
            dve.wait_ge(s_wT, 1)
            dve.wait_ge(s_va, 16)

            vh = lambda t: t.rearrange("p (h w) -> p h w", w=VW)

            def prepare(it, i):
                b = it * 2 + i
                dve.wait_ge(s_free, it * 2 + (i + 1))
                dve.tensor_scalar(rd(LS[i][:]), ahl[:], con[:, bass.ds(CONST["of_seq"][0] + b, 1)], None,
                                  ALU.mult).then_inc(s_ls, 1)
                dve.tensor_tensor(Ks[i][:].rearrange("p (h d) -> p h d", d=DH0),
                                  vh(vaug[:, b * CH, :])[:, :, 0:DH0],
                                  wT[:, 0, bass.ds(b * H0, H0)].unsqueeze(2).broadcast_to([P, H0, DH0]),
                                  ALU.mult).then_inc(s_ks, 1)

            def pair(it, last):
                for u in range(4):
                    i, c = u // 2, u % 2
                    b = it * 2 + i
                    dve.wait_ge(s_S, it * 4 + (u + 1))
                    dve.wait_ge(s_D, it * 4 + (u + 1))
                    dve.wait_ge(s_PV, it * 4 + (u + 1))
                    dve.tensor_tensor(Cm[u % 2][:], pw[1][:], Dm[u % 2][:], ALU.mult).then_inc(s_C, 1)
                    if c == 0:
                        dve.wait_ge(s_st, it * 2 + (i + 1))
                        dve.tensor_tensor(stm[:], ps[1][:, 0:H0 * VW], C("quarter_block"), ALU.mult).then_inc(s_stm, 1)
                        dve.wait_ge(s_PV, it * 4 + (u + 3))
                        dve.tensor_copy(num[:, b * CH, :], ps[0][:, 0:H0 * VW]).then_inc(s_num, 1)
                    else:
                        dve.wait_ge(s_I, it * 2 + (i + 1))
                        dve.tensor_tensor(vh(tmp[:]), vh(ps[1][:, 256:256 + H0 * VW]),
                                          wT[:, 1, bass.ds(b * H0, H0)].unsqueeze(2).broadcast_to([P, H0, VW]),
                                          ALU.mult).then_inc(s_It, 1)
                        dve.wait_ge(s_It, it * 2 + (i + 2))
                        dve.wait_ge(s_PV, it * 4 + (u + 3))
                        dve.tensor_tensor(num[:, b * CH + 1, :], tmp[:], ps[0][:, 0:H0 * VW], ALU.add).then_inc(s_num, 1)
                        if not last:
                            prepare(it + 1, i)

            for i in range(2):
                prepare(0, i)
            loop_pairs(dve, pair)
            dve.wait_ge(s_num, NT + 1)

            n4 = num[:].rearrange("p t (h w) -> p (t h) w", w=VW)
            th = lambda t: t.rearrange("p (b c h) -> p b c h", c=CH, h=H0)
            v.link(dve.tensor_scalar(den[:], n4[:, :, DH0], -1.0, None, ALU.mult))
            v.link(dve.tensor_tensor(den[:], den[:], n4[:, :, DH0], ALU.max))
            v.link(dve.tensor_tensor(th(den[:]), th(den[:]), wT[:, 2:4, :].rearrange("p c (b h) -> p b c h", h=H0), ALU.max))
            v.link(dve.tensor_scalar(den[:], den[:], NORM_EPS, None, ALU.add))
            v.link(dve.reciprocal(den[:], den[:]))
            v.link(dve.tensor_tensor(xn[:].rearrange("p t (h d) -> p (t h) d", d=DH0), n4[:, :, 0:DH0],
                                     den[:].unsqueeze(2).broadcast_to([P, NT * H0, DH0]), ALU.mult))
            ln_stats(dve, v, xn)
            ln_apply(dve, xn, xn, s_v)
            v.n += NT
            dve.wait_ge(s_v, v.value())
            v.link(dve.tensor_tensor(xn[:], xn[:], lnsg[:].unsqueeze(1).broadcast_to([P, NT, D]), ALU.mult))
            dve.tensor_tensor(x[:], x[:], xn[:], ALU.add).then_inc(s_x1, 1)
            dve.wait_ge(s_x1, 1)

            dve.wait_ge(s_wl, 2 + 2 * E0)
            dve.wait_ge(s_clr, 16)
            ln_stats(dve, v, x)
            ln_apply(dve, xn, x, s_xn)
            te = lambda t: t.rearrange("p (t e) -> p t e", e=E0)
            tile1 = lambda t: t.unsqueeze(2).broadcast_to([P, NT, E0])
            pr, eq, s1, s2, tc, inc, pos, one = (rt[:, i, :] for i in range(8))
            dve.memset(one, 1.0).then_inc(s_v, 1)
            v.n += 1
            dve.wait_ge(s_lg, 1)
            lg = pw[0][:, 0:NT * E0]
            v.link(dve.tensor_reduce(sm[:, 0, :], te(lg), AX.X, ALU.max))
            dve.tensor_tensor(te(pr), te(lg), tile1(sm[:, 0, :]), ALU.subtract).then_inc(s_lx, 1)
            dve.wait_ge(s_ex, 1)
            v.link(dve.tensor_reduce(sm[:, 0, :], te(eq), AX.X, ALU.add))
            v.link(dve.reciprocal(sm[:, 1, :], sm[:, 0, :]))
            v.link(dve.tensor_tensor(te(pr), te(eq), tile1(sm[:, 1, :]), ALU.mult))
            pick(dve, v, te(pr), te(eq), te(s1), sm[:, 2, :], sm[:, 4, :], C("rev8"), NT, E0)
            pick(dve, v, te(pr), te(eq), te(s2), sm[:, 3, :], sm[:, 4, :], C("rev8"), NT, E0)
            dve.tensor_tensor(routed[:], s1, s2, ALU.add).then_inc(s_ro, 1)
            v.link(dve.tensor_tensor(sm[:, 4, :], sm[:, 2, :], sm[:, 3, :], ALU.add))
            v.link(dve.reciprocal(sm[:, 5, :], sm[:, 4, :]))
            v.link(dve.tensor_scalar(sm[:, 5, :], sm[:, 5, :], tg[:, 1:2], None, ALU.mult))
            for k in range(2):
                v.send(dve.tensor_tensor(xa[k][:, :, D + 1], sm[:, 2 + k, :], sm[:, 5, :], ALU.mult))
                v.send(dve.tensor_scalar(xa[k][:, :, D], C("result_row"), float(k * T), None, ALU.add))
            et = lambda t: t.rearrange("p (e t) -> p e t", t=NT)
            dve.wait_ge(s_rk, 1)
            v.link(dve.tensor_copy(et(tc), ps[0][:, P:2 * P].rearrange("p (t e) -> p e t", e=E0)))
            v.link(dve.tensor_tensor_scan(inc, C("not_first"), tc, 0.0, ALU.mult, ALU.add))
            v.link(dve.tensor_tensor(et(pos), et(inc)[:, :, NT - 1].unsqueeze(2).broadcast_to([P, E0, NT]),
                                     C("block_start").unsqueeze(1).broadcast_to([P, E0, NT]), ALU.is_gt))
            v.link(dve.tensor_reduce(ex[:, 0, :], et(pos), AX.X, ALU.add))
            v.link(dve.tensor_tensor_scan(ex[:, 1, :], one[:, 0:E0], ex[:, 0, :], 0.0, ALU.mult, ALU.add))
            v.link(dve.tensor_tensor(ex[:, 2, :], ex[:, 1, :], ex[:, 0, :], ALU.subtract))
            v.link(dve.tensor_scalar(ex[:, 2, :], ex[:, 2, :], float(P), None, ALU.mult))
            v.link(dve.tensor_tensor(inc, inc, tc, ALU.subtract))
            v.link(dve.tensor_tensor(et(inc), et(inc), ex[:, 2, :].unsqueeze(2).broadcast_to([P, E0, NT]), ALU.add))
            v.link(dve.tensor_tensor(te(pos), te(ps[0][:, 0:P]), inc.rearrange("p (e t) -> p t e", t=NT), ALU.add))
            v.send(dve.tensor_tensor(eq, s1, pos, ALU.mult))
            v.link(dve.tensor_tensor(s2, s2, pos, ALU.mult))
            for k, s in enumerate((eq, s2)):
                v.link(dve.tensor_reduce(sm[:, 6 + k, :], te(s), AX.X, ALU.add))
                dve.tensor_copy(slot[:, k, :], sm[:, 6 + k, :]).then_inc(s_sl, 1)
            b3 = lambda t: t.rearrange("p (j e) -> p j e", e=E0)
            v.link(dve.tensor_tensor(b3(cmpb[0:1, :]), b3(C("block_index")[0:1, :]),
                                     ex[0:1, 1, :].unsqueeze(1).broadcast_to([1, NBLK, E0]), ALU.is_ge))
            v.link(dve.tensor_reduce(bcol[:, 0, :], b3(cmpb[0:1, :]), AX.X, ALU.add))
            v.link(dve.tensor_scalar(bcol[:, 1, :], bcol[:, 0, :], float(E0 - 1), float(F0), ALU.min, ALU.mult))
            dve.tensor_copy(boff[:], bcol[:, 1, :]).then_inc(s_be, 1)

            def split_tokens(j, i):
                dve.wait_ge(s_T, j + 1)
                ge(dve, s_U, j - 1)
                dve.tensor_copy(rd(xgh[i][:]), ps[0][:, 0:P]).then_inc(s_xp, 1)
                dve.wait_ge(s_xp, j * 2 + 1)
                dve.tensor_tensor(rd(xgl[i][:]), ps[0][:, 0:P], xgh[i][:], ALU.subtract).then_inc(s_xp, 1)

            def hidden(j, i):
                dve.wait_ge(s_U, j + 1)
                dve.wait_ge(s_sg, j + 1)
                ge(dve, s_H, j - 1)
                dve.tensor_tensor(hb[i][:], sg[i][:], pw[1][:, i * F0:(i + 1) * F0], ALU.mult).then_inc(s_hb, 1)

            def result_rows():
                dve.wait_ge(s_dw, 16)
                v.link(dve.tensor_scalar(cmpb[:, 0:NBLK], dw[:, :, 0], 0.0, None, ALU.is_equal))
                v.link(dve.tensor_tensor(cmpb[:, 0:NBLK], cmpb[:, 0:NBLK], C("spare_row"), ALU.mult))
                v.link(dve.tensor_tensor(rows[:], dw[:, :, 0], cmpb[:, 0:NBLK], ALU.add))

            def block_out(j, i):
                if isinstance(j, int) and j == 0:
                    result_rows()
                dve.wait_ge(s_Y, j + 1)
                if isinstance(j, int):
                    ge(dve, s_ys[i], 16 * (j // 2))
                else:
                    dve.wait_ge(s_ys[i], (j - i) * 8)
                dve.tensor_copy(row[i][:], rows[:, bass.ds(j, 1)])
                dve.tensor_copy(wt[i][:], dw[:, bass.ds(j, 1), 1]).then_inc(s_rw, 1)
                dve.wait_ge(s_rw, j + 1)
                dve.tensor_scalar(yb[i][:], ps[3][:, 0:P], wt[i][:], None, ALU.mult).then_inc(s_yb, 1)

            pipelined(dve, NBLK, [(split_tokens, -1), (hidden, 0), (block_out, 2)], peel=2)
            def prepare_attention():
                for i in range(2):
                    dve.memset(vp[i][:], 0.0).then_inc(c_z, 1)
                dve.memset(mp[:], 0.0).then_inc(c_z, 1)
                dve.wait_ge(c_z, 3)
                for i in range(2):
                    dve.memset(vp[i][:, :, :, DH1:DH1 + 1], 1.0).then_inc(c_z, 1)
                dve.wait_ge(c_z, 5)
                v.link(dve.tensor_scalar(bqs[:], A("bq"), float(DH1) ** -0.5, None, ALU.mult))
                dve.wait_ge(c_w, 48)
                v.link(dve.tensor_reduce(wem[:], we[:].rearrange("p e d -> p d e"), AX.X, ALU.add))
                v.link(dve.tensor_scalar(wem[:], wem[:], tg[:, 2:3], 1.0 / EO, ALU.mult, ALU.mult))
                v.link(dve.tensor_reduce(bem[:], A("be"), AX.X, ALU.add))
                v.link(dve.tensor_scalar(bem[:], bem[:], tg[:, 2:3], 1.0 / EO, ALU.mult, ALU.mult))
                dve.tensor_copy(bemb[:], bem[:, 0:1].broadcast_to([P, P])).then_inc(c_wa, 1)
                dve.wait_ge(c_wp, 1)
                dve.tensor_copy(wc[:], ps[0][:, 0:P]).then_inc(c_wc, 1)
                dve.scalar_tensor_tensor(out=cb[:], in0=A("bo"), scalar=tg[:, 2:3], in1=ps[0][:, P:2 * P],
                                         op0=ALU.mult, op1=ALU.add).then_inc(c_wc, 1)
                dve.wait_ge(c_wc, 2)
            prepare_attention()
            for q in range(4):
                t4 = slice(4 * q, 4 * q + 4)
                dve.wait_ge(s_y2[q], 32)
                v.link(dve.tensor_tensor(x[:, t4, :], x[:, t4, :], xa[0][:, t4, 0:D], ALU.add))
                dve.tensor_tensor(x[:, t4, :], x[:, t4, :], xa[1][:, t4, 0:D], ALU.add).then_inc(s_x2, 1)
            dve.wait_ge(s_x2, 4)

            ln_stats(dve, v, x)
            ln_apply(dve, xn, x, s_xn)
            dve.wait_ge(s_xn, 3 * NT)
            v.link(dve.tensor_tensor(x[:], x[:], cb[:].unsqueeze(1).broadcast_to([P, NT, D]), ALU.add))

            def take_max(b, n):
                c, g, half = n // 8, n // 2 % 4, n % 2
                dve.wait_ge(c_P1, b * NU + (n + 1))
                h = g * HJ + half * 2
                dve.tensor_reduce(mx[:, c, h:h + 2], pw[0][:, half * 512:(half + 1) * 512]
                                  .rearrange("p (j t) -> p j t", t=S), AX.X, ALU.max).then_inc(c_R, 1)

            def split_max(b):
                dve.wait_ge(c_R, b * NU + NU)
                ge(dve, c_MT, b)
                col = lambda k: mp[:].rearrange("p c g (j r) -> p c (g j) r", r=ST)[:, :, :, SM + k]
                dve.tensor_scalar(rd(col(0)), mx[:], -1.0, None, ALU.mult).then_inc(c_mp, 1)
                dve.wait_ge(c_mp, b * 2 + 1)
                dve.scalar_tensor_tensor(out=rd(col(1)), in0=mx[:], scalar=-1.0, in1=col(0),
                                         op0=ALU.mult, op1=ALU.subtract).then_inc(c_mp, 1)

            def add_values(b, i):
                dve.wait_ge(c_V, b + 1)
                ge(dve, c_PV, (b - 1) * HG)
                dve.tensor_tensor(vp[i][:, :, :, 0:DH1],
                                  ps[0][:, 0:CH * D].rearrange("p (c h d) -> p c h d", h=H1, d=DH1),
                                  A("bv").rearrange("p (h d) -> p h d", d=DH1).unsqueeze(1).broadcast_to([P, CH, H1, DH1]),
                                  ALU.add).then_inc(c_vp, 1)

            def add_max(b, i):
                dve.wait_ge(c_MT, b + 1)
                dve.wait_ge(c_qs, b + 1)
                ge(dve, c_qd, b * 64)
                for k in range(2):
                    dve.tensor_tensor(rd(Q2[:, 2 * k:2 * k + 2, :]), Qs[i][:, 2 * k:2 * k + 2, :],
                                      ps[k][:].rearrange("p (g s) -> p g s", s=S), ALU.add).then_inc(c_q2, 1)

            def normalize(b, i):
                dve.wait_ge(c_OT, b + 1)
                for c in range(CH):
                    o = ps[2 + c][:].rearrange("p (h r) -> p h r", r=ST)
                    dve.reciprocal(rec[:, c, :], o[:, :, DH1]).then_inc(c_rec, 1)
                dve.wait_ge(c_rec, b * 2 + 2)
                ge(dve, c_nT, b)
                for c in range(CH):
                    o = ps[2 + c][:].rearrange("p (h r) -> p h r", r=ST)
                    dve.tensor_tensor(on[:, c, :].rearrange("p (h d) -> p h d", d=DH1), o[:, :, 0:DH1],
                                      rec[:, c, :].unsqueeze(2).broadcast_to([P, H1, DH1]), ALU.mult).then_inc(c_on, 1)

            def residual3(b, i):
                dve.wait_ge(c_Y, b + 1)
                dve.tensor_tensor(x[:, bass.ds(b * CH, CH), :], x[:, bass.ds(b * CH, CH), :],
                                  ps[3][:, 0:CH * D].rearrange("p (c d) -> p c d", d=D), ALU.add).then_inc(s_x3, 1)

            def attend(k, i):
                for n in range(NU):
                    if among(k, B):
                        take_max(k, n)
                    if n == 3 and among(k - 2, B):
                        normalize(k - 2, i)
                    if n == 3 and isinstance(k, int) and k == B:
                        ln_stats(dve, v, x, range(12))
                        ln_apply(dve, xn, x, s_xn, range(12))
                    if n == 8 and among(k - 2, B):
                        residual3(k - 2, i)
                    if n == 13 and among(k, B):
                        add_values(k, i)
                if among(k, B):
                    split_max(k)
                    add_max(k, i)

            turns(dve, B, 1, 2, 1, attend)
            dve.wait_ge(s_x3, B)

            ln_stats(dve, v, x, range(12, NT))
            ln_apply(dve, xn, x, s_xn, range(12, NT))
            dve.memset(cT[:], 0.0).then_inc(d_c, 1)
            dve.tensor_copy(rd(ecol[:]), C("expert_cols")).then_inc(d_c, 1)
            SC, SB, ACC = (r1[:, i, :] for i in range(3))
            v.link(dve.memset(mk[:, :, E1:], -LOWEST))
            te = lambda t: t.rearrange("p (t e) -> p t e", e=E1)
            dve.wait_ge(d_sg, 1)
            v.link(dve.tensor_scalar(SC, SC, 1.0, None, ALU.add))
            v.link(dve.reciprocal(SC, SC))
            v.link(dve.tensor_tensor(te(SB), te(SC), A("e_bias").unsqueeze(1).broadcast_to([P, NT, E1]), ALU.add))
            q3 = SB.rearrange("p (m k) -> p m k", k=NG1)
            q4 = SB.rearrange("p (t g k) -> p t g k", g=NG1, k=NG1)
            W = [r4[:, i, :] for i in range(12)]
            v.send(dve.tensor_tensor(W[0], q3[:, :, 0], q3[:, :, 1], ALU.max))
            v.send(dve.tensor_tensor(W[1], q3[:, :, 0], q3[:, :, 1], ALU.min))
            v.send(dve.tensor_tensor(W[2], q3[:, :, 2], q3[:, :, 3], ALU.max))
            v.link(dve.tensor_tensor(W[3], q3[:, :, 2], q3[:, :, 3], ALU.min))
            v.send(dve.tensor_tensor(W[4], W[0], W[2], ALU.max))
            v.send(dve.tensor_tensor(W[5], W[0], W[2], ALU.min))
            v.link(dve.tensor_tensor(W[6], W[1], W[3], ALU.max))
            v.link(dve.tensor_tensor(W[5], W[5], W[6], ALU.max))
            v.link(dve.tensor_tensor(W[4], W[4], W[5], ALU.add))
            g3 = lambda t: t.rearrange("p (t g) -> p t g", g=NG1)
            rev4 = C("rev8")[:, E0 - NG1:]
            pick(dve, v, g3(W[4]), g3(W[7]), g3(W[8]), s4[:, 0, :], s4[:, 1, :], rev4, NT, NG1)
            pick(dve, v, g3(W[4]), g3(W[7]), g3(W[9]), s4[:, 0, :], s4[:, 1, :], rev4, NT, NG1)
            v.link(dve.tensor_tensor(W[8], W[8], W[9], ALU.add))
            v.link(dve.tensor_tensor(mk[:, :, 0:E1].rearrange("p t (g k) -> p t g k", k=NG1), q4,
                                     g3(W[8]).unsqueeze(3).broadcast_to([P, NT, NG1, NG1]), ALU.mult))
            for t in range(NT):
                dve.max(top8[:, t, :], mk[:, t, 0:E1]).then_inc(s_v, 1)
            v.n += NT
            dve.wait_ge(s_v, v.value())
            v.link(dve.memset(top8[:, :, K1:], -LOWEST))
            for t in range(NT):
                dve.match_replace(mrep[:, t, :], top8[:, t, :], mk[:, t, :], LOWEST).then_inc(s_v, 1)
            v.n += NT
            dve.wait_ge(s_v, v.value())
            v.link(dve.tensor_tensor(te(ACC), mk[:, :, 0:E1], mrep[:, :, 0:E1], ALU.not_equal))
            v.link(dve.tensor_tensor(ACC, ACC, SC, ALU.mult))
            v.link(dve.tensor_reduce(s4[:, 2, :], te(ACC), AX.X, ALU.add))
            v.link(dve.tensor_scalar(s4[:, 2, :], s4[:, 2, :], 1e-20, None, ALU.add))
            v.link(dve.reciprocal(s4[:, 3, :], s4[:, 2, :]))
            v.link(dve.tensor_scalar(s4[:, 3, :], s4[:, 3, :], SHARE1, None, ALU.mult))
            v.link(dve.tensor_tensor(te(ACC), te(ACC), s4[:, 3, :].unsqueeze(2).broadcast_to([P, NT, E1]), ALU.mult))
            v.link(dve.tensor_copy(rd(chl[:, :, 0:E1]), te(ACC)))
            dve.tensor_tensor(rd(chl[:, :, E1:]), te(ACC), chl[:, :, 0:E1], ALU.subtract).then_inc(d_cm, 1)
            for i in range(4):
                dve.wait_ge(d_cT, i + 1)
                dve.tensor_copy(rd(cT[0:2 * E1, i * 512:(i + 1) * 512]), ps[i][0:2 * E1, :]).then_inc(d_cc, 1)

            with dve.Fori(0, T // TT // 2) as it:
                for k in range(2):
                    for c in range(FC1):
                        n = k * FC1 + c
                        dve.wait_ge(d_U, it * (2 * FC1) + (n + 1))
                        dve.wait_ge(d_sl, it * (2 * FC1) + (n + 1))
                        if c == 0:
                            dve.wait_ge(d_Y, it * 2 + (k + 1))
                        if c == FC1 - 1:
                            dve.tensor_tensor(hT1[k][:, c, :], sg1[n % 2][:], pw[1][:, n % 2 * TT:(n % 2 + 1) * TT],
                                              ALU.mult).then_inc(d_h1, 1)
                            dve.wait_ge(d_h1, it * (2 * FC1) + (n + 3))
                            continue
                        dve.tensor_tensor(h1[n % 2][:], sg1[n % 2][:], pw[1][:, n % 2 * TT:(n % 2 + 1) * TT],
                                          ALU.mult).then_inc(d_h1, 1)
                        dve.wait_ge(d_h1, it * (2 * FC1) + (n + 3))
                        dve.tensor_tensor(hT1[k][:, c, :], h1[n % 2][:], ps[c % 2][:], ALU.mult).then_inc(d_h, 1)
                    dve.wait_ge(d_Y, it * 2 + (k + 3))
                    at = bass.ds((it * 2 + k) * (TT // P), TT // P)
                    dve.scalar_tensor_tensor(out=x[:, at, :], in0=ps[2 + k][:].rearrange("p (t d) -> p t d", d=D),
                                             scalar=tg[:, 3:4], in1=x[:, at, :], op0=ALU.mult, op1=ALU.add)\
                        .then_inc(d_x4, 1)

        @block.scalar
        def _(act):
            ch = Chain(act, s_a)
            act.wait_ge(s_par, 16)
            act.activation(tg[:], A("gates"), ACT.Tanh).then_inc(s_tg, 1)
            for i in range(4):
                act.wait_ge(s_gps, i + 1)
                act.activation(xn_gates(xn)[:, i * 512:(i + 1) * 512], wide[i][0:2 * H0, :], ACT.Copy).then_inc(s_gT, 1)
            IG, FG, AZ, EZ, L, LF, CS, AA, MM, ONE = range(10)
            g = lambda i: g64[:, i, :]
            act.wait_ge(s_z, 1)
            ch.link(act.activation(g(AZ), g(FG), ACT.Abs))
            ch.link(act.activation(g(EZ), g(AZ), ACT.Exp, scale=-1.0))
            act.activation(g(L), g(EZ), ACT.Ln, bias=1.0).then_inc(s_sp, 1)
            act.wait_ge(s_aM, 1)
            act.activation(t64[:, 0:P], g64[:, AA, 0:P], ACT.Exp, bias=negM[:, 0:1]).then_inc(s_t64, 1)
            act.activation(t64[:, 2 * P:], g(CS), ACT.Exp, scale=-1.0).then_inc(s_t64, 1)
            act.activation(t64[:, P:2 * P], g64[:, MM, P:S], ACT.Exp, bias=g64[:, MM, P - 1:P], scale=-1.0)\
               .then_inc(s_t64, 1)
            with act.Fori(0, B // 2) as it:
                for u in range(4):
                    if u % 2 == 0:
                        act.wait_ge(s_free, it * 2 + (u // 2 + 1))
                        act.activation(qS[u // 2][:], xT[:, bass.ds((it * 2 + u // 2) * S + P, P)], ACT.Copy)\
                            .then_inc(s_qS, 1)
                    act.wait_ge(s_E, it * 4 + (u + 1))
                    act.wait_ge(s_C, it * 4 + (u + 1))
                    act.activation(Dm[u % 2][:], pw[0][:], ACT.Exp).then_inc(s_D, 1)
                    act.wait_ge(s_w[u % 2], it * 32 + (16 * (u // 2 + 1)))
                    act.activation(rd(wh[:, bass.ds((it * 4 + u) * F0, F0)]), wst[u % 2][:], ACT.Copy)\
                        .then_inc(s_wh, 1)

            for i in range(4):
                act.wait_ge(s_tr, 5 + i)
                act.activation(xT[:, i * 512:(i + 1) * 512], ps[i][:], ACT.Copy).then_inc(s_xT, 1)
            act.wait_ge(s_lx, 1)
            act.activation(rt[:, 1, :], rt[:, 0, :], ACT.Exp).then_inc(s_ex, 1)
            act.wait_ge(s_xn, 2 * NT)
            for k in range(2):
                act.activation(xa[k][:, :, 0:D], xn[:], ACT.Copy).then_inc(s_xa, 1)

            def silu(j, i):
                act.wait_ge(s_G, j + 1)
                ge(act, s_hb, j - 1)
                act.activation(sg[i][:], pw[0][:, i * F0:(i + 1) * F0], ACT.Silu).then_inc(s_sg, 1)

            def copy_hidden(j, i):
                act.wait_ge(s_H, j + 1)
                ge(act, s_Y, j - 1)
                act.activation(hT[i][:], ps[1 + i][:], ACT.Copy).then_inc(s_hT, 1)

            pipelined(act, NBLK, [(silu, 0), (copy_hidden, 1)], peel=2)

            def exponentials(b, n):
                g, c, half = n // 4, n // 2 % 2, n % 2
                act.wait_ge(c_P2, b * NU + (n + 1))
                if n % 4 == 0:
                    ge(act, c_PV, b * HG + (g - 1))
                act.activation(et3[g % 2][c][:, 2 * half:2 * half + 2, :],
                               pw[1][:, half * 512:(half + 1) * 512].rearrange("p (j s) -> p j s", s=S), ACT.Exp)\
                    .then_inc(c_X, 1)

            def copy_sums(b, k):
                act.wait_ge(c_PV, b * HG + (2 * k + 2))
                if k == 0:
                    ge(act, c_OT, b)
                act.activation(o32[:, 2 * k:2 * k + 2, :], ps[2 + k][:].rearrange("p (g s) -> p g s", s=S), ACT.Copy)\
                    .then_inc(c_O, 1)

            def copy_keys(b):
                act.wait_ge(c_K, b + 1)
                ge(act, c_ks, b)
                for g in range(HG):
                    act.activation(k32[:, g, :], ps[g // 2][:, g % 2 * S:(g % 2 + 1) * S], ACT.Identity,
                                   bias=A("bk")[:, g:g + 1]).then_inc(c_k32, 1)

            def round_keys(b):
                act.wait_ge(c_k32, b * HG + HG)
                act.activation(rd(khi[:]), k32[:], ACT.Copy, scale=C("key_lo")).then_inc(c_khi, 1)

            def copy_queries(b, g):
                if g == 0:
                    act.wait_ge(c_Q, b + 1)
                    ge(act, c_qs, b)
                act.activation(q32[:, g, :], ps[g // 2][:, g % 2 * S:(g % 2 + 1) * S], ACT.Identity,
                               bias=bqs[:, g:g + 1], scale=float(DH1) ** -0.5).then_inc(c_q32, 1)

            def round_queries(b):
                act.wait_ge(c_q32, b * HG + HG)
                act.activation(rd(qhi[:]), q32[:], ACT.Copy, scale=C("query_lo")).then_inc(c_qhi, 1)

            def copy_turned(b):
                act.wait_ge(c_nT, b + 1)
                ge(act, c_Y, b)
                act.activation(onT[:], ps[2][:, 0:CH * P].rearrange("p (c s) -> p c s", s=P), ACT.Copy)\
                    .then_inc(c_nc, 1)

            def attend(k, i):
                if among(k + 1, B):
                    copy_keys(k + 1)
                if isinstance(k, int) and k < 0:
                    for q in range(4):
                        act.wait_ge(s_tr, 9 + q)
                        act.activation(xT[:, q * 512:(q + 1) * 512], wide[q], ACT.Copy).then_inc(s_xT, 1)
                for n in range(NU):
                    if among(k - 1, B):
                        exponentials(k - 1, n)
                    if n == 1 and among(k - 2, B):
                        copy_turned(k - 2)
                    if n == 2 and among(k + 1, B):
                        round_keys(k + 1)
                    if 4 <= n < 4 + HG and among(k + 1, B):
                        copy_queries(k + 1, n - 4)
                    if n == 9 and among(k + 1, B):
                        round_queries(k + 1)
                    if n == 11 and among(k - 1, B):
                        copy_sums(k - 1, 0)
                if among(k - 1, B):
                    copy_sums(k - 1, 1)

            act.wait_ge(c_wc, 2)
            turns(act, B, 1, 2, 1, attend)

            act.wait_ge(s_x3, B)
            for q, bank in enumerate((wide[0], wide[1], ps[0][:], ps[3][:])):
                act.wait_ge(s_tr, 13 + q)
                act.activation(xT[:, q * 512:(q + 1) * 512], bank, ACT.Copy).then_inc(s_xT, 1)
            act.wait_ge(d_lg, 1)
            act.activation(r1[:, 0, :], ps[1][:, 0:NT * E1], ACT.Exp, scale=-1.0).then_inc(d_sg, 1)
            act.wait_ge(d_w, 32)
            for k in range(2):
                at = slice(k * FC1 * P, (k + 1) * FC1 * P)
                act.activation(rd(guh[:, at]), graw[:, at], ACT.Copy).then_inc(d_wh, 1)
            act.wait_ge(s_xT, 16)
            for q in range(4):
                at = slice(q * 512, (q + 1) * 512)
                act.activation(rd(xTh[:, at]), xT[:, at], ACT.Copy).then_inc(d_xh, 1)
            with act.Fori(0, T // TT // 2) as it:
                for n in range(2 * FC1):
                    act.wait_ge(d_G, it * (2 * FC1) + (n + 1))
                    act.wait_ge(d_h1, it * (2 * FC1) + (n + 1))
                    act.activation(sg1[n % 2][:], pw[0][:, n % 2 * TT:(n % 2 + 1) * TT], ACT.Silu).then_inc(d_sl, 1)

        @block.gpsimd
        def _(pool):
            pool.sem_inc(s_free, 2)
            pool.sem_inc(s_PV, 2)
            pool.sem_inc(s_num, 1)
            pool.sem_inc(s_It, 1)
            pool.sem_inc(s_C, 2)
            pool.sem_inc(s_wl, 2)
            pool.wait_ge(s_xT, 4)
            with pool.Fori(0, B // 2) as it:
                for i in range(2):
                    b = it * 2 + i
                    pool.wait_ge(s_free, it * 2 + (i + 1))
                    pool.tensor_tensor(Qm[i][:], xT[:, bass.ds(b * S, S)].unsqueeze(1).broadcast_to([P, H0, S]),
                                       C("quarter_of_head").unsqueeze(2).broadcast_to([P, H0, S]), ALU.mult)\
                        .then_inc(s_qm, 1)
                    for u in (2 * i, 2 * i + 1):
                        pool.wait_ge(s_wh, it * 4 + (u + 1))
                        at = bass.ds((it * 4 + u) * F0, F0)
                        pool.tensor_tensor(rd(wl[:, at]), wst[u % 2][:], wh[:, at], ALU.subtract).then_inc(s_wl, 1)

            pool.wait_ge(s_clr, 16)
            for k in range(2):
                pool.wait_ge(s_sl, k + 1)
                pool.wait_ge(s_xa, k + 1)
                for t in range(NT):
                    pool.indirect_dma_start(out=scr_x, out_offset=bass.IndirectOffsetOnAxis(slot[:, k, t:t + 1], axis=0),
                                            in_=xa[k][:, t, :], in_offset=None).then_inc(s_sc, 16)
            def store_block(j, i):
                pool.wait_ge(s_yb, j + 1)
                pool.sem_inc(s_seen, 1)
                pool.indirect_dma_start(out=scr_y, out_offset=bass.IndirectOffsetOnAxis(row[i][:], axis=0),
                                        in_=yb[i][:], in_offset=None).then_inc(s_ys[i], 16)

            pipelined(pool, NBLK, [(store_block, 0)])

            for i in range(2):
                pool.wait_ge(s_ys[i], 16 * (NBLK // 2))
            for t in (Kd[0], Qd, Kd[1]):
                pool.memset(t[:], 0.0).then_inc(c_zk, 1)

            def split(k, i):
                if not among(k + 1, B):
                    return
                pool.wait_ge(c_khi, k + 2)
                if among(k, B):
                    pool.wait_ge(c_kd[i], loads(k, i, 64))
                    pool.wait_ge(c_kst[i], loads(k, i, 16))
                pool.tensor_tensor(rd(Kn[:]), k32[:], khi[:], ALU.subtract).then_inc(c_ks, 1)
                pool.wait_ge(c_qhi, k + 2)
                ge(pool, c_q2, k * 2)
                pool.tensor_tensor(rd(Qs[1 - i][:]), q32[:], qhi[:], ALU.subtract).then_inc(c_qs, 1)

            turns(pool, B, 1, 0, 3, split)

            pool.sem_inc(d_Y, 2)
            pool.sem_inc(d_h1, 2)
            pool.sem_inc(d_h, 2)
            for k in range(2):
                at = slice(k * FC1 * P, (k + 1) * FC1 * P)
                pool.wait_ge(d_wh, k + 1)
                pool.tensor_tensor(rd(gul[:, at]), graw[:, at], guh[:, at], ALU.subtract).then_inc(d_wl, 1)
            for q in range(4):
                at = slice(q * 512, (q + 1) * 512)
                pool.wait_ge(d_xh, q + 1)
                pool.tensor_tensor(rd(xTl[:, at]), xT[:, at], xTh[:, at], ALU.subtract).then_inc(d_xT, 1)

        @block.tensor
        def _(pe):
            def turn_xn(use, banks, groups=range(4)):
                for i in groups:
                    pe.wait_ge(s_xn, use * NT + 4 * (i + 1))
                    for k in range(4):
                        ins = pe.transpose(banks[i][:, k * P:(k + 1) * P], xn[:, 4 * i + k, :], C("ident"))
                    ins.then_inc(s_tr, 1)

            pe.wait_ge(s_con, 16)
            turn_xn(0, ps)
            pe.wait_ge(s_ctx, 16)
            pe.wait_ge(s_bc, 8)
            for i in range(4):
                pe.wait_ge(s_xT, i + 1)
                pe.matmul(wide[i][0:2 * H0, :], A("gwq"), xT[:, i * 512:(i + 1) * 512], start=True, stop=False)
                pe.matmul(wide[i][0:2 * H0, :], gwc[:], ctxT[:, i * 512:(i + 1) * 512], start=False, stop=True)\
                    .then_inc(s_gps, 1)
            pe.wait_ge(s_t64, 3)
            for k in range(4):
                pe.transpose(ps[0][:, k * BH:(k + 1) * BH], t64[:, k * P:(k + 1) * P], C("ident")[0:BH, 0:BH])\
                    .then_inc(s_wps, 1)
            pe.wait_ge(s_bc, 9)
            pe.wait_ge(s_wT, 1)
            pe.wait_ge(s_gT, 4)

            def exponent(it, u):
                i, c = u // 2, u % 2
                if c == 0:
                    pe.wait_ge(s_ls, it * 2 + (i + 1))
                ge(pe, s_D, it * 4 + u)
                for half in range(2):
                    o = pw[0][:, half * 512:(half + 1) * 512]
                    hs = slice(4 * half, 4 * half + 4)
                    pe.matmul(o, ident_bf[:], future_bf[:], start=True, stop=False)
                    pe.matmul(o, rd(LS[i][:, 2 * P:]), rd(Rm[:, hs, c * P:(c + 1) * P]), start=False, stop=False)
                    ins = pe.matmul(o, rd(LS[i][:, c * P:(c + 1) * P]), rd(dlt[:, hs, :]), start=False, stop=True)
                ins.then_inc(s_E, 1)

            def pair(it, last):
                for u in range(4):
                    i, c = u // 2, u % 2
                    b = it * 2 + i
                    if c == 0:
                        pe.wait_ge(s_ct[i], it * 16 + 16)
                        pe.wait_ge(s_qm, it * 2 + (i + 1))
                    for half in range(2):
                        ins = pe.matmul(pw[1][:, half * 512:(half + 1) * 512], ctS[i][:, c * P:(c + 1) * P],
                                        Qm[i][:, 4 * half:4 * half + 4, c * P:(c + 1) * P], start=True, stop=True)
                    ins.then_inc(s_S, 1)
                    if c == 0:
                        pe.wait_ge(s_ks, it * 2 + (i + 1))
                        pe.wait_ge(s_It, it * 2 + (i + 1))
                        pe.matmul(ps[1][:, 0:H0 * VW], Ks[i][:], vaug[:, b * CH, :], start=True, stop=True)\
                            .then_inc(s_st, 1)
                    if u < 3:
                        exponent(it, u + 1)
                    elif not last:
                        exponent(it + 1, 0)
                    if c == 1:
                        pe.wait_ge(s_stm, it * 2 + (i + 1))
                        pe.wait_ge(s_qS, it * 2 + (i + 1))
                        pe.matmul(ps[1][:, 256:256 + H0 * VW], qS[i][:], stm[:], start=True, stop=True)\
                            .then_inc(s_I, 1)
                    pe.wait_ge(s_C, it * 4 + (u + 3))
                    pe.wait_ge(s_num, it * 4 + (u + 1))
                    for h in range(H0):
                        ins = pe.matmul(ps[0][:, h * VW:(h + 1) * VW], Cm[u % 2][:, h * P:(h + 1) * P],
                                        vaug[:, b * CH + c, h * VW:(h + 1) * VW], start=True, stop=True)
                    ins.then_inc(s_PV, 1)
                    if c == 1:
                        pe.matmul(ps[3][0:32, 0:2], ones_bf[:, 0:32], ones_bf[:, 0:2], start=True, stop=True)\
                            .then_inc(s_free, 1)

            exponent(0, 0)
            loop_pairs(pe, pair)
            pe.wait_ge(s_num, NT + 1)

            for q in range(5):
                if q < 4:
                    turn_xn(1, ps, [q])
                if q:
                    pe.wait_ge(s_xT, 4 + q)
                    for t in range(4 * q - 4, 4 * q):
                        ins = pe.matmul(pw[0][:, t * E0:(t + 1) * E0], xT[:, t * P:(t + 1) * P], A("router0"),
                                        start=True, stop=True)
            ins.then_inc(s_lg, 1)
            pe.wait_ge(s_ro, 1)
            pe.matmul(ps[0][:, 0:P], before_bf[:], routed[:], start=True, stop=True)
            pe.matmul(ps[0][:, P:2 * P], ones_bf[:], routed[:], start=True, stop=True).then_inc(s_rk, 1)
            pe.wait_ge(s_be, 1)
            pe.wait_ge(s_w2, 16)
            pe.wait_ge(s_wl, 2 + 2 * E0)

            def tokens(j, i):
                ge(pe, s_xp, j * 2)
                if isinstance(j, int):
                    pe.wait_ge(s_xg[i], 16 * (j // 2 + 1))
                else:
                    pe.wait_ge(s_xg[i], (j - i) * 8 + 16)
                pe.transpose(ps[0][:, 0:P], xg[i][:], C("ident")).then_inc(s_T, 1)

            def up(j, i):
                at = pe.value_load(boff[0:1, bass.ds(j, 1)], min_val=0, max_val=(E0 - 1) * F0)
                pe.wait_ge(s_xp, j * 2 + 2)
                for bank, m, free, ready in ((pw[0], 0, s_sg, s_G), (pw[1], 1, s_hb, s_U)):
                    o = bank[:, i * F0:(i + 1) * F0]
                    ge(pe, free, j - 1)
                    hi, lo = (w[:, bass.ds(at + m * E0 * F0, F0)] for w in (wh, wl))
                    pe.matmul(o, rd(xgh[i][:]), rd(hi), start=True, stop=False)
                    pe.matmul(o, rd(xgh[i][:]), rd(lo), start=False, stop=False)
                    pe.matmul(o, rd(xgl[i][:]), rd(hi), start=False, stop=True).then_inc(ready, 1)

            def turn_hidden(j, i):
                pe.wait_ge(s_hb, j + 1)
                ge(pe, s_hT, j - 1)
                for c in range(FC0):
                    ins = pe.transpose(ps[1 + i][:, c * P:(c + 1) * P], hb[i][:, c * P:(c + 1) * P], C("ident"))
                ins.then_inc(s_H, 1)

            def down(j, i):
                at = pe.value_load(boff[0:1, bass.ds(j, 1)], min_val=0, max_val=(E0 - 1) * F0)
                pe.wait_ge(s_hT, j + 1)
                ge(pe, s_yb, j)
                for c in range(FC0):
                    ins = pe.matmul(ps[3][:, 0:P], hT[i][:, c * P:(c + 1) * P], w2[:, bass.ds(at + c * D, D)],
                                    start=(c == 0), stop=(c == FC0 - 1))
                ins.then_inc(s_Y, 1)

            pipelined(pe, NBLK, [(up, 0), (tokens, -1), (turn_hidden, 1), (down, 2)], peel=2)

            pe.wait_ge(s_yb, NBLK)
            pe.wait_ge(c_wa, 1)
            pe.matmul(ps[0][:, 0:P], wem[:], A("wo"), start=True, stop=True)
            pe.matmul(ps[0][:, P:2 * P], bemb[:], A("wo"), start=True, stop=True).then_inc(c_wp, 1)
            pe.wait_ge(c_wc, 2)

            def logits2(of):
                for t in of:
                    if t % 4 == 0:
                        pe.wait_ge(s_xT, 13 + t // 4)
                    ins = pe.matmul(ps[1][:, t * E1:(t + 1) * E1], xT[:, t * P:(t + 1) * P], A("router1"),
                                    start=True, stop=True)
                return ins

            def scores_for_max(b, i, n):
                c, g, half = n // 8, n // 2 % 4, n % 2
                if n == 0:
                    pe.wait_ge(c_qs, b + 1)
                    pe.wait_ge(c_kd[i], loads(b, i, 64))
                ge(pe, c_R, b * NU + (n - 1) if n else (b - 1) * NU + (NU - 1))
                pe.matmul(pw[0][:, half * 512:(half + 1) * 512], rd(Qs[i][:, g, c * P:(c + 1) * P]),
                          rd(Kd[i][:, g, 2 * half:2 * half + 2, :]), start=True, stop=True).then_inc(c_P1, 1)

            def scores_less_max(b, i, n):
                g, c, half = n // 4, n // 2 % 2, n % 2
                if n == 0:
                    pe.wait_ge(c_qd, b * 64 + 64)
                    pe.wait_ge(c_kst[i], loads(b, i, 16))
                ge(pe, c_X, b * NU + (n - 1) if n else (b - 1) * NU + (NU - 1))
                pe.matmul(pw[1][:, half * 512:(half + 1) * 512], rd(Kst[i][:, g, c * P:(c + 1) * P]),
                          rd(Qd[:, g, 2 * half:2 * half + 2, :]), start=True, stop=True).then_inc(c_P2, 1)

            def weighted_sums(b, i, g):
                pe.wait_ge(c_X, b * NU + (4 * g + 4))
                if g == 0:
                    pe.wait_ge(c_vp, b + 1)
                    ge(pe, c_nc, b)
                if g == 2:
                    ge(pe, s_x3, b)
                for c in range(CH):
                    for j in range(HJ):
                        ins = pe.matmul(ps[2 + g // 2][j * ST:(j + 1) * ST, g % 2 * S:(g % 2 + 1) * S],
                                        vp[i][:, c, HJ * g + j, :], et3[g % 2][c][:, j, :],
                                        start=(c == 0), stop=(c == CH - 1), skip_group_check=True)
                ins.then_inc(c_PV, 1)

            def keys(b):
                ge(pe, c_q2, (b - 1) * 2)
                for g in range(HG):
                    ins = pe.matmul(ps[g // 2][:, g % 2 * S:(g % 2 + 1) * S], wks[:, g * P:(g + 1) * P],
                                    ctxT[:, bass.ds(b * S, S)], start=True, stop=True)
                ins.then_inc(c_K, 1)

            def queries(b):
                pe.wait_ge(c_k32, b * HG + HG)
                for g in range(HG):
                    ins = pe.matmul(ps[g // 2][:, g % 2 * S:(g % 2 + 1) * S], wqs[:, g * P:(g + 1) * P],
                                    xT[:, bass.ds(b * S, S)], start=True, stop=True)
                ins.then_inc(c_Q, 1)

            def values(b, i):
                pe.wait_ge(c_ct[i], loads(b, i, 16))
                pe.wait_ge(c_q32, min(b + 2, B) * HG if isinstance(b, int) else b * HG + 2 * HG)
                for c in range(CH):
                    ins = pe.matmul(ps[0][:, c * D:(c + 1) * D], ctS[i][:, c * P:(c + 1) * P], A("wv"),
                                    start=True, stop=True)
                ins.then_inc(c_V, 1)

            def max_rows(b):
                pe.wait_ge(c_mp, b * 2 + 2)
                pe.wait_ge(c_vp, b + 1)
                for g in range(HG):
                    for c in range(CH):
                        at = g % 2 * S + c * P
                        ins = pe.transpose(ps[g // 2][:, at:at + P], mp[:, c, g, :], C("ident"))
                ins.then_inc(c_MT, 1)

            def turn_sums(b):
                pe.wait_ge(c_O, b * 2 + 2)
                for c in range(CH):
                    for g in range(HG):
                        ins = pe.transpose(ps[2 + c][:, g * P:(g + 1) * P], o32[:, g, c * P:(c + 1) * P], C("ident"))
                ins.then_inc(c_OT, 1)

            def turn_attention(b):
                pe.wait_ge(c_on, b * 2 + 2)
                for c in range(CH):
                    ins = pe.transpose(ps[2][:, c * P:(c + 1) * P], on[:, c, :], C("ident"))
                ins.then_inc(c_nT, 1)

            def attention_out(b):
                pe.wait_ge(c_nc, b + 1)
                for c in range(CH):
                    ins = pe.matmul(ps[3][:, c * D:(c + 1) * D], onT[:, c, :], wc[:], start=True, stop=True)
                ins.then_inc(c_Y, 1)

            def attend(k, i):
                for n in range(NU + 4):
                    if n < NU and among(k, B):
                        scores_for_max(k, i, n)
                    if n == 1 and among(k + 1, B):
                        keys(k + 1)
                        if isinstance(k, int) and k < 0:
                            turn_xn(2, wide)
                            pe.wait_ge(s_xT, 12)
                    if n == 2 and among(k - 2, B):
                        turn_sums(k - 2)
                    if n >= 4 and among(k - 1, B):
                        scores_less_max(k - 1, 1 - i, n - 4)
                    if n == 5 and among(k - 2, B):
                        turn_attention(k - 2)
                    if n == 6 and among(k + 1, B):
                        queries(k + 1)
                    if n == 8 and among(k - 2, B):
                        attention_out(k - 2)
                    if n in (9, 13, 17) and among(k - 1, B):
                        weighted_sums(k - 1, 1 - i, (n - 9) // 4)
                    if n == 13 and among(k, B):
                        values(k, i)
                    if n == 19 and among(k, B):
                        max_rows(k)
                if among(k - 1, B):
                    weighted_sums(k - 1, 1 - i, 3)

            turns(pe, B, 1, 2, 1, attend)

            turn_xn(3, [wide[0], wide[1], ps[0]], range(3))
            logits2(range(12))
            turn_xn(3, ps, [3])
            logits2(range(12, NT)).then_inc(d_lg, 1)
            pe.wait_ge(d_cm, 1)
            for i in range(4):
                for k in range(4):
                    ins = pe.transpose(ps[i][0:2 * E1, k * P:(k + 1) * P], chl[:, 4 * i + k, :], C("ident"))
                ins.then_inc(d_cT, 1)
            pe.wait_ge(d_cc, 4)
            pe.wait_ge(d_wl, 2)
            pe.wait_ge(d_c, 2)
            pe.wait_ge(d_xT, 4)

            def hidden_units(it, k, c):
                n = k * FC1 + c
                t = bass.ds((it * 2 + k) * TT, TT)
                half = slice(n % 2 * TT, (n % 2 + 1) * TT)
                for m, (bank, free, ready) in enumerate(((pw[0], d_sl, d_G), (pw[1], d_h1, d_U))):
                    if n >= 2:
                        pe.wait_ge(free, it * (2 * FC1) + (n - 1 + 2 * m))
                    f = slice((m * FC1 + c) * P, (m * FC1 + c + 1) * P)
                    pe.matmul(bank[:, half], rd(guh[:, f]), rd(xTh[:, t]), start=True, stop=False)
                    pe.matmul(bank[:, half], rd(gul[:, f]), rd(xTh[:, t]), start=False, stop=False)
                    ins = pe.matmul(bank[:, half], rd(guh[:, f]), rd(xTl[:, t]), start=False, stop=True)
                    if m == 0:
                        ins.then_inc(ready, 1)
                if c < FC1 - 1:
                    pe.wait_ge(d_h, it * (2 * (FC1 - 1)) + (k * (FC1 - 1) + c + 1))
                    ins = pe.matmul(ps[c % 2][:], rd(ecol[:, c * P:(c + 1) * P]), rd(cT[:, t]), start=True, stop=True)
                ins.then_inc(ready, 1)

            def down2(it, k):
                pe.wait_ge(d_h1, it * (2 * FC1) + (k * FC1 + FC1 + 2))
                pe.wait_ge(d_h, it * (2 * (FC1 - 1)) + ((k + 1) * (FC1 - 1) + 2))
                for q in range(TT // P):
                    for c in range(FC1):
                        ins = pe.matmul(ps[2 + k][:, q * D:(q + 1) * D], hT1[k][:, c, q * P:(q + 1) * P], dn[:, c, :],
                                        start=(c == 0), stop=(c == FC1 - 1))
                ins.then_inc(d_Y, 1)

            with pe.Fori(0, T // TT // 2) as it:
                for c in range(FC1):
                    hidden_units(it, 0, c)
                for c in range(FC1):
                    hidden_units(it, 1, c)
                    if c == 1:
                        down2(it, 0)
                down2(it, 1)


def xn_gates(xn):
    return xn[0:2 * H0, :, :].rearrange("p t d -> p (t d)")


def kernel(**inputs):
    import numpy as np
    import concourse.bacc as bacc
    from concourse.bass_utils import run_bass_kernel_spmd as run

    nc = bacc.Bacc("TRN2", target_bir_lowering=False, num_devices=1)
    arrays = lay_out(np, {k: np.asarray(v) for k, v in inputs.items()})
    aps = {}
    for name, arr in arrays.items():
        aps[name] = nc.dram_tensor("in_" + name, arr.shape, mybir.dt.from_np(arr.dtype), kind="ExternalInput").ap()
    out = nc.dram_tensor("out", (P, NT * D), F32, kind="ExternalOutput").ap()
    scr_x = nc.dram_tensor("scratch_x", (NBLK * P, D + 2), F32).ap()
    scr_y = nc.dram_tensor("scratch_y", (1 + 2 * T + NBLK * P, D), F32).ap()
    build(nc, aps, scr_x, scr_y, out)
    r = run(nc, [{"in_" + n: t for n, t in arrays.items()}], core_ids=[0])
    got = r.results[0]["out"]
    return np.ascontiguousarray(got.reshape(P, NT, D).transpose(1, 0, 2).reshape(B, S, D))


def lay_out(np, v):
    f = np.float32

    def tiles(t):
        return t.reshape(NT, P, D).transpose(1, 0, 2)

    x, ctx = v["x"].reshape(T, D), v["ctx_1024"].reshape(T, D)
    va = np.ones((P, NT, H0, VW), f)
    va[..., :DH0] = tiles(ctx).reshape(P, NT, H0, DH0)

    r = np.arange(P)
    con = np.zeros((P, NCONST), f)
    c = {k: con[:, s:e] for k, (s, e) in CONST.items()}
    c["ident"][:] = np.eye(P)
    c["future"][:] = np.where(r[:, None] > r[None, :], NEG, 0.0)
    c["before"][:] = r[:, None] < r[None, :]
    c["of_seq"][:] = (r[:, None] % BH) // H0 == np.arange(B)
    c["of_head"][:] = r[:, None] % H0 == np.arange(H0)
    c["neg_of_head"][:] = -1.0 * (r[:, None] % H0 == np.arange(H0))
    c["quarter_of_head"][:] = 0.25 * (r[:, None] // DH0 == np.arange(H0))
    c["quarter_block"][:] = np.repeat(0.25 * (r[:, None] // DH0 == np.arange(H0)), VW, 1)
    c["block_start"][:] = P * np.arange(NT)
    c["result_row"][:] = 1 + P * np.arange(NT) + r[:, None]
    c["spare_row"][:] = 1 + 2 * T + P * np.arange(NBLK) + r[:, None]
    c["not_first"][:] = np.arange(P) % NT != 0
    c["block_index"][:] = np.repeat(np.arange(NBLK), E0)
    c["rev8"][:] = E0 - np.arange(E0)
    c["query_lo"][:, 0] = 1.0 * (r % ST // DH1 == 2)
    c["key_lo"][:, 0] = 1.0 * (r % ST // DH1 == 1)
    for e in range(E1):
        for row in (e, E1 + e):
            c["expert_cols"][row, I1 * e:I1 * (e + 1)] = 1.0
    par = np.zeros((P, NPARAM), f)
    q = {k: par[:, s:e] for k, (s, e) in PARAM.items()}
    iw, fw = v["L0_xattn_igate_w"], v["L0_xattn_fgate_w"]
    for k, name in enumerate(("gwq", "gwk", "gwv")):
        q[name][:, :H0] = iw[:, k * D:(k + 1) * D].T
        q[name][:, H0:] = fw[:, k * D:(k + 1) * D].T
    q["gate_b"][:BH, 0] = np.tile(v["L0_xattn_igate_b"], B)
    q["gate_b"][:BH, 1] = np.tile(v["L0_xattn_fgate_b"], B)
    q["ln_scale"][:] = v["L0_xattn_ln_scale"]
    q["gates"][:, 0], q["gates"][:, 1] = v["g_xattn"][0], v["g_ffn"][0]
    q["gates"][:, 2], q["gates"][:, 3] = v["g_xattn"][1], v["g_ffn"][1]
    q["router0"][:] = v["L0_ffn_gate_w"]
    q["router1"][:] = v["L1_ffn_router_weight"].T
    q["e_bias"][:] = v["L1_ffn_e_bias"]
    wqs, wks = np.zeros((P, HG, HJ, ST), f), np.zeros((P, HG, HJ, ST), f)
    for w, wt, bias in ((wqs, "L1_xattn_Wq", "bq"), (wks, "L1_xattn_Wk", "bk")):
        b4 = v["L1_xattn_" + bias].reshape(HG, HJ, DH1)
        for k in range(3):
            at = slice(k * DH1, (k + 1) * DH1)
            w[:, :, :, at] = v[wt].T.reshape(P, HG, HJ, DH1)
            q[bias].reshape(HJ, ST, HG)[:, at, :] = b4.transpose(1, 2, 0)
    for j in range(HJ):
        q["bk"][j * ST + SM:j * ST + SM + 2] = 1.0
    q["bv"][:] = v["L1_xattn_bv"]
    q["wv"][:] = v["L1_xattn_Wv"].T
    q["wo"][:] = v["L1_xattn_Wo"].T
    q["be"][:] = v["L1_xattn_be"].T
    q["bo"][:] = v["L1_xattn_bo"]
    gu = np.zeros((P, 2, FC1 * P), f)
    for m, (routed, shared) in enumerate((("L1_ffn_gate_w", "L1_ffn_sh_gate_w"), ("L1_ffn_up_w", "L1_ffn_sh_up_w"))):
        gu[:, m, :E1 * I1] = v[routed].transpose(2, 0, 1).reshape(P, E1 * I1)
        gu[:, m, E1 * I1:] = v[shared].T
    down = np.zeros((P, FC1, D), f)
    down[:, :FC1 - 1] = v["L1_ffn_down_w"].transpose(0, 2, 1).reshape(FC1 - 1, P, D).transpose(1, 0, 2)
    down[:, FC1 - 1] = v["L1_ffn_sh_down_w"].T
    w13 = np.zeros((P, 2 * E0 * F0), f)
    w13[:, :E0 * F0] = v["L0_ffn_w1"].transpose(1, 0, 2).reshape(P, E0 * F0)
    w13[:, E0 * F0:2 * E0 * F0] = v["L0_ffn_w3"].transpose(1, 0, 2).reshape(P, E0 * F0)
    arrays = {
        "x_nat": tiles(x).reshape(P, NT * D), "ctxT": ctx.T, "vaug": va.reshape(P, NT * H0 * VW),
        "const": con, "param": par, "w13": w13,
        "wqs": wqs.reshape(P, HG * P), "wks": wks.reshape(P, HG * P),
        "we": v["L1_xattn_We"].transpose(1, 0, 2).reshape(P, EO * D),
        "gu": gu.reshape(P, 2 * FC1 * P), "down": down.reshape(P, FC1 * D),
        "w2": v["L0_ffn_w2"].reshape(E0, FC0, P, D).transpose(2, 0, 1, 3).reshape(P, E0 * F0),
    }
    return {k: np.ascontiguousarray(t) for k, t in arrays.items()}
```
